# Optimizing a Trainium2 kernel written in Bass

```python
import numpy as np
import jax
import jax.numpy as jnp

def _softmax(x, axis=-1):
    return jax.nn.softmax(x, axis=axis)

def _gelu(x):
    return jax.nn.gelu(x, approximate=True)

def _silu(x):
    return jax.nn.silu(x)

def _sigmoid(x):
    return jax.nn.sigmoid(x)

def _layernorm(x, axis=-1, eps=1e-05):
    m = jnp.mean(x, axis=axis, keepdims=True)
    v = jnp.var(x, axis=axis, keepdims=True)
    return (x - m) / jnp.sqrt(v + eps)

def _scatter_add(tgt, idx, src, axis=0):
    return tgt.at[idx].add(src)

def _segment_sum(src, seg, n):
    return jax.ops.segment_sum(src, seg, n)
kernel_name = 'mk_decoder_postln_d2_seqx_r4_39d455'

def setup_inputs(seed: int=0):
    np.random.seed(seed)
    _w = jnp.asarray

    def _rec_inputs():
        import jax
        import jax.numpy as jnp
        _rk = jax.random.key(seed)
        x = 7.22e-05 + 1 * jax.random.normal(jax.random.fold_in(_rk, 1), (8, 256, 256), jnp.float32)
        _lenS = 256 - jax.random.randint(jax.random.fold_in(_rk, 7), (8,), 0, max(1, 256 // 4) + 1, jnp.int32)
        _lenS2 = 77 - jax.random.randint(jax.random.fold_in(_rk, 8), (8,), 0, max(1, 77 // 4) + 1, jnp.int32)
        _ctx_768P = jax.random.normal(jax.random.fold_in(_rk, 11), (8, 16, 192), jnp.float32)
        _ctx_768c = jax.random.dirichlet(jax.random.fold_in(_rk, 511), 0.3 * jnp.ones((16,), jnp.float32), (8, 77))
        _ctx_768t = jnp.einsum('bsk,bkd->bsd', _ctx_768c, _ctx_768P)
        _ctx_768t = _ctx_768t * jax.lax.rsqrt(jnp.mean(jnp.square(_ctx_768t)) + 1e-12) * 0.953939
        ctx_768 = 2.09791e-05 + 1.00001 * (_ctx_768t + 0.3 * jax.random.normal(jax.random.fold_in(_rk, 611), (8, 77, 192), jnp.float32))
        return (x, ctx_768)
    x, ctx_768 = _rec_inputs()

    def _L0_attn_setup():
        import jax, jax.numpy as jnp
        import numpy as np
        D_STATE = 16

        def _silu(v):
            return v * jax.nn.sigmoid(v)
        key = jax.random.key(seed)
        ks = jax.random.split(key, 7)
        B, L, d_model = (2, 1024, 256)
        d_inner, d_conv, d_state = (512, 4, D_STATE)
        s = 0.02
        return {'x': jax.random.normal(ks[0], (B, L, d_model), jnp.float32), 'W_in': jax.random.normal(ks[1], (2 * d_inner, d_model), jnp.float32) * s, 'conv_w': jax.random.normal(ks[2], (d_inner, d_conv), jnp.float32) * 0.3, 'conv_b': jax.random.normal(ks[3], (d_inner,), jnp.float32) * 0.1, 'W_xproj': jax.random.normal(ks[4], (2 * d_state + d_inner, d_inner), jnp.float32) * s, 'D': jnp.ones((d_inner,), jnp.float32), 'W_out': jax.random.normal(ks[5], (d_model, d_inner), jnp.float32) * s}
    _L0_attn_all = _L0_attn_setup()
    _L0_attn_in = {k: v for k, v in _L0_attn_all.items() if k in ('W_in', 'conv_w', 'conv_b', 'W_xproj', 'D', 'W_out')}
    del _L0_attn_all

    def _L0_xattn_setup():
        import jax, jax.numpy as jnp
        import numpy as np
        HEADS = 16
        DIM_HEAD = 64
        key = jax.random.key(seed)
        ks = jax.random.split(key, 7)
        B, Nq, Dq = (4, 512, 256)
        Nk, Dc = (256, 192)
        inner = HEADS * DIM_HEAD
        sq = 1.0 / np.sqrt(Dq)
        sc = 1.0 / np.sqrt(Dc)
        si = 1.0 / np.sqrt(inner)
        return {'x': jax.random.normal(ks[0], (B, Nq, Dq), dtype=jnp.float32), 'context': jax.random.normal(ks[1], (B, Nk, Dc), dtype=jnp.float32), 'Wq': jax.random.normal(ks[2], (Dq, inner), dtype=jnp.float32) * sq, 'Wk': jax.random.normal(ks[3], (Dc, inner), dtype=jnp.float32) * sc, 'Wv': jax.random.normal(ks[4], (Dc, inner), dtype=jnp.float32) * sc, 'Wo': jax.random.normal(ks[5], (inner, Dq), dtype=jnp.float32) * si, 'bo': jax.random.normal(ks[6], (Dq,), dtype=jnp.float32) * 0.01}
    _L0_xattn_all = _L0_xattn_setup()
    _L0_xattn_in = {k: v for k, v in _L0_xattn_all.items() if k in ('Wq', 'Wk', 'Wv', 'Wo', 'bo')}
    del _L0_xattn_all

    def _L0_ffn_setup():
        import jax, jax.numpy as jnp
        import numpy as np
        N_EXPERTS = 8
        TOP_K = 2
        D_MODEL = 256
        HIDDEN = 1024
        ROUTED_H = 256
        BATCH, SEQ = (2, 1024)
        key = jax.random.key(seed)
        ks = jax.random.split(key, 8)
        std = 0.02
        return {'x': jax.random.normal(ks[0], (BATCH, SEQ, D_MODEL), dtype=jnp.float32), 'w12': std * jax.random.normal(ks[1], (N_EXPERTS, 2 * ROUTED_H, D_MODEL), dtype=jnp.float32), 'w3': std * jax.random.normal(ks[2], (N_EXPERTS, D_MODEL, ROUTED_H), dtype=jnp.float32), 'shared_w1': std * jax.random.normal(ks[3], (HIDDEN, D_MODEL), dtype=jnp.float32), 'shared_w2': std * jax.random.normal(ks[4], (HIDDEN, D_MODEL), dtype=jnp.float32), 'shared_w3': std * jax.random.normal(ks[5], (D_MODEL, HIDDEN), dtype=jnp.float32), 'router_w': std * jax.random.normal(ks[6], (N_EXPERTS, D_MODEL), dtype=jnp.float32), 'expert_bias': jnp.zeros((N_EXPERTS,), dtype=jnp.float32)}
    _L0_ffn_all = _L0_ffn_setup()
    _L0_ffn_in = {k: v for k, v in _L0_ffn_all.items() if k in ('w12', 'w3', 'shared_w1', 'shared_w2', 'shared_w3', 'router_w', 'expert_bias')}
    del _L0_ffn_all

    def _L1_attn_setup():
        import jax, jax.numpy as jnp
        import numpy as np
        B, S, D = (2, 512, 256)
        H = 16
        HD = D // H
        SCALE = HD ** (-0.5)

        def _rope_tables(seq_len, dim, dtype=jnp.float32):
            inv_freq = 1.0 / 10000.0 ** (jnp.arange(0, dim, 2, dtype=jnp.float32) / dim)
            t = jnp.arange(seq_len, dtype=jnp.float32)
            freqs = t[:, None] * inv_freq[None, :]
            return (jnp.cos(freqs).astype(dtype), jnp.sin(freqs).astype(dtype))

        def _apply_rope(x, cos, sin):
            half = x.shape[-1] // 2
            x1, x2 = (x[..., :half], x[..., half:])
            c = cos[None, None, :, :]
            s = sin[None, None, :, :]
            rx1 = x1 * c - x2 * s
            rx2 = x1 * s + x2 * c
            return jnp.concatenate([rx1, rx2], axis=-1)
        key = jax.random.key(seed)
        k1, k2, k3 = jax.random.split(key, 3)
        x = jax.random.normal(k1, (B, S, D), dtype=jnp.float32)
        w_qkv = jax.random.normal(k2, (3 * D, D), dtype=jnp.float32) * D ** (-0.5)
        w_out = jax.random.normal(k3, (D, D), dtype=jnp.float32) * D ** (-0.5)
        b_out = jnp.zeros((D,), dtype=jnp.float32)
        return {'x': x, 'w_qkv': w_qkv, 'w_out': w_out, 'b_out': b_out}
    _L1_attn_all = _L1_attn_setup()
    _L1_attn_in = {k: v for k, v in _L1_attn_all.items() if k in ('w_qkv', 'w_out', 'b_out')}
    del _L1_attn_all

    def _L1_xattn_setup():
        import jax, jax.numpy as jnp
        import numpy as np
        HEADS = 16
        DIM_HEAD = 64
        SCALE = DIM_HEAD ** (-0.5)
        key = jax.random.key(seed)
        ks = jax.random.split(key, 6)
        B, N, C = (4, 1024, 256)
        M, Cc = (128, 192)
        inner = HEADS * DIM_HEAD
        s = lambda d: d ** (-0.5)
        return {'x': jax.random.normal(ks[0], (B, N, C), jnp.float32), 'context': jax.random.normal(ks[1], (B, M, Cc), jnp.float32), 'Wq': jax.random.normal(ks[2], (C, inner), jnp.float32) * s(C), 'Wk': jax.random.normal(ks[3], (Cc, inner), jnp.float32) * s(Cc), 'Wv': jax.random.normal(ks[4], (Cc, inner), jnp.float32) * s(Cc), 'Wo': jax.random.normal(ks[5], (inner, C), jnp.float32) * s(inner), 'bo': jnp.zeros((C,), jnp.float32)}
    _L1_xattn_all = _L1_xattn_setup()
    _L1_xattn_in = {k: v for k, v in _L1_xattn_all.items() if k in ('Wq', 'Wk', 'Wv', 'Wo', 'bo')}
    del _L1_xattn_all

    def _L1_ffn_setup():
        import jax, jax.numpy as jnp
        import numpy as np
        B, N, C, H, REG = (1, 2309, 256, 16, 5)
        D = C // H
        key = jax.random.key(seed)
        k0, k1, k2, k3 = jax.random.split(key, 4)
        x = jax.random.normal(k0, (B, N, C), dtype=jnp.float32)
        g_info = jax.random.normal(k1, (12, 2, C), dtype=jnp.float32)
        W_qkv = jax.random.normal(k2, (C, 3 * C), dtype=jnp.float32) * 0.02
        W_proj = jax.random.normal(k3, (C, C), dtype=jnp.float32) * 0.02
        b_proj = jnp.zeros((C,), dtype=jnp.float32)
        return {'x': x, 'g_info': g_info, 'W_qkv': W_qkv, 'W_proj': W_proj, 'b_proj': b_proj}
    _L1_ffn_all = _L1_ffn_setup()
    _L1_ffn_in = {k: v for k, v in _L1_ffn_all.items() if k in ('g_info', 'W_qkv', 'W_proj', 'b_proj')}
    del _L1_ffn_all
    return {'x': x, 'ctx_768': ctx_768, 'L0_attn_W_in': _L0_attn_in['W_in'], 'L0_attn_conv_w': _L0_attn_in['conv_w'], 'L0_attn_conv_b': _L0_attn_in['conv_b'], 'L0_attn_W_xproj': _L0_attn_in['W_xproj'], 'L0_attn_D': _L0_attn_in['D'], 'L0_attn_W_out': _L0_attn_in['W_out'], 'L0_xattn_Wq': _L0_xattn_in['Wq'], 'L0_xattn_Wk': _L0_xattn_in['Wk'], 'L0_xattn_Wv': _L0_xattn_in['Wv'], 'L0_xattn_Wo': _L0_xattn_in['Wo'], 'L0_xattn_bo': _L0_xattn_in['bo'], 'L0_ffn_w12': _L0_ffn_in['w12'], 'L0_ffn_w3': _L0_ffn_in['w3'], 'L0_ffn_shared_w1': _L0_ffn_in['shared_w1'], 'L0_ffn_shared_w2': _L0_ffn_in['shared_w2'], 'L0_ffn_shared_w3': _L0_ffn_in['shared_w3'], 'L0_ffn_router_w': _L0_ffn_in['router_w'], 'L0_ffn_expert_bias': _L0_ffn_in['expert_bias'], 'L1_attn_w_qkv': _L1_attn_in['w_qkv'], 'L1_attn_w_out': _L1_attn_in['w_out'], 'L1_attn_b_out': _L1_attn_in['b_out'], 'L1_xattn_Wq': _L1_xattn_in['Wq'], 'L1_xattn_Wk': _L1_xattn_in['Wk'], 'L1_xattn_Wv': _L1_xattn_in['Wv'], 'L1_xattn_Wo': _L1_xattn_in['Wo'], 'L1_xattn_bo': _L1_xattn_in['bo'], 'L1_ffn_g_info': _L1_ffn_in['g_info'], 'L1_ffn_W_qkv': _L1_ffn_in['W_qkv'], 'L1_ffn_W_proj': _L1_ffn_in['W_proj'], 'L1_ffn_b_proj': _L1_ffn_in['b_proj']}

def reference(x, ctx_768, L0_attn_W_in, L0_attn_conv_w, L0_attn_conv_b, L0_attn_W_xproj, L0_attn_D, L0_attn_W_out, L0_xattn_Wq, L0_xattn_Wk, L0_xattn_Wv, L0_xattn_Wo, L0_xattn_bo, L0_ffn_w12, L0_ffn_w3, L0_ffn_shared_w1, L0_ffn_shared_w2, L0_ffn_shared_w3, L0_ffn_router_w, L0_ffn_expert_bias, L1_attn_w_qkv, L1_attn_w_out, L1_attn_b_out, L1_xattn_Wq, L1_xattn_Wk, L1_xattn_Wv, L1_xattn_Wo, L1_xattn_bo, L1_ffn_g_info, L1_ffn_W_qkv, L1_ffn_W_proj, L1_ffn_b_proj):
    import jax
    import jax.numpy as jnp

    def _L0_attn_ref(x, W_in, conv_w, conv_b, W_xproj, D, W_out):
        import jax, jax.numpy as jnp
        import numpy as np
        D_STATE = 16

        def _silu(v):
            return v * jax.nn.sigmoid(v)
        Bsz, L, _ = x.shape
        d_inner, d_conv = conv_w.shape
        d_state = D_STATE
        xz = jnp.einsum('bld,ed->ble', x, W_in)
        xb, z = (xz[..., :d_inner], xz[..., d_inner:])
        xpad = jnp.pad(xb, ((0, 0), (d_conv - 1, 0), (0, 0)))
        xc = conv_b
        for k in range(d_conv):
            xc = xc + conv_w[:, k] * xpad[:, k:k + L, :]
        xc = _silu(xc)
        proj = jnp.einsum('bld,ed->ble', xc, W_xproj)
        Bm = proj[..., :d_state]
        Cm = proj[..., d_state:2 * d_state]
        delta = jax.nn.softplus(proj[..., 2 * d_state:])
        bc = jnp.einsum('bls,bls->bl', Bm, Cm)
        y = delta * xc * bc[..., None] + D * xc
        y = y * _silu(z)
        return jnp.einsum('bld,ed->ble', y, W_out)

    def _L0_xattn_ref(x, context, Wq, Wk, Wv, Wo, bo):
        import jax, jax.numpy as jnp
        import numpy as np
        HEADS = 16
        DIM_HEAD = 64
        B, Nq, _ = x.shape
        Nk = context.shape[1]
        h, dh = (HEADS, DIM_HEAD)
        q = (x @ Wq).reshape(B, Nq, h, dh)
        k = (context @ Wk).reshape(B, Nk, h, dh)
        v = (context @ Wv).reshape(B, Nk, h, dh)
        scale = 1.0 / jnp.sqrt(jnp.asarray(dh, dtype=x.dtype))
        scores = jnp.einsum('bqhd,bkhd->bhqk', q, k) * scale
        attn = jax.nn.softmax(scores, axis=-1)
        out = jnp.einsum('bhqk,bkhd->bqhd', attn, v).reshape(B, Nq, h * dh)
        return out @ Wo + bo

    def _L0_ffn_ref(x, w12, w3, shared_w1, shared_w2, shared_w3, router_w, expert_bias):
        import jax, jax.numpy as jnp
        import numpy as np
        N_EXPERTS = 8
        TOP_K = 2
        D_MODEL = 256
        HIDDEN = 1024
        ROUTED_H = 256
        BATCH, SEQ = (2, 1024)
        b, s, d = x.shape
        xf = x.reshape(-1, d)
        shared = jax.nn.silu(xf @ shared_w1.T) * (xf @ shared_w2.T) @ shared_w3.T
        scores = jax.nn.sigmoid(xf @ router_w.T)
        _, top_idx = jax.lax.top_k(scores + expert_bias, TOP_K)
        mask = jax.nn.one_hot(top_idx, N_EXPERTS, dtype=xf.dtype).sum(axis=-2)
        gates = scores * mask
        h12 = jnp.einsum('td,ehd->teh', xf, w12)
        h1, h2 = jnp.split(h12, 2, axis=-1)
        h = jax.nn.silu(h1) * h2 * gates[:, :, None]
        routed = jnp.einsum('teh,edh->td', h, w3)
        return (shared + routed).reshape(b, s, d)

    def _L1_attn_ref(x, w_qkv, w_out, b_out):
        import jax, jax.numpy as jnp
        import numpy as np
        B, S, D = (2, 512, 256)
        H = 16
        HD = D // H
        SCALE = HD ** (-0.5)

        def _rope_tables(seq_len, dim, dtype=jnp.float32):
            inv_freq = 1.0 / 10000.0 ** (jnp.arange(0, dim, 2, dtype=jnp.float32) / dim)
            t = jnp.arange(seq_len, dtype=jnp.float32)
            freqs = t[:, None] * inv_freq[None, :]
            return (jnp.cos(freqs).astype(dtype), jnp.sin(freqs).astype(dtype))

        def _apply_rope(x, cos, sin):
            half = x.shape[-1] // 2
            x1, x2 = (x[..., :half], x[..., half:])
            c = cos[None, None, :, :]
            s = sin[None, None, :, :]
            rx1 = x1 * c - x2 * s
            rx2 = x1 * s + x2 * c
            return jnp.concatenate([rx1, rx2], axis=-1)
        b, s, d = x.shape
        qkv = jnp.einsum('bsd,ed->bse', x, w_qkv)
        qkv = qkv.reshape(b, s, 3, H, HD).transpose(2, 0, 3, 1, 4)
        q, k, v = (qkv[0], qkv[1], qkv[2])
        cos, sin = _rope_tables(s, HD, x.dtype)
        q = _apply_rope(q, cos, sin)
        k = _apply_rope(k, cos, sin)
        scores = jnp.einsum('bhsd,bhtd->bhst', q, k) * SCALE
        attn = jax.nn.softmax(scores, axis=-1)
        out = jnp.einsum('bhst,bhtd->bhsd', attn, v)
        out = out.transpose(0, 2, 1, 3).reshape(b, s, d)
        return jnp.einsum('bsd,ed->bse', out, w_out) + b_out

    def _L1_xattn_ref(x, context, Wq, Wk, Wv, Wo, bo):
        import jax, jax.numpy as jnp
        import numpy as np
        HEADS = 16
        DIM_HEAD = 64
        SCALE = DIM_HEAD ** (-0.5)
        B, N, _ = x.shape
        M = context.shape[1]
        q = (x @ Wq).reshape(B, N, HEADS, DIM_HEAD).transpose(0, 2, 1, 3)
        k = (context @ Wk).reshape(B, M, HEADS, DIM_HEAD).transpose(0, 2, 1, 3)
        v = (context @ Wv).reshape(B, M, HEADS, DIM_HEAD).transpose(0, 2, 1, 3)
        dots = jnp.einsum('bhnd,bhmd->bhnm', q, k) * SCALE
        attn = jax.nn.softmax(dots, axis=-1)
        out = jnp.einsum('bhnm,bhmd->bhnd', attn, v)
        out = out.transpose(0, 2, 1, 3).reshape(B, N, HEADS * DIM_HEAD)
        return out @ Wo + bo

    def _L1_ffn_ref(x, g_info, W_qkv, W_proj, b_proj):
        import jax, jax.numpy as jnp
        import numpy as np
        B, N, C, H, REG = (1, 2309, 256, 16, 5)
        D = C // H
        Bx, Nx, Cx = x.shape
        scale = D ** (-0.5)
        qkv = (x @ W_qkv).reshape(Bx, Nx, 3, H, D)
        q, k, v = (qkv[:, :, 0], qkv[:, :, 1], qkv[:, :, 2])
        g_layer = g_info[0].reshape(-1, H, D)
        q_g = g_layer[0]
        q_pure = q[:, REG:]
        q_n = q_pure / jnp.linalg.norm(q_pure, axis=-1, keepdims=True)
        qg_n = q_g / jnp.linalg.norm(q_g, axis=-1, keepdims=True)
        sim = (qg_n[None, None] * q_n).sum(-1).mean(-1)
        sim = (sim - sim.min()) / (sim.max() - sim.min())
        pos = sim > 0.9
        logits = jnp.einsum('bqhd,bkhd->bhqk', q * scale, k)

        def masked_attn(tok_mask):
            key_mask = jnp.concatenate([jnp.ones((Bx, REG), bool), tok_mask], axis=1)
            l = jnp.where(key_mask[:, None, None, :], logits, -jnp.inf)
            a = jax.nn.softmax(l, axis=-1)
            return jnp.einsum('bhqk,bkhd->bqhd', a, v)
        x_pos = masked_attn(pos)
        x_neg = masked_attn(~pos)
        reg_out = (x_pos[:, :REG] + x_neg[:, :REG]) * 0.5
        tok_out = jnp.where(pos[:, :, None, None], x_pos[:, REG:], x_neg[:, REG:])
        out = jnp.concatenate([reg_out, tok_out], axis=1).reshape(Bx, Nx, Cx)
        return out @ W_proj + b_proj
    x = _layernorm(x + _L0_attn_ref(x, L0_attn_W_in, L0_attn_conv_w, L0_attn_conv_b, L0_attn_W_xproj, L0_attn_D, L0_attn_W_out), axis=-1)
    x = _layernorm(x + _L0_xattn_ref(x, ctx_768, L0_xattn_Wq, L0_xattn_Wk, L0_xattn_Wv, L0_xattn_Wo, L0_xattn_bo), axis=-1)
    x = _layernorm(x + _L0_ffn_ref(x, L0_ffn_w12, L0_ffn_w3, L0_ffn_shared_w1, L0_ffn_shared_w2, L0_ffn_shared_w3, L0_ffn_router_w, L0_ffn_expert_bias), axis=-1)
    x = _layernorm(x + _L1_attn_ref(x, L1_attn_w_qkv, L1_attn_w_out, L1_attn_b_out), axis=-1)
    x = _layernorm(x + _L1_xattn_ref(x, ctx_768, L1_xattn_Wq, L1_xattn_Wk, L1_xattn_Wv, L1_xattn_Wo, L1_xattn_bo), axis=-1)
    x = _layernorm(x + _L1_ffn_ref(x, L1_ffn_g_info, L1_ffn_W_qkv, L1_ffn_W_proj, L1_ffn_b_proj), axis=-1)
    return x

_drawn_inputs = setup_inputs


def setup_inputs(seed=0):
    import zlib

    import numpy as np

    out = dict(_drawn_inputs(seed))
    spreads = {'L0_attn_D': (1.0, 0.6),
     'L0_ffn_expert_bias': (0.0, 0.7),
     'L1_attn_b_out': (0.0, 0.1),
     'L1_xattn_bo': (0.0, 0.1),
     'L1_ffn_b_proj': (0.0, 0.1)}
    factors = {'L0_attn_W_in': 8.0,
     'L0_attn_conv_w': 8.0,
     'L0_attn_conv_b': 8.0,
     'L0_attn_W_xproj': 8.0,
     'L0_attn_W_out': 7.254,
     'L0_xattn_bo': 5.596,
     'L0_ffn_w12': 5.229,
     'L0_ffn_w3': 4.857,
     'L0_ffn_router_w': 7.997,
     'L1_ffn_g_info': 64.0,
     'L0_ffn_shared_w1': 5.091,
     'L0_ffn_shared_w2': 5.053,
     'L0_ffn_shared_w3': 5.023}
    for name, (base, spread) in spreads.items():
        noise = np.random.default_rng([zlib.crc32(name.encode()), seed]).standard_normal(out[name].shape)
        drawn = base * np.exp(spread * noise) if base else spread * noise
        out[name] = jnp.asarray(drawn.astype(out[name].dtype))
    for name, factor in factors.items():
        out[name] = (out[name] * factor).astype(out[name].dtype)
    return out
```

```python
from contextlib import ExitStack

import numpy as np

import concourse.bass as bass
from concourse import mybir

F32 = mybir.dt.float32
ALU = mybir.AluOpType
ACT = mybir.ActivationFunctionType
AX = mybir.AxisListType
RMAX = bass.bass_isa.ReduceOp.max

P = 128
B, S, D, CK, CD = 8, 256, 256, 77, 192
H = 16
NE = 8
REG = 5
BIG = float(2.0 ** 100)
EPS = 1e-5

LAY0 = [("win", 2048), ("conv", 24), ("wxp", 2176), ("wout", 1024), ("wq", 2048), ("wkv", 3072), ("wo", 2048), ("bo", 256)]
LAYQ = [("w12", 8192), ("w3", 4096), ("s12", 4096), ("rw", 16), ("rb", 8), ("s3", 2048)]
LAY1 = [("wqkv", 1536), ("wao", 512), ("bao", 256), ("wq", 2048), ("wkv", 3072), ("wo", 2048), ("bo", 256),
        ("fqkv", 1536), ("fproj", 512), ("fb", 256), ("g", 256)]
LAYC = [("ident", 128), ("ones", 128), ("ropec", 32), ("ropes", 32), ("tri", 64), ("vm", 16), ("vmi", 16), ("half", 32)]


def places(lay):
    at, out = 0, {}
    for name, n in lay:
        out[name] = (at, n)
        at += n
    return out, at


P0, N0 = places(LAY0)
PQ, NQ = places(LAYQ)
P1, N1 = places(LAY1)
PC, NC_ = places(LAYC)
NSTREAM = 6040
NAUX = 3084


class Token:

    def __init__(self, lane, index):
        self.lane, self.index, self.used = lane, index, False


class Lane:

    def __init__(self, name, sem):
        self.name, self.sem, self.items = name, sem, []

    def wait(self, *tokens):
        for t in tokens:
            if t is not None:
                t.used = True
                self.items.append(("wait", t))

    def do(self, call):
        t = Token(self, len(self.items))
        self.items.append(("do", call, t))
        return t

    def count(self):
        n = 0
        for it in self.items:
            if it[0] == "do" and it[2].used:
                n += 1
                it[2].value = n

    def emit(self, eng):
        seen = {}
        for it in self.items:
            if it[0] == "wait":
                t = it[1]
                if seen.get(t.lane.name, 0) < t.value:
                    seen[t.lane.name] = t.value
                    eng.wait_ge(t.lane.sem, t.value)
            else:
                ins = it[1](eng)
                if it[2].used:
                    ins.then_inc(self.sem, 1)


class Stream:
    pass


def program(nc, x_in, ctx_in, w0_in, wq_in, w1_in, const_in, out):
    es = ExitStack()
    with es:
        def sb(name, n):
            return es.enter_context(nc.sbuf_tensor(name, [P, n], F32))

        def sem(name):
            return es.enter_context(nc.semaphore(name))

        xres = sb("xres", 16 * D)
        ctxT = sb("ctxT", 2 * B * CK)
        cst = sb("cst", NC_)
        regP = sb("regP", max(N0, N1))
        regQ = sb("regQ", NQ)
        small = sb("small", 512)
        x = xres[:, :].rearrange("p (t d) -> p t d", d=D)
        ctx = ctxT[:, :].rearrange("p (k n) -> p k n", k=2)

        def part(t, pl, name, c=None):
            a, n = pl[name]
            v = t[:, a:a + n]
            return v if c is None else v.rearrange("p (c n) -> p c n", c=c)

        ident = part(cst, PC, "ident")
        ones = part(cst, PC, "ones")
        ropec = part(cst, PC, "ropec", 2)
        ropes = part(cst, PC, "ropes", 2)
        tri = part(cst, PC, "tri", 8)
        vm = part(cst, PC, "vm")
        vmi = part(cst, PC, "vmi")
        mhalf = part(cst, PC, "half")

        pe, act, dve, pool = (Lane(n, sem(f"s_{n}")) for n in ("pe", "act", "dve", "pool"))
        d_cst, d_x, d_ctx, d_w0, d_wq, d_s3, d_w1, d_out = (
            sem(f"d_{n}") for n in ("cst", "x", "ctx", "w0", "wq", "s3", "w1", "out"))

        def loaded(lane, s, v=16):
            lane.items.append(("do", lambda e: e.wait_ge(s, v), Token(lane, 0)))

        streams = []
        for i in range(2):
            st = Stream()
            st.i = i
            st.xTt = sb(f"xT{i}", 512)
            st.xT = st.xTt[:, :].rearrange("p (k n) -> p k n", k=2)
            st.m = sb(f"main{i}", NSTREAM)
            st.sm = sb(f"sm{i}", 448)
            st.ps = es.enter_context(nc.psum_tensor(f"ps{i}", [P, 2048], F32))
            st.bf = [None] * 4
            st.xT_rd = None
            st.last = {"pe": None, "act": None, "dve": None, "pool": None}
            st.batches = [b for b in range(B) if b % 2 == i]
            st.pt = regQ[:, PQ["s3"][0] + 1024 * i:PQ["s3"][0] + 1024 * (i + 1)]
            a = 16 * 768 + NAUX * i
            st.aux = regQ[:, a:a + NAUX]
            streams.append(st)
        qkvall = regQ[:, 0:16 * 768].rearrange("p (t e) -> p t e", e=768)

        x_ok = [None] * 16
        st_free = {}

        def bank(st, i, n=512):
            return st.ps[:, 512 * i:512 * i + n]

        def pair(st, i):
            return st.ps[:, 1024 * i:1024 * (i + 1)]

        def mm(o, l, r, start, stop):
            return pe.do(lambda e: e.matmul(o, l, r, start=start, stop=stop))

        def tp(o, i, n=128):
            return pe.do(lambda e: e.transpose(o, i, ident[0:n, 0:n]))

        def copy(o, i):
            return act.do(lambda e: e.activation(o, i, ACT.Copy))

        def func(o, i, f, scale=1.0, bias=0.0):
            return act.do(lambda e: e.activation(o, i, f, scale=scale, bias=bias))

        def tt(o, a, b_, op, lane=None):
            return (lane or dve).do(lambda e: e.tensor_tensor(o, a, b_, op))

        def ts(o, a, s1, s2, op0, op1=None, lane=None):
            if op1 is None:
                return (lane or dve).do(lambda e: e.tensor_scalar(o, a, s1, None, op0))
            return (lane or dve).do(lambda e: e.tensor_scalar(o, a, s1, s2, op0, op1))

        def stt(o, a, s, b_, op0, op1):
            return dve.do(lambda e: e.scalar_tensor_tensor(out=o, in0=a, scalar=s, in1=b_, op0=op0, op1=op1))

        def mset(lane, o, v):
            return lane.do(lambda e: e.memset(o, v))

        def fence(st):
            for lane in (pe, act, dve, pool):
                lane.wait(*[t for n, t in st.last.items() if n != lane.name])

        def ended(st, **last):
            st.last.update(last)

        def to_xT(st, b):
            pe.wait(x_ok[2 * b], x_ok[2 * b + 1], st.bf[0])
            bk = bank(st, 0)
            for c in range(2):
                for j in range(2):
                    m = tp(bk[:, c * 256 + j * 128:c * 256 + (j + 1) * 128], x[:, 2 * b + j, c * 128:(c + 1) * 128])
            st.xT_src = m
            act.wait(m, st.xT_rd)
            st.xT_ok = copy(st.xTt[:, :], bk)
            st.bf[0] = st.xT_ok

        def add_bias(st, b, bias):
            pool.wait(st.xT_src, x_ok[2 * b], x_ok[2 * b + 1])
            for j in range(2):
                t = tt(x[:, 2 * b + j, :], x[:, 2 * b + j, :], bias, ALU.add, pool)
            return t

        def layernorm(st, b, ps=None, bk=None, after=(), final=False):
            xb = x[:, 2 * b:2 * b + 2, :]
            dve.wait(x_ok[2 * b], x_ok[2 * b + 1], *after)
            if ps is not None:
                r = tt(xb, ps, xb, ALU.add)
                st.bf[bk] = r
                dve.wait(r)
            s6 = st.sm[:, 0:12].rearrange("p (j n) -> p j n", j=2)
            mv = st.sm[:, 12:16].rearrange("p (j n) -> p j n", j=2)
            rs = st.sm[:, 16:18]
            t = [dve.do(lambda e, j=j: e.bn_stats(s6[:, j, :], xb[:, j, :])) for j in range(2)]
            for j in range(2):
                dve.wait(t[j])
                g = dve.do(lambda e, j=j: e.bn_aggr(mv[:, j, :], s6[:, j, :]))
            pool.wait(g)
            a = ts(rs, mv[:, :, 1], EPS, None, ALU.add, None, pool)
            pool.wait(a)
            q = tt(rs, rs, mhalf[:, 0:2], ALU.pow, pool)
            dve.wait(q, g)
            for j in range(2):
                n = ts(xb[:, j, :], xb[:, j, :], mv[:, j, 0:1], rs[:, j:j + 1], ALU.subtract, ALU.mult)
                x_ok[2 * b + j] = n
                if final:
                    outs.append((2 * b + j, n))
            ended(st, dve=n, pool=q)

        outs = []

        def l0_attn(st, b):
            fence(st)
            xb = st.m[:, 0:1036].rearrange("p (c n) -> p c n", c=4)
            xcf = st.m[:, 1036:2060]
            xc = xcf.rearrange("p (c n) -> p c n", c=4)
            szf = st.m[:, 2060:3084]
            sz = szf.rearrange("p (c n) -> p c n", c=4)
            tAf = st.m[:, 3084:4108]
            tA = tAf.rearrange("p (c n) -> p c n", c=4)
            Bc = st.m[:, 4108:4364]
            win = part(regP, P0, "win", 2)
            cv = part(regP, P0, "conv", 4)
            wxp = part(regP, P0, "wxp", 4)
            wout = part(regP, P0, "wout", 4)
            z0 = mset(dve, xb[:, :, 0:3], 0.0)
            to_xT(st, b)
            yield
            pe.wait(st.xT_ok, st.bf[2], st.bf[3])
            for c in range(4):
                for k in range(2):
                    m = mm(st.ps[:, 1024 + c * 256:1280 + c * 256], win[:, k, c * 128:(c + 1) * 128], st.xT[:, k, :], k == 0, k == 1)
            act.wait(m)
            cp = copy(xb[:, :, 3:259], pair(st, 1).rearrange("p (c n) -> p c n", c=4))
            st.bf[2] = st.bf[3] = cp
            pe.wait(st.bf[0], st.bf[1])
            for c in range(4):
                for k in range(2):
                    m = mm(st.ps[:, c * 256:256 + c * 256], win[:, k, 512 + c * 128:512 + (c + 1) * 128], st.xT[:, k, :], k == 0, k == 1)
            st.xT_rd = m
            act.wait(m)
            zs = func(szf, pair(st, 0), ACT.Silu)
            st.bf[0] = st.bf[1] = zs
            yield
            dve.wait(cp, z0)
            last = [ts(xc[:, c, :], xb[:, c, 3:259], cv[:, c, 3:4], cv[:, c, 4:5], ALU.mult, ALU.add) for c in range(4)]
            for k in (2, 1, 0):
                for c in range(4):
                    dve.wait(last[c])
                    last[c] = stt(xc[:, c, :], xb[:, c, k:k + 256], cv[:, c, k:k + 1], xc[:, c, :], ALU.mult, ALU.add)
            act.wait(last[3])
            xs = func(xcf, xcf, ACT.Silu)
            yield
            pe.wait(xs, st.bf[2], st.bf[3])
            for c in range(4):
                for k in range(4):
                    m = mm(st.ps[:, 1024 + c * 256:1280 + c * 256], wxp[:, k, 32 + c * 128:32 + (c + 1) * 128], xc[:, k, :], k == 0, k == 3)
            pe.wait(st.bf[0])
            for c in range(2):
                for k in range(4):
                    m2 = mm(st.ps[0:16, c * 256:(c + 1) * 256], wxp[:, k, 16 * c:16 * c + 16], xc[:, k, :], k == 0, k == 3)
            act.wait(m2)
            t = copy(Bc[0:16, :], st.ps[0:16, 0:256])
            dve.wait(t, m)
            t = tt(Bc[0:16, :], Bc[0:16, :], st.ps[0:16, 256:512], ALU.mult)
            st.bf[0] = t
            pe.wait(t, st.bf[1])
            mb = mm(st.ps[:, 512:768], ones[0:16, :], Bc[0:16, :], True, True)
            yield
            t = ts(tAf, pair(st, 1), 30.0, None, ALU.min)
            act.wait(t)
            t = func(tAf, tAf, ACT.Exp)
            act.wait(t)
            t = func(tAf, tAf, ACT.Ln, bias=1.0)
            dve.wait(t)
            t = tt(tAf, tAf, pair(st, 1), ALU.max)
            st.bf[2] = st.bf[3] = t
            dve.wait(t, mb)
            t = tt(tA, tA, st.ps[:, 512:768].unsqueeze(1).to_broadcast([P, 4, 256]), ALU.mult)
            st.bf[1] = t
            dve.wait(t, xs, zs)
            for c in range(4):
                t = stt(tA[:, c, :], tA[:, c, :], cv[:, c, 5:6], xc[:, c, :], ALU.add, ALU.mult)
            dve.wait(t)
            t = tt(szf, szf, tAf, ALU.mult)
            yield
            pe.wait(t, st.bf[3])
            for j in range(2):
                for k in range(4):
                    m = mm(bank(st, 3)[:, j * 256:(j + 1) * 256], sz[:, k, j * 128:(j + 1) * 128], wout[:, k, :], k == 0, k == 3)
            ended(st, pe=m, act=zs)
            layernorm(st, b, bank(st, 3).rearrange("p (j n) -> p j n", j=2), 3, (m,))
            yield

        def xattn(st, b, pl, lay, PT, ptf):
            fence(st)
            QTf = st.m[:, 0:2048]
            QT = QTf.rearrange("p (c n) -> p c n", c=8)
            KT = st.m[:, 2048:2664].rearrange("p (c n) -> p c n", c=8)
            V = st.m[0:CK, 2664:3704].rearrange("p (h n) -> p h n", h=16)
            O = st.m[:, 3704:5752].rearrange("p (j n) -> p j n", j=2)
            nmT = st.m[:, 5752:6008]
            nm = st.sm[:, 32:288].rearrange("p (j n) -> p j n", j=2)
            rc = st.sm[:, 288:296].rearrange("p (j n) -> p j n", j=2)
            wq = part(regP, pl, "wq", 2)
            wkv = part(regP, pl, "wkv", 3)
            wo = part(regP, pl, "wo", 8)
            kw = [(wkv[:, 0, :], 0, 128, 0), (wkv[0:64, 2, :], 0, 64, 1)]
            vw = [(wkv[:, 1, :], 0, 128, 0), (wkv[64:128, 2, :], 64, 64, 1)]
            pool.wait(st.last["pool"])
            mset(pool, st.sm[:, 32:288], 0.0)
            one = mset(pool, V[:, :, 64:65], 1.0)
            to_xT(st, b)
            xbias = add_bias(st, b, part(regP, pl, "bo"))
            pe.wait(st.bf[2], st.bf[3])
            for c in range(8):
                for k, (w, p0, n, r) in enumerate(kw):
                    m = mm(st.ps[:, 1024 + 512 * (c // 4) + 77 * (c % 4):1024 + 512 * (c // 4) + 77 * (c % 4) + 77],
                           w[:, c * 128:(c + 1) * 128], ctx[p0:p0 + n, r, b * CK:(b + 1) * CK], k == 0, k == 1)
            act.wait(m)
            for i in range(2):
                kok = copy(KT[:, 4 * i:4 * i + 4, :], bank(st, 2 + i)[:, 0:308].rearrange("p (c n) -> p c n", c=4))
            st.bf[2] = st.bf[3] = kok
            yield
            pe.wait(st.bf[0], st.bf[1])
            for i in range(2):
                for k, (w, p0, n, r) in enumerate(vw):
                    m = mm(bank(st, i)[0:CK, :], ctx[p0:p0 + n, r, b * CK:(b + 1) * CK], w[:, i * 512:(i + 1) * 512], k == 0, k == 1)
            act.wait(m)
            vok = copy(V[:, :, 0:64], st.ps[0:CK, 0:1024].rearrange("p (h n) -> p h n", h=16))
            st.bf[0] = st.bf[1] = vok
            yield
            pe.wait(st.xT_ok)
            for i in (1, 0):
                pe.wait(st.bf[2 * i], st.bf[2 * i + 1])
                for c in range(4):
                    cc = c + 4 * (1 - i)
                    for k in range(2):
                        m = mm(pair(st, i)[:, c * 256:(c + 1) * 256], wq[:, k, cc * 128:(cc + 1) * 128], st.xT[:, k, :], k == 0, k == 1)
                act.wait(m)
                qok = copy(QTf[:, 1024 * (1 - i):1024 * (2 - i)], pair(st, i))
                st.bf[2 * i] = st.bf[2 * i + 1] = qok
            st.xT_rd = m
            yield
            pe.wait(qok, kok)
            for j in range(2):
                for i in range(2):
                    pe.wait(st.bf[2 * i], st.bf[2 * i + 1])
                    for hh in range(8):
                        h = 8 * i + hh
                        r = 64 * (h % 2)
                        m = mm(bank(st, 2 * i + hh % 2)[:, 77 * (hh // 2):77 * (hh // 2) + 77],
                               QT[r:r + 64, h // 2, j * 128:(j + 1) * 128], KT[r:r + 64, h // 2, :], True, True)
                    dve.wait(m, one)
                    src = pair(st, i).rearrange("p (a n) -> p a n", a=2)[:, :, 0:308].rearrange("p a (c n) -> p a c n", c=4)
                    dst = nm[:, j, 8 * i:8 * i + 8].rearrange("p (c a) -> p a c", a=2)
                    t = dve.do(lambda e, dst=dst, src=src: e.tensor_reduce(dst, src, AX.X, ALU.max, negate=True))
                    dve.wait(t)
                    up = dve.do(lambda e, i=i, j=j: e.tensor_copy(nm[:, j, 64 + 8 * i:72 + 8 * i], nm[:, j, 8 * i:8 * i + 8]))
                    st.bf[2 * i] = st.bf[2 * i + 1] = t
                yield
            pe.wait(up, t)
            for j in range(2):
                m = tp(st.ps[:, j * 128:(j + 1) * 128], nm[:, j, :])
            act.wait(m)
            nok = copy(nmT, st.ps[:, 0:256])
            st.bf[0] = nok
            pe.wait(nok)
            first = True
            for g in range(4):
                pe.wait(st.bf[0], st.bf[1])
                for hh in range(4):
                    h = 4 * g + hh
                    r = 64 * (h % 2)
                    at = (hh % 2) * 512 + (hh // 2) * 256
                    o = st.ps[0:CK, at:at + 256]
                    mm(o, KT[r:r + 64, h // 2, :], QT[r:r + 64, h // 2, :], True, False)
                    m = mm(o, ident[r:r + 64, r + h:r + h + 1].to_broadcast([64, CK]), nmT[r:r + 64, :], False, True)
                act.wait(m, None if first else mo)
                eok = func(ptf[0:CK, :], st.ps[0:CK, 0:1024], ACT.Exp, scale=0.125)
                st.bf[0] = st.bf[1] = eok
                yield
                pe.wait(eok, vok, one, st.bf[2], st.bf[3])
                for j in range(2):
                    for hh in range(4):
                        mo = mm(bank(st, 2 + j)[:, hh * 65:(hh + 1) * 65], PT[0:CK, 2 * (hh % 2) + hh // 2, j * 128:(j + 1) * 128],
                                V[:, 4 * g + hh, :], True, True)
                dve.wait(mo)
                ob = pair(st, 1).rearrange("p (j n) -> p j n", j=2)[:, :, 0:260].rearrange("p j (c n) -> p j c n", c=4)
                t = dve.do(lambda e, ob=ob: e.reciprocal(rc, ob[:, :, :, 64]))
                dve.wait(t)
                for j in range(2):
                    t = tt(O[:, j, 256 * g:256 * (g + 1)].rearrange("p (c n) -> p c n", c=4), ob[:, j, :, 0:64],
                           rc[:, j, :].unsqueeze(2).to_broadcast([P, 4, 64]), ALU.mult)
                st.bf[2] = st.bf[3] = t
                first = False
                yield
            pe.wait(t)
            for i in range(2):
                pe.wait(st.bf[2 * i], st.bf[2 * i + 1])
                for c in range(4):
                    for j in range(2):
                        m = tp(pair(st, i)[:, c * 256 + j * 128:c * 256 + (j + 1) * 128], O[:, j, (4 * i + c) * 128:(4 * i + c + 1) * 128])
                act.wait(m)
                ook = copy(QTf[:, 1024 * i:1024 * (i + 1)], pair(st, i))
                st.bf[2 * i] = st.bf[2 * i + 1] = ook
            pe.wait(ook)
            for j in range(2):
                for c in range(8):
                    m = mm(bank(st, 0)[:, j * 256:(j + 1) * 256], QT[:, c, j * 128:(j + 1) * 128], wo[:, c, :], c == 0, c == 7)
            ended(st, pe=m, act=ook)
            layernorm(st, b, bank(st, 0).rearrange("p (j n) -> p j n", j=2), 0, (m, xbias))
            yield

        def moe(st, b):
            fence(st)
            hb = [st.m[:, 512 * i:512 * (i + 1)] for i in range(2)]
            sc = st.sm[:, 32:48]
            v = st.sm[:, 48:64]
            gate = st.sm[:, 64:80]
            cmp1 = st.sm[:, 80:208]
            cmp2 = st.sm[:, 208:336]
            rank = st.sm[:, 336:352]
            w12 = part(regQ, PQ, "w12", 16)
            w3 = part(regQ, PQ, "w3", 16)
            s12 = part(regQ, PQ, "s12", 8)
            s3 = part(regQ, PQ, "s3", 8)
            rw = part(regQ, PQ, "rw", 2)
            rb = part(regQ, PQ, "rb")
            to_xT(st, b)
            src = st.xT_src
            pe.wait(st.xT_ok, st.bf[1])
            for j in range(2):
                for k in range(2):
                    m = mm(bank(st, 1)[:, 8 * j:8 * j + 8], st.xT[:, k, j * 128:(j + 1) * 128], rw[:, k, :], k == 0, k == 1)
            act.wait(m)
            t = func(sc, bank(st, 1)[:, 0:16], ACT.Tanh, scale=0.5)
            st.bf[1] = t
            dve.wait(t)
            t = ts(sc, sc, 0.5, 0.5, ALU.mult, ALU.add)
            dve.wait(t)
            t = tt(v.rearrange("p (j e) -> p j e", j=2), sc.rearrange("p (j e) -> p j e", j=2),
                   rb.unsqueeze(1).to_broadcast([P, 2, 8]), ALU.add)
            dve.wait(t)
            for j in range(2):
                mine = v[:, 8 * j:8 * j + 8].unsqueeze(2).to_broadcast([P, 8, 8])
                other = v[:, 8 * j:8 * j + 8].unsqueeze(1).to_broadcast([P, 8, 8])
                c1 = cmp1[:, 64 * j:64 * j + 64].rearrange("p (e f) -> p e f", e=8)
                c2 = cmp2[:, 64 * j:64 * j + 64].rearrange("p (e f) -> p e f", e=8)
                tt(c1, other, mine, ALU.is_gt)
                t = tt(c2, other, mine, ALU.is_equal)
                dve.wait(t)
                t = tt(c2, c2, tri, ALU.mult)
            dve.wait(t)
            t = tt(cmp1, cmp1, cmp2, ALU.add)
            dve.wait(t)
            t = dve.do(lambda e: e.tensor_reduce(rank, cmp1.rearrange("p (a f) -> p a f", f=8), AX.X, ALU.add))
            dve.wait(t)
            gok = stt(gate, rank, 2.0, sc, ALU.is_lt, ALU.mult)
            acc = gok
            yield
            mh = [None, None]
            prev = None

            def down(prev):
                u, hok, w = prev
                yb = 2 + u % 2
                pe.wait(hok, st.bf[yb])
                for j in range(2):
                    for k in range(2):
                        m = mm(bank(st, yb)[:, j * 256:(j + 1) * 256], hb[u % 2].rearrange("p (k n) -> p k n", k=2)[:, k, j * 128:(j + 1) * 128],
                               w[:, k, :], k == 0, k == 1)
                mh[u % 2] = m
                dve.wait(m, down.acc, src)
                for j in range(2):
                    xs = x[:, 2 * b + j, :]
                    if u < NE:
                        t = stt(xs, bank(st, yb)[:, j * 256:(j + 1) * 256], gate[:, 8 * j + u:8 * j + u + 1], xs, ALU.mult, ALU.add)
                    else:
                        t = tt(xs, bank(st, yb)[:, j * 256:(j + 1) * 256], xs, ALU.add)
                st.bf[yb] = t
                down.acc = t

            down.acc = acc
            for u in range(NE + 4):
                if u < NE:
                    up = [w12[:, 2 * u + k, :] for k in range(2)]
                    dn = w3[:, 2 * u:2 * u + 2, :]
                    cols = [(0, 0), (0, 128), (1, 256), (1, 384)]
                else:
                    up = [s12[:, 2 * (u - NE) + k, :] for k in range(2)]
                    dn = s3[:, 2 * (u - NE):2 * (u - NE) + 2, :]
                    cols = [(0, 0), (0, 128), (1, 256), (1, 384)]
                pe.wait(st.bf[0], st.bf[1])
                for n, (bk, cc) in enumerate(cols):
                    for k in range(2):
                        m = mm(bank(st, bk)[:, (n % 2) * 256:(n % 2 + 1) * 256], up[k][:, cc:cc + 128], st.xT[:, k, :], k == 0, k == 1)
                    if n == 1:
                        act.wait(m, mh[u % 2])
                        sok = func(hb[u % 2], bank(st, 0), ACT.Silu)
                        st.bf[0] = sok
                if u == NE + 3:
                    st.xT_rd = m
                dve.wait(m, sok)
                hok = tt(hb[u % 2], hb[u % 2], bank(st, 1), ALU.mult)
                st.bf[1] = hok
                if prev is not None:
                    down(prev)
                prev = (u, hok, dn)
                yield
            down(prev)
            ended(st, pe=mh[(NE + 3) % 2], act=sok)
            x_ok[2 * b] = x_ok[2 * b + 1] = down.acc
            layernorm(st, b)
            yield

        def heads(st):
            m, a = st.m, st.aux
            qp = m[:, 0:1024].rearrange("p (j h n) -> p j h n", j=2, h=16)
            kp = m[:, 1024:2048].rearrange("p (j h n) -> p j h n", j=2, h=16)
            qT = m[:, 2048:3072].rearrange("p (c n) -> p c n", c=4)
            kT = m[:, 3072:4096].rearrange("p (c n) -> p c n", c=4)
            pt = m[:, 4096:5120]
            oT = m[:, 5120:5632].rearrange("p (c n) -> p c n", c=2)
            va = a[:, 0:544].rearrange("p (k h n) -> p k h n", k=2, h=16)
            o = a[:, 544:1056].rearrange("p (j n) -> p j n", j=2)
            t1 = a[:, 1056:2080].rearrange("p (j h n) -> p j h n", j=2, h=32)
            t2 = a[:, 2080:3084][:, 0:512].rearrange("p (h n) -> p h n", h=32)
            return qp, kp, qT, kT, pt, oT, va, o, t1, t2

        def turn(st, srcs, dsts):
            for i, (s, d) in enumerate(zip(srcs, dsts)):
                pe.wait(st.bf[2 * i], st.bf[2 * i + 1])
                for c in range(4):
                    for j in range(2):
                        m = tp(pair(st, i)[:, c * 256 + j * 128:c * 256 + (j + 1) * 128],
                               s[:, j, 4 * c:4 * c + 4, :].rearrange("p h n -> p (h n)"))
                act.wait(m)
                t = copy(d.rearrange("p c n -> p (c n)"), pair(st, i))
                st.bf[2 * i] = st.bf[2 * i + 1] = t
            return m, t

        def maxima(st, qT, kT, qp, K, turned):
            for j in range(2):
                for g in range(2):
                    pe.wait(*st.bf)
                    for hh in range(4):
                        r = 32 * hh
                        for c in range(2):
                            m = mm(bank(st, hh)[:, c * 256:(c + 1) * 256], qT[r:r + K, 2 * g + c, j * 128:(j + 1) * 128],
                                   kT[r:r + K, 2 * g + c, :], True, True)
                    dve.wait(m, turned)
                    t = dve.do(lambda e, j=j, g=g: e.tensor_reduce(
                        qp[:, j, 8 * g:8 * g + 8, 16].rearrange("p (c h) -> p h c", h=4),
                        st.ps[:, :].rearrange("p (h c n) -> p h c n", h=4, c=2), AX.X, ALU.max, negate=True))
                    st.bf = [t] * 4
                    yield
            st.max_ok, st.max_pe = t, m

        def weigh(st, qT, kT, pt, va, K, scale, vok, prev):
            mo = prev
            pe.wait(st.bf[2], st.bf[3], vok)
            p4 = pt.rearrange("p (a k n) -> p a k n", a=2, k=2)
            for g in range(8):
                pe.wait(st.bf[0], st.bf[1])
                for a in range(2):
                    h = 2 * g + a
                    r = 32 * (h % 4)
                    for k in range(2):
                        m = mm(pair(st, 0)[:, (2 * a + k) * 256:(2 * a + k + 1) * 256], kT[r:r + K, h // 4, k * 128:(k + 1) * 128],
                               qT[r:r + K, h // 4, :], True, True)
                act.wait(m, mo)
                eok = func(pt, pair(st, 0), ACT.Exp, scale=scale)
                st.bf[0] = st.bf[1] = eok
                yield
                pe.wait(eok)
                for a in range(2):
                    h = 2 * g + a
                    for j in range(2):
                        for k in range(2):
                            mo = mm(bank(st, 2 + j)[:, 17 * h:17 * h + 17], p4[:, a, k, j * 128:(j + 1) * 128], va[:, k, h, :], k == 0, k == 1)
            st.pv_ok, st.pv_exp, st.s_pe = mo, eok, m

        def normalise(st, o):
            rc = st.sm[:, 64:96].rearrange("p (j n) -> p j n", j=2)
            dve.wait(st.pv_ok)
            ob = pair(st, 1).rearrange("p (j n) -> p j n", j=2)[:, :, 0:272].rearrange("p j (h n) -> p j h n", h=16)
            t = dve.do(lambda e: e.reciprocal(rc, ob[:, :, :, 16]))
            dve.wait(t)
            for j in range(2):
                t = tt(o[:, j, :].rearrange("p (h n) -> p h n", h=16), ob[:, j, :, 0:16],
                       rc[:, j, :].unsqueeze(2).to_broadcast([P, 16, 16]), ALU.mult)
            st.bf[2] = st.bf[3] = t
            return t

        def project(st, b, o, oT, w, ook, xbias, final=False):
            pe.wait(ook, st.bf[0], st.bf[1])
            for c in range(2):
                for j in range(2):
                    m = tp(bank(st, 0)[:, c * 256 + j * 128:c * 256 + (j + 1) * 128], o[:, j, c * 128:(c + 1) * 128])
            act.wait(m)
            t = copy(oT.rearrange("p c n -> p (c n)"), bank(st, 0))
            st.bf[0] = t
            pe.wait(t)
            for j in range(2):
                for c in range(2):
                    m = mm(bank(st, 1)[:, j * 256:(j + 1) * 256], oT[:, c, j * 128:(j + 1) * 128], w[:, c, :], c == 0, c == 1)
            ended(st, pe=m, act=t)
            layernorm(st, b, bank(st, 1).rearrange("p (j n) -> p j n", j=2), 1, (m, xbias), final)

        def qkv_mm(st, w):
            pe.wait(st.xT_ok)
            for j in range(2):
                pe.wait(st.bf[2 + j])
                for k in range(2):
                    m = mm(bank(st, 2 + j), st.xT[:, k, j * 128:(j + 1) * 128], w[:, k, 0:512], k == 0, k == 1)
            pe.wait(st.bf[1])
            for j in range(2):
                for k in range(2):
                    m = mm(bank(st, 1)[:, j * 256:(j + 1) * 256], st.xT[:, k, j * 128:(j + 1) * 128], w[:, k, 512:768], k == 0, k == 1)
            st.xT_rd = m
            return m

        def l1_attn(st, b):
            fence(st)
            qp, kp, qT, kT, pt, oT, va, o, t1, t2 = heads(st)
            pool.wait(st.last["pool"])
            mset(pool, st.m[:, 0:2048], 0.0)
            z = mset(pool, va[:, :, :, 16:17], 1.0)
            pool.wait(z)
            z = mset(pool, kp[:, :, :, 16:17], 1.0)
            to_xT(st, b)
            xbias = add_bias(st, b, part(regP, P1, "bao"))
            m = qkv_mm(st, part(regP, P1, "wqkv", 2))
            act.wait(m)
            vok = copy(va[:, :, :, 0:16], bank(st, 1).rearrange("p (k h n) -> p k h n", k=2, h=16))
            st.bf[1] = vok
            yield
            dve.wait(m, z)
            tl = None
            for j in range(2):
                qk = bank(st, 2 + j).rearrange("p (h n) -> p h n", h=32)
                a = tt(t1[:, j, :, :], qk, ropec[:, j, :].unsqueeze(1).to_broadcast([P, 32, 16]), ALU.mult)
                dve.wait(tl)
                tt(t2[:, :, 0:8], qk[:, :, 8:16], ropes[:, j, 0:8].unsqueeze(1).to_broadcast([P, 32, 8]), ALU.mult)
                a = tt(t2[:, :, 8:16], qk[:, :, 0:8], ropes[:, j, 8:16].unsqueeze(1).to_broadcast([P, 32, 8]), ALU.mult)
                st.bf[2 + j] = a
                dve.wait(a)
                tt(qp[:, j, :, 0:16], t1[:, j, 0:16, :], t2[:, 0:16, :], ALU.add)
                tl = tt(kp[:, j, :, 0:16], t1[:, j, 16:32, :], t2[:, 16:32, :], ALU.add)
            pe.wait(tl, z)
            m, t = turn(st, (qp, kp), (qT, kT))
            yield
            pe.wait(t)
            yield from maxima(st, qT, kT, qp, 16, m)
            pe.wait(st.max_ok)
            act.wait(st.max_pe)
            m, t = turn(st, (qp,), (qT,))
            pe.wait(t)
            yield
            yield from weigh(st, qT, kT, pt, va, 17, 0.25, vok, None)
            ook = normalise(st, o)
            yield
            project(st, b, o, oT, part(regP, P1, "wao", 2), ook, xbias)
            yield

        sim = small[:, 0:16]
        gg = small[:, 16:32]
        pos = small[:, 32:48]
        qf = small[:, 48:80].rearrange("p (t n) -> p t n", n=2)
        kf = small[:, 80:112].rearrange("p (t n) -> p t n", n=2)
        qxf = small[:, 112:144].rearrange("p (t n) -> p t n", n=2)
        ext = small[:, 144:146]
        ext2 = small[:, 146:148]
        den = small[:, 148:149]
        tmp16 = small[:, 149:165]
        tmpb = small[:, 165:181]
        gsq = small[:, 192:448]
        g_ok = []
        sim_ok = []

        def guide():
            g = part(regP, P1, "g")
            t = tt(gsq, g, g, ALU.mult)
            dve.wait(t)
            g_ok.append(dve.do(lambda e: e.tensor_reduce(gg, gsq.rearrange("p (h n) -> p h n", h=16), AX.X, ALU.add)))

        def ffn_qkv(st, b):
            fence(st)
            g = part(regP, P1, "g")
            sq = st.m[:, 0:512].rearrange("p (j n) -> p j n", j=2)
            qg = st.m[:, 512:1024].rearrange("p (j n) -> p j n", j=2)
            qq = st.sm[:, 32:64].rearrange("p (j n) -> p j n", j=2)
            dq = st.sm[:, 64:96].rearrange("p (j n) -> p j n", j=2)
            to_xT(st, b)
            add = add_bias(st, b, part(regP, P1, "fb"))
            x_ok[2 * b] = x_ok[2 * b + 1] = add
            m = qkv_mm(st, part(regP, P1, "fqkv", 2))
            act.wait(m)
            for j in range(2):
                c1 = copy(qkvall[:, 2 * b + j, 0:512], bank(st, 2 + j))
                st.bf[2 + j] = c1
            c2 = copy(qkvall[:, 2 * b:2 * b + 2, 512:768], bank(st, 1).rearrange("p (j n) -> p j n", j=2))
            st.bf[1] = c2
            yield
            dve.wait(c1)
            qv = qkvall[:, 2 * b:2 * b + 2, 0:256]
            tt(sq, qv, qv, ALU.mult)
            t = tt(qg, qv, g.unsqueeze(1).to_broadcast([P, 2, 256]), ALU.mult)
            dve.wait(t)
            dve.do(lambda e: e.tensor_reduce(qq, sq.rearrange("p j (h n) -> p j h n", h=16), AX.X, ALU.add))
            t = dve.do(lambda e: e.tensor_reduce(dq, qg.rearrange("p j (h n) -> p j h n", h=16), AX.X, ALU.add))
            dve.wait(t, g_ok[0])
            t = tt(qq, qq, gg.unsqueeze(1).to_broadcast([P, 2, 16]), ALU.mult)
            pool.wait(t)
            p = tt(qq, qq, mhalf.rearrange("p (j n) -> p j n", j=2), ALU.pow, pool)
            dve.wait(p)
            t = tt(dq, dq, qq, ALU.mult)
            dve.wait(t)
            t = dve.do(lambda e: e.tensor_reduce(sim[:, 2 * b:2 * b + 2], dq, AX.X, ALU.add))
            sim_ok.append(t)
            ended(st, pe=m, act=c2, dve=t, pool=p)
            yield

        def choose():
            dve.wait(*sim_ok)
            t = ts(sim, sim, 1.0 / 16.0, None, ALU.mult)
            dve.wait(t)
            t = tt(tmp16, sim, vm, ALU.mult)
            dve.wait(t)
            t = stt(tmpb, vmi, -BIG, tmp16, ALU.mult, ALU.add)
            t2 = stt(tmp16, vmi, BIG, tmp16, ALU.mult, ALU.add)
            dve.wait(t, t2)
            dve.do(lambda e: e.tensor_reduce(ext[:, 0:1], tmpb, AX.X, ALU.max))
            t = dve.do(lambda e: e.tensor_reduce(ext[:, 1:2], tmp16, AX.X, ALU.min, negate=True))
            pool.wait(t)
            t = pool.do(lambda e: e.partition_all_reduce(ext2, ext, P, RMAX))
            dve.wait(t)
            t = tt(den, ext2[:, 0:1], ext2[:, 1:2], ALU.add)
            t2 = ts(tmp16, sim, ext2[:, 1:2], None, ALU.add)
            dve.wait(t, t2)
            t = ts(den, den, 0.9, None, ALU.mult)
            dve.wait(t)
            t = ts(pos, tmp16, den, None, ALU.is_gt)
            dve.wait(t)
            t = tt(pos, pos, vm, ALU.mult)
            dve.wait(t)
            tt(kf[:, :, 0], vm, pos, ALU.subtract)
            dve.do(lambda e: e.tensor_copy(kf[:, :, 1], pos))
            t = tt(tmpb, pos, vmi, ALU.add)
            dve.wait(t)
            ts(qf[:, :, 0], tmpb, -BIG, None, ALU.mult)
            t = ts(qf[:, :, 1], tmpb, BIG, -BIG, ALU.mult, ALU.add)
            dve.wait(t)
            dve.do(lambda e: e.tensor_copy(qxf[:, :, 0], qf[:, :, 1]))
            t = dve.do(lambda e: e.tensor_copy(qxf[:, :, 1], qf[:, :, 0]))
            sim_ok.append(t)

        def ffn_attn(st, b):
            fence(st)
            qp, kp, qT, kT, pt, oT, va, o, t1, t2 = heads(st)
            a = st.aux
            qx = a[0:32, 1056:1568].rearrange("p (h n) -> p h n", h=16)
            qxT = a[:, 1568:1696].rearrange("p (c n) -> p c n", c=4)
            ptx = a[:, 1696:1952].rearrange("p (h k n) -> p h k n", h=16, k=2)
            ox = a[0:8, 1952:2208].rearrange("p (h n) -> p h n", h=16)
            rx = st.sm[0:8, 96:112]
            pool.wait(st.last["pool"])
            mset(pool, st.m[:, 0:2048], 0.0)
            z = mset(pool, va[:, :, :, 16:17], 1.0)
            pool.wait(z)
            z = mset(pool, kp[:, :, :, 16:17], 1.0)
            tb = slice(2 * b, 2 * b + 2)
            act.wait(z)
            for j in range(2):
                copy(qp[:, j, :, 0:16], qkvall[:, 2 * b + j, 0:256].rearrange("p (h n) -> p h n", h=16))
                copy(kp[:, j, :, 0:16], qkvall[:, 2 * b + j, 256:512].rearrange("p (h n) -> p h n", h=16))
                vok = copy(va[:, j, :, 0:16], qkvall[:, 2 * b + j, 512:768].rearrange("p (h n) -> p h n", h=16))
            dve.wait(z, sim_ok[-1])
            for j in range(2):
                dve.do(lambda e, j=j: e.tensor_copy(qp[:, j, :, 17:19], qf[:, 2 * b + j, :].unsqueeze(1).to_broadcast([P, 16, 2])))
                t = dve.do(lambda e, j=j: e.tensor_copy(kp[:, j, :, 17:19], kf[:, 2 * b + j, :].unsqueeze(1).to_broadcast([P, 16, 2])))
            dve.wait(t, vok)
            t = dve.do(lambda e: e.tensor_copy(qx, qp[0:32, 0, :, :]))
            dve.wait(t)
            xq = dve.do(lambda e: e.tensor_copy(qx[:, :, 17:19], qxf[0:32, 2 * b, :].unsqueeze(1).to_broadcast([32, 16, 2])))
            yield
            pe.wait(xq, vok, z)
            m, t = turn(st, (qp, kp), (qT, kT))

            def turn_x():
                pe.wait(st.bf[0])
                for c in range(4):
                    m = tp(bank(st, 0)[:, 32 * c:32 * c + 32], qx[:, 4 * c:4 * c + 4, :].rearrange("p h n -> p (h n)"), 32)
                act.wait(m)
                t = copy(qxT.rearrange("p c n -> p (c n)"), bank(st, 0)[:, 0:128])
                st.bf[0] = t
                return m, t

            mx, t = turn_x()
            yield
            pe.wait(t)
            yield from maxima(st, qT, kT, qp, 19, mx)
            for g in range(2):
                pe.wait(*st.bf)
                for hh in range(4):
                    r = 32 * hh
                    for c in range(2):
                        m = mm(bank(st, hh)[0:8, c * 256:(c + 1) * 256], qxT[r:r + 19, 2 * g + c, 0:8], kT[r:r + 19, 2 * g + c, :], True, True)
                dve.wait(m)
                t = dve.do(lambda e, g=g: e.tensor_reduce(
                    qx[0:8, 8 * g:8 * g + 8, 16].rearrange("p (c h) -> p h c", h=4),
                    st.ps[0:8, :].rearrange("p (h c n) -> p h c n", h=4, c=2), AX.X, ALU.max, negate=True))
                st.bf = [t] * 4
            yield
            pe.wait(t, st.max_ok)
            act.wait(m)
            turn(st, (qp,), (qT,))
            m, t = turn_x()
            pe.wait(t)
            yield
            yield from weigh(st, qT, kT, pt, va, 19, 0.25, vok, None)
            ook = normalise(st, o)
            yield
            pe.wait(*st.bf)
            for h in range(16):
                r = 32 * (h % 4)
                for k in range(2):
                    at = 16 * (h // 4) + 8 * k
                    m = mm(bank(st, h % 4)[:, at:at + 8], kT[r:r + 19, h // 4, k * 128:(k + 1) * 128],
                           qxT[r:r + 19, h // 4, 0:8], True, True)
            act.wait(m)
            t = func(ptx.rearrange("p (r c) k n -> p r (c k n)", r=4), st.ps[:, :].rearrange("p (r n) -> p r n", r=4)[:, :, 0:64],
                     ACT.Exp, scale=0.25)
            st.bf = [t] * 4
            pe.wait(t)
            for h in range(16):
                for k in range(2):
                    m = mm(bank(st, 1)[0:8, 17 * h:17 * h + 17], ptx[:, 4 * (h % 4) + h // 4, k, :], va[:, k, h, :], k == 0, k == 1)
            dve.wait(m)
            ob = bank(st, 1)[0:8, 0:272].rearrange("p (h n) -> p h n", h=16)
            t = dve.do(lambda e: e.reciprocal(rx, ob[:, :, 16]))
            dve.wait(t)
            t = tt(ox, ob[:, :, 0:16], rx.unsqueeze(2).to_broadcast([8, 16, 16]), ALU.mult)
            st.bf[1] = t
            dve.wait(t, ook)
            ov = o[0:REG, 0, :].rearrange("p (h n) -> p h n", h=16)
            t = tt(ov, ov, ox[0:REG, :, :], ALU.add)
            dve.wait(t)
            ook = ts(o[0:REG, 0, :], o[0:REG, 0, :], 0.5, None, ALU.mult)
            yield
            project(st, b, o, oT, part(regP, P1, "fproj", 2), ook, x_ok[2 * b], True)
            yield

        def together(work):
            gens = [(w() if callable(w) else w) for w in work]
            while gens:
                for g in list(gens):
                    try:
                        next(g)
                    except StopIteration:
                        gens.remove(g)

        def each(st, *fs):
            for b in st.batches:
                for f in fs:
                    yield from f(st, b)

        for lane in (pe, act, dve, pool):
            for s in (d_cst, d_x, d_ctx, d_w0):
                loaded(lane, s)
        pt0 = [st.pt.rearrange("p (h n) -> p h n", h=4) for st in streams]
        together([each(st, l0_attn, lambda st, b: xattn(st, b, P0, None, pt0[st.i], st.pt)) for st in streams])
        phase1 = [t for st in streams for t in st.last.values()]
        for lane in (pe, act, dve, pool):
            loaded(lane, d_wq)
            loaded(lane, d_s3)
        together([each(st, moe) for st in streams])
        phase2 = [t for st in streams for t in st.last.values()]
        for lane in (pe, act, dve, pool):
            loaded(lane, d_w1)
            lane.wait(*phase2)
        guide()
        pt1 = [st.aux[:, 0:1024] for st in streams]
        together([each(st, l1_attn, lambda st, b: xattn(st, b, P1, None, pt1[st.i].rearrange("p (h n) -> p h n", h=4), pt1[st.i]),
                       ffn_qkv) for st in streams])
        choose()
        together([each(st, ffn_attn) for st in streams])

        sync = Lane("sync", d_out)

        for lane in (pe, act, dve, pool, sync):
            for t in phase1:
                if t is not None and lane is sync:
                    t.used = True
        for _, t in outs:
            t.used = True
        for lane in (pe, act, dve, pool):
            lane.count()

        block = es.enter_context(nc.Block())

        @block.sync
        def _(eng):
            eng.dma_start(cst[:, :], const_in).then_inc(d_cst, 16)
            eng.dma_start(xres[:, :], x_in).then_inc(d_x, 16)
            eng.dma_start(regP[:, 0:N0], w0_in).then_inc(d_w0, 16)
            eng.dma_start(ctxT[:, :], ctx_in).then_inc(d_ctx, 16)
            a = PQ["s3"][0]
            eng.dma_start(regQ[:, 0:a], wq_in[:, 0:a]).then_inc(d_wq, 16)
            for t in phase1:
                if t is not None:
                    eng.wait_ge(t.lane.sem, t.value)
            eng.dma_start(regQ[:, a:NQ], wq_in[:, a:NQ]).then_inc(d_s3, 16)
            eng.dma_start(regP[:, 0:N1], w1_in).then_inc(d_w1, 16)
            for tile, t in outs:
                eng.wait_ge(t.lane.sem, t.value)
                eng.dma_start(out[tile * P:(tile + 1) * P, :], x[:, tile, :]).then_inc(d_out, 16)
            eng.wait_ge(d_out, 16 * len(outs))

        @block.tensor
        def _(eng):
            pe.emit(eng)

        @block.scalar
        def _(eng):
            act.emit(eng)

        @block.vector
        def _(eng):
            dve.emit(eng)

        @block.gpsimd
        def _(eng):
            pool.emit(eng)


def consts():
    c = np.zeros((P, NC_), np.float32)

    def put(name, v):
        a, n = PC[name]
        c[:, a:a + n] = v

    put("ident", np.eye(P, dtype=np.float32))
    put("ones", 1.0)
    inv = (1.0 / np.float32(10000.0) ** (np.arange(0, 16, 2, dtype=np.float32) / np.float32(16))).astype(np.float32)
    ang = np.arange(S, dtype=np.float32)[:, None] * inv[None, :]
    cos, sin = np.cos(ang).astype(np.float32), np.sin(ang).astype(np.float32)
    put("ropec", np.concatenate([cos, cos], 1).reshape(2, P, 16).transpose(1, 0, 2).reshape(P, 32))
    put("ropes", np.concatenate([-sin, sin], 1).reshape(2, P, 16).transpose(1, 0, 2).reshape(P, 32))
    put("tri", np.tril(np.ones((8, 8), np.float32), -1).reshape(1, 64))
    valid = np.ones((P, 16), np.float32)
    valid[0:REG, 0::2] = 0.0
    put("vm", valid)
    put("vmi", 1.0 - valid)
    put("half", -0.5)
    return c


def kernel(**inputs):
    import concourse.bacc as _bacc
    from concourse.bass_utils import run_bass_kernel_spmd as _run

    a = {k: np.asarray(v) for k, v in inputs.items()}

    def rows(w):
        k, n = w.shape
        return w.reshape(k // P, P, n).transpose(1, 0, 2).reshape(P, -1)

    def all_rows(v):
        return np.broadcast_to(v.reshape(1, -1), (P, v.size))

    def kv(wk, wv):
        return np.concatenate([wk[0:P], wv[0:P], np.concatenate([wk[P:CD], wv[P:CD]], 0)], 1)

    conv = np.concatenate([a["L0_attn_conv_w"], a["L0_attn_conv_b"][:, None], a["L0_attn_D"][:, None]], 1)
    w0 = np.concatenate([
        rows(a["L0_attn_W_in"].T), rows(conv), rows(a["L0_attn_W_xproj"].T), rows(a["L0_attn_W_out"].T),
        rows(a["L0_xattn_Wq"]), kv(a["L0_xattn_Wk"], a["L0_xattn_Wv"]), rows(a["L0_xattn_Wo"]), all_rows(a["L0_xattn_bo"])], 1)
    s1 = a["L0_ffn_shared_w1"].T.reshape(2, P, 4, 256)
    s2 = a["L0_ffn_shared_w2"].T.reshape(2, P, 4, 256)
    s12 = np.concatenate([s1, s2], 3).transpose(1, 2, 0, 3).reshape(P, -1)
    w12 = a["L0_ffn_w12"].transpose(0, 2, 1).reshape(NE, 2, P, 512).transpose(2, 0, 1, 3).reshape(P, -1)
    w3 = a["L0_ffn_w3"].transpose(0, 2, 1).reshape(NE, 2, P, 256).transpose(2, 0, 1, 3).reshape(P, -1)
    wq = np.concatenate([w12, w3, s12, rows(a["L0_ffn_router_w"].T), all_rows(a["L0_ffn_expert_bias"]),
                         rows(a["L0_ffn_shared_w3"].T)], 1)
    w1 = np.concatenate([
        rows(a["L1_attn_w_qkv"].T), rows(a["L1_attn_w_out"].T), all_rows(a["L1_attn_b_out"]),
        rows(a["L1_xattn_Wq"]), kv(a["L1_xattn_Wk"], a["L1_xattn_Wv"]), rows(a["L1_xattn_Wo"]), all_rows(a["L1_xattn_bo"]),
        rows(a["L1_ffn_W_qkv"]), rows(a["L1_ffn_W_proj"]), all_rows(a["L1_ffn_b_proj"]), all_rows(a["L1_ffn_g_info"][0, 0])], 1)
    cT = a["ctx_768"].reshape(B * CK, CD).T
    ctx = np.concatenate([cT[0:P], np.concatenate([cT[P:CD], cT[P:CD]], 0)], 1)
    x = a["x"].reshape(16, P, D).transpose(1, 0, 2).reshape(P, -1)
    arrays = {"x_dram": x, "ctx_dram": ctx, "w0_dram": w0, "wq_dram": wq, "w1_dram": w1, "const_dram": consts()}
    arrays = {k: np.ascontiguousarray(v) for k, v in arrays.items()}

    nc = _bacc.Bacc("TRN2", target_bir_lowering=False, num_devices=1)
    args = [nc.dram_tensor(k, v.shape, F32, kind="ExternalInput").ap() for k, v in arrays.items()]
    args.append(nc.dram_tensor("out_dram", (B * S, D), F32, kind="ExternalOutput").ap())
    program(nc, *args)
    r = _run(nc, [arrays], core_ids=[0])
    return r.results[0]["out_dram"].reshape(B, S, D)
```

```python
from contextlib import ExitStack

import numpy as np

import concourse.bass as bass
from concourse import mybir

F32 = mybir.dt.float32
F32R = mybir.dt.float32r
ALU = mybir.AluOpType
ACT = mybir.ActivationFunctionType
AX = mybir.AxisListType
RMAX = bass.bass_isa.ReduceOp.max

P = 128
B, S, D, CK, CD = 8, 256, 256, 77, 192
H = 16
NE = 8
REG = 5
BIG = float(2.0 ** 100)
EPS = 1e-5

LAY0 = [("win", 2048), ("wxp", 2176), ("wq", 2048), ("wo", 2048), ("wout", 1024)]
LAY0F = [("wkv", 3072), ("conv", 24), ("bo", 256)]
LAY1 = [("wqkv", 1536), ("wao", 512), ("wq", 2048), ("wo", 2048), ("fqkv", 1536), ("fproj", 512)]
LAY1F = [("wkv", 3072), ("bao", 256), ("bo", 256), ("fb", 256), ("g", 256)]
LAYR = [("rw", 16), ("rb", 8)]
LAYC = [("ident", 128), ("ones", 128), ("ropec", 32), ("ropes", 32), ("tri", 64), ("vm", 16), ("vmi", 16), ("half", 32)]
NU = NE + 4
UW = 1536
CP = 78


def places(lay):
    at, out = 0, {}
    for name, n in lay:
        out[name] = (at, n)
        at += n
    return out, at


P0, N0 = places(LAY0)
P0F, N0F = places(LAY0F)
P1, N1 = places(LAY1)
P1F, N1F = places(LAY1F)
PR, NR = places(LAYR)
PC, NC_ = places(LAYC)


class Token:

    def __init__(self, lane, index):
        self.lane, self.index, self.used = lane, index, False


class Lane:

    def __init__(self, name, sem):
        self.name, self.sem, self.items = name, sem, []

    def wait(self, *tokens):
        for t in tokens:
            if t is not None:
                t.used = True
                self.items.append(("wait", t))

    def do(self, call):
        t = Token(self, len(self.items))
        self.items.append(("do", call, t))
        return t

    def count(self):
        n = 0
        for it in self.items:
            if it[0] == "do" and it[2].used:
                n += 1
                it[2].value = n

    def emit(self, eng):
        seen = {}
        for it in self.items:
            if it[0] == "wait":
                t = it[1]
                if seen.get(t.lane.name, 0) < t.value:
                    seen[t.lane.name] = t.value
                    eng.wait_ge(t.lane.sem, t.value)
            else:
                ins = it[1](eng)
                if it[2].used:
                    ins.then_inc(self.sem, 1)


class Stream:
    pass


def program(nc, x_in, ctx_in, w0_in, w0f_in, wu_in, wr_in, w1_in, w1f_in, const_in, out, keep):
    es = ExitStack()
    with es:
        def sb(name, n, dt=F32, scope=es):
            return scope.enter_context(nc.sbuf_tensor(name, [P, n], dt))

        def sem(name):
            return es.enter_context(nc.semaphore(name))

        xres = sb("xres", 16 * D)
        ctxT = sb("ctxT", 2 * B * CP)
        cst = sb("cst", NC_)
        identr_t = sb("identr", P, F32R)
        small = sb("small", 512)
        x = xres[:, :].rearrange("p (t d) -> p t d", d=D)
        ctx = ctxT[:, :].rearrange("p (k n) -> p k n", k=2)

        def part(t, pl, name, c=None):
            a, n = pl[name]
            v = t[:, a:a + n]
            return v if c is None else v.rearrange("p (c n) -> p c n", c=c)

        def pair_of(t, pl, name, c):
            return part(t[0], pl, name, c), part(t[1], pl, name, c)

        ident = part(cst, PC, "ident")
        identr = identr_t[:, :]
        ones = part(cst, PC, "ones")
        ropec = part(cst, PC, "ropec", 2)
        ropes = part(cst, PC, "ropes", 2)
        tri = part(cst, PC, "tri", 8)
        vm = part(cst, PC, "vm")
        vmi = part(cst, PC, "vmi")
        mhalf = part(cst, PC, "half")

        pe, act, dve, pool, sp = (Lane(n, sem(f"s_{n}")) for n in ("pe", "act", "dve", "pool", "sp"))
        d_cst, d_x, d_ctx, d_w0f, d_wr, d_w1f, d_w1, d_keep, d_out = (
            sem(f"d_{n}") for n in ("cst", "x", "ctx", "w0f", "wr", "w1f", "w1", "keep", "out"))
        d_w0 = [sem(f"d_w0{i}") for i in range(4)]
        d_u = [sem(f"d_u{i}") for i in range(2)]
        d_raw = [sem(f"d_raw{i}") for i in range(2)]

        def loaded(lane, s, v=16):
            lane.items.append(("do", lambda e: e.wait_ge(s, v), Token(lane, 0)))

        def dma(o, i, s):
            sp.do(lambda e: e.dma_start(o, i).then_inc(s, 16))

        streams = []
        for i in range(2):
            st = Stream()
            st.i = i
            st.sm = sb(f"sm{i}", 448)
            st.ps = es.enter_context(nc.psum_tensor(f"ps{i}", [P, 2048], F32))
            st.bf = [None] * 4
            st.xT_rd = None
            st.last = {"pe": None, "act": None, "dve": None, "pool": None}
            st.batches = [b for b in range(B) if b % 2 == i]
            streams.append(st)

        x_ok = [None] * 16

        def work(scope, name, nf, nr):
            for st in streams:
                st.m = sb(f"m{name}{st.i}", nf, F32, scope)
                st.r = sb(f"r{name}{st.i}", nr, F32R, scope)

        def over():
            return [t for st in streams for t in st.last.values()]

        def bank(st, i, n=512):
            return st.ps[:, 512 * i:512 * i + n]

        def pair(st, i):
            return st.ps[:, 1024 * i:1024 * (i + 1)]

        def mm(o, l, r, start, stop):
            return pe.do(lambda e: e.matmul(o, l, r, start=start, stop=stop))

        def tp(o, i, n=128):
            return pe.do(lambda e: e.transpose(o, i, ident[0:n, 0:n]))

        def copy(o, i):
            return act.do(lambda e: e.activation(o, i, ACT.Copy))

        def func(o, i, f, scale=1.0, bias=0.0):
            return act.do(lambda e: e.activation(o, i, f, scale=scale, bias=bias))

        def tt(o, a, b_, op, lane=None):
            return (lane or dve).do(lambda e: e.tensor_tensor(o, a, b_, op))

        def ts(o, a, s1, s2, op0, op1=None, lane=None):
            if op1 is None:
                return (lane or dve).do(lambda e: e.tensor_scalar(o, a, s1, None, op0))
            return (lane or dve).do(lambda e: e.tensor_scalar(o, a, s1, s2, op0, op1))

        def stt(o, a, s, b_, op0, op1):
            return dve.do(lambda e: e.scalar_tensor_tensor(out=o, in0=a, scalar=s, in1=b_, op0=op0, op1=op1))

        A = slice(None)

        def mset(lane, o, v):
            return lane.do(lambda e: e.memset(o, v))

        def split(ps, hi, lo, made, rd=None):
            act.wait(made, rd)
            h = copy(hi, ps)
            dve.wait(h, made)
            return tt(lo, ps, hi.bitcast(F32), ALU.subtract)

        def mm3(o, l, r, start, stop):
            mm(o, l[0], r[0], start, False)
            mm(o, l[0], r[1], False, False)
            return mm(o, l[1], r[0], False, stop)

        def cols(t, *idx):
            return tuple(v[idx] for v in t)

        def fence(st):
            for lane in (pe, act, dve, pool):
                lane.wait(*[t for n, t in st.last.items() if n != lane.name])

        def ended(st, **last):
            st.last.update(last)

        def to_xT(st, b, hi, lo, rd):
            pe.wait(x_ok[2 * b], x_ok[2 * b + 1], st.bf[0])
            bk = bank(st, 0)
            for c in range(2):
                for j in range(2):
                    m = tp(bk[:, c * 256 + j * 128:c * 256 + (j + 1) * 128], x[:, 2 * b + j, c * 128:(c + 1) * 128])
            st.xT_src = m
            st.xT_ok = split(bk.rearrange("p (k n) -> p k n", k=2), hi, lo, m, rd)
            st.bf[0] = st.xT_ok

        def own_xT(st, b):
            st.xT = tuple(st.r[:, 512 * i:512 * (i + 1)].rearrange("p (k n) -> p k n", k=2) for i in range(2))
            to_xT(st, b, *st.xT, None)

        def add_bias(st, b, bias):
            pool.wait(st.xT_src, x_ok[2 * b], x_ok[2 * b + 1])
            for j in range(2):
                t = tt(x[:, 2 * b + j, :], x[:, 2 * b + j, :], bias, ALU.add, pool)
            return t

        def layernorm(st, b, ps=None, bk=None, after=(), final=False):
            xb = x[:, 2 * b:2 * b + 2, :]
            dve.wait(x_ok[2 * b], x_ok[2 * b + 1], *after)
            if ps is not None:
                r = tt(xb, ps, xb, ALU.add)
                st.bf[bk] = r
                dve.wait(r)
            s6 = st.sm[:, 0:12].rearrange("p (j n) -> p j n", j=2)
            mv = st.sm[:, 12:16].rearrange("p (j n) -> p j n", j=2)
            rs = st.sm[:, 16:18]
            t = [dve.do(lambda e, j=j: e.bn_stats(s6[:, j, :], xb[:, j, :])) for j in range(2)]
            for j in range(2):
                dve.wait(t[j])
                g = dve.do(lambda e, j=j: e.bn_aggr(mv[:, j, :], s6[:, j, :]))
            pool.wait(g)
            a = ts(rs, mv[:, :, 1], EPS, None, ALU.add, None, pool)
            pool.wait(a)
            q = tt(rs, rs, mhalf[:, 0:2], ALU.pow, pool)
            dve.wait(q, g)
            for j in range(2):
                n = ts(xb[:, j, :], xb[:, j, :], mv[:, j, 0:1], rs[:, j:j + 1], ALU.subtract, ALU.mult)
                x_ok[2 * b + j] = n
                if final:
                    outs.append((2 * b + j, n))
            ended(st, dve=n, pool=q)

        outs = []

        def l0_attn(st, b):
            fence(st)
            xb = st.m[:, 0:1036].rearrange("p (c n) -> p c n", c=4)
            xcf = st.m[:, 1036:2060]
            xc = xcf.rearrange("p (c n) -> p c n", c=4)
            szf = st.m[:, 2060:3084]
            tAf = st.m[:, 3084:4108]
            tA = tAf.rearrange("p (c n) -> p c n", c=4)
            Bc = st.m[:, 4108:4364]
            xr = tuple(st.r[:, 1024 * i:1024 * (i + 1)].rearrange("p (c n) -> p c n", c=4) for i in (1, 2))
            yr = tuple(st.r[:, 1024 * i:1024 * (i + 1)].rearrange("p (c n) -> p c n", c=4) for i in (3, 4))
            win = pair_of(w0, P0, "win", 2)
            cv = part(w0f, P0F, "conv", 4)
            wxp = pair_of(w0, P0, "wxp", 4)
            wout = pair_of(w0, P0, "wout", 4)
            z0 = mset(dve, xb[:, :, 0:3], 0.0)
            own_xT(st, b)
            yield
            pe.wait(st.xT_ok, st.bf[2], st.bf[3])
            for c in range(4):
                for k in range(2):
                    m = mm3(st.ps[:, 1024 + c * 256:1280 + c * 256], cols(win, A, k, slice(c * 128, (c + 1) * 128)), cols(st.xT, A, k), k == 0, k == 1)
            act.wait(m)
            cp = copy(xb[:, :, 3:259], pair(st, 1).rearrange("p (c n) -> p c n", c=4))
            st.bf[2] = st.bf[3] = cp
            pe.wait(st.bf[0], st.bf[1])
            for c in range(4):
                for k in range(2):
                    m = mm3(st.ps[:, c * 256:256 + c * 256], cols(win, A, k, slice(512 + c * 128, 640 + c * 128)), cols(st.xT, A, k), k == 0, k == 1)
            act.wait(m)
            zs = func(szf, pair(st, 0), ACT.Silu)
            st.bf[0] = st.bf[1] = zs
            yield
            dve.wait(cp, z0)
            last = [ts(xc[:, c, :], xb[:, c, 3:259], cv[:, c, 3:4], cv[:, c, 4:5], ALU.mult, ALU.add) for c in range(4)]
            for k in (2, 1, 0):
                for c in range(4):
                    dve.wait(last[c])
                    last[c] = stt(xc[:, c, :], xb[:, c, k:k + 256], cv[:, c, k:k + 1], xc[:, c, :], ALU.mult, ALU.add)
            act.wait(last[3])
            xs = func(xcf, xcf, ACT.Silu)
            act.wait(xs)
            t = copy(xr[0], xc)
            dve.wait(t, xs)
            xs = tt(xr[1], xc, xr[0].bitcast(F32), ALU.subtract)
            yield
            pe.wait(xs, st.bf[2], st.bf[3])
            for c in range(4):
                for k in range(4):
                    m = mm3(st.ps[:, 1024 + c * 256:1280 + c * 256], cols(wxp, A, k, slice(32 + c * 128, 160 + c * 128)), cols(xr, A, k), k == 0, k == 3)
            pe.wait(st.bf[0])
            for c in range(2):
                for k in range(4):
                    m2 = mm3(st.ps[:, c * 256:(c + 1) * 256], cols(wxp, A, k, slice(16 * c, 16 * c + 128)), cols(xr, A, k), k == 0, k == 3)
            act.wait(m2)
            t = copy(Bc[0:16, :], st.ps[0:16, 0:256])
            dve.wait(t, m)
            t = tt(Bc[0:16, :], Bc[0:16, :], st.ps[0:16, 256:512], ALU.mult)
            st.bf[0] = t
            pe.wait(t, st.bf[1])
            mb = mm(st.ps[:, 512:768], ones[0:16, :], Bc[0:16, :], True, True)
            yield
            t = ts(tAf, pair(st, 1), 30.0, None, ALU.min)
            act.wait(t)
            t = func(tAf, tAf, ACT.Exp)
            act.wait(t)
            t = func(tAf, tAf, ACT.Ln, bias=1.0)
            dve.wait(t)
            t = tt(tAf, tAf, pair(st, 1), ALU.max)
            st.bf[2] = st.bf[3] = t
            dve.wait(t, mb)
            t = tt(tA, tA, st.ps[:, 512:768].unsqueeze(1).to_broadcast([P, 4, 256]), ALU.mult)
            st.bf[1] = t
            dve.wait(t, xs, zs)
            for c in range(4):
                t = stt(tA[:, c, :], tA[:, c, :], cv[:, c, 5:6], xc[:, c, :], ALU.add, ALU.mult)
            dve.wait(t)
            t = tt(szf, szf, tAf, ALU.mult)
            act.wait(t)
            ya = copy(yr[0], szf.rearrange("p (c n) -> p c n", c=4))
            dve.wait(ya)
            t = tt(yr[1], szf.rearrange("p (c n) -> p c n", c=4), yr[0].bitcast(F32), ALU.subtract)
            yield
            pe.wait(t, st.bf[3])
            for j in range(2):
                for k in range(4):
                    m = mm3(bank(st, 3)[:, j * 256:(j + 1) * 256], cols(yr, A, k, slice(j * 128, (j + 1) * 128)), cols(wout, A, k), k == 0, k == 3)
            ended(st, pe=m, act=ya)
            layernorm(st, b, bank(st, 3).rearrange("p (j n) -> p j n", j=2), 3, (m,))
            yield

        def xattn(st, b, w, pl, wf, plf):
            fence(st)
            V = st.m[0:CK, 0:1040].rearrange("p (h n) -> p h n", h=16)
            ptf = st.m[:, 1040:2064]
            PT = ptf.rearrange("p (h n) -> p h n", h=4)
            O = st.m[:, 2064:4112].rearrange("p (j n) -> p j n", j=2)
            QT = tuple(st.r[:, 1024 + 2048 * i:3072 + 2048 * i].rearrange("p (c n) -> p c n", c=8) for i in range(2))
            KT = tuple(st.r[:, 5120 + 624 * i:5744 + 624 * i].rearrange("p (c n) -> p c n", c=8) for i in range(2))
            nmT = st.r[:, 0:256]
            nm = st.sm[:, 32:288].rearrange("p (j n) -> p j n", j=2)
            rc = st.sm[:, 288:296].rearrange("p (j n) -> p j n", j=2)
            wq = pair_of(w, pl, "wq", 2)
            wkv = part(wf, plf, "wkv", 3)
            wo = pair_of(w, pl, "wo", 8)
            kw = [(wkv[:, 0, :], 0, 128, 0), (wkv[0:64, 2, :], 0, 64, 1)]
            vw = [(wkv[:, 1, :], 0, 128, 0), (wkv[64:128, 2, :], 64, 64, 1)]
            pool.wait(st.last["pool"])
            mset(pool, st.sm[:, 32:288], 0.0)
            one = mset(pool, V[:, :, 64:65], 1.0)
            own_xT(st, b)
            xbias = add_bias(st, b, part(wf, plf, "bo"))
            pe.wait(st.bf[2], st.bf[3])
            for c in range(8):
                for k, (w_, p0, n, r) in enumerate(kw):
                    m = mm(st.ps[:, 1024 + 512 * (c // 4) + CP * (c % 4):1024 + 512 * (c // 4) + CP * (c % 4) + CP],
                           w_[:, c * 128:(c + 1) * 128], ctx[p0:p0 + n, r, b * CP:(b + 1) * CP], k == 0, k == 1)
            for i in range(2):
                kok = split(bank(st, 2 + i)[:, 0:4 * CP].rearrange("p (c n) -> p c n", c=4), *cols(KT, A, slice(4 * i, 4 * i + 4)), m)
            st.bf[2] = st.bf[3] = kok
            yield
            pe.wait(st.bf[0], st.bf[1])
            for i in range(2):
                for k, (w_, p0, n, r) in enumerate(vw):
                    m = mm(bank(st, i)[0:CK, :], ctx[p0:p0 + n, r, b * CP:b * CP + CK], w_[:, i * 512:(i + 1) * 512], k == 0, k == 1)
            act.wait(m)
            vok = copy(V[:, :, 0:64], st.ps[0:CK, 0:1024].rearrange("p (h n) -> p h n", h=16))
            st.bf[0] = st.bf[1] = vok
            yield
            pe.wait(st.xT_ok)
            for i in (1, 0):
                pe.wait(st.bf[2 * i], st.bf[2 * i + 1])
                for c in range(4):
                    cc = c + 4 * (1 - i)
                    for k in range(2):
                        m = mm3(pair(st, i)[:, c * 256:(c + 1) * 256], cols(wq, A, k, slice(cc * 128, (cc + 1) * 128)), cols(st.xT, A, k), k == 0, k == 1)
                qok = split(pair(st, i).rearrange("p (c n) -> p c n", c=4), *cols(QT, A, slice(4 - 4 * i, 8 - 4 * i)), m)
                st.bf[2 * i] = st.bf[2 * i + 1] = qok
            yield
            pe.wait(qok, kok)
            for j in range(2):
                for i in range(2):
                    pe.wait(st.bf[2 * i], st.bf[2 * i + 1])
                    for hh in range(8):
                        h = 8 * i + hh
                        r = 64 * (h % 2)
                        m = mm(bank(st, 2 * i + hh % 2)[:, CP * (hh // 2):CP * (hh // 2) + CP],
                               QT[0][r:r + 64, h // 2, j * 128:(j + 1) * 128], KT[0][r:r + 64, h // 2, :], True, True)
                    dve.wait(m, one)
                    src = pair(st, i).rearrange("p (a n) -> p a n", a=2)[:, :, 0:4 * CP].rearrange("p a (c n) -> p a c n", c=4)
                    dst = nm[:, j, 8 * i:8 * i + 8].rearrange("p (c a) -> p a c", a=2)
                    t = dve.do(lambda e, dst=dst, src=src: e.tensor_reduce(dst, src, AX.X, ALU.max, negate=True))
                    dve.wait(t)
                    up = dve.do(lambda e, i=i, j=j: e.tensor_copy(nm[:, j, 64 + 8 * i:72 + 8 * i], nm[:, j, 8 * i:8 * i + 8]))
                    st.bf[2 * i] = st.bf[2 * i + 1] = t
                yield
            pe.wait(up, t)
            for j in range(2):
                m = tp(st.ps[:, j * 128:(j + 1) * 128], nm[:, j, :])
            act.wait(m)
            nok = copy(nmT, st.ps[:, 0:256])
            st.bf[0] = nok
            pe.wait(nok)
            first = True
            for g in range(4):
                pe.wait(st.bf[0], st.bf[1])
                for hh in range(4):
                    h = 4 * g + hh
                    r = 64 * (h % 2)
                    at = (hh % 2) * 512 + (hh // 2) * 256
                    o = st.ps[0:CK, at:at + 256]
                    mm3(o, cols(KT, slice(r, r + 64), h // 2, slice(0, CK)), cols(QT, slice(r, r + 64), h // 2), True, False)
                    m = mm(o, identr[r:r + 64, r + h:r + h + 1].to_broadcast([64, CK]), nmT[r:r + 64, :], False, True)
                act.wait(m, None if first else mo)
                eok = func(ptf[0:CK, :], st.ps[0:CK, 0:1024], ACT.Exp, scale=0.125)
                st.bf[0] = st.bf[1] = eok
                yield
                pe.wait(eok, vok, one, st.bf[2], st.bf[3])
                for j in range(2):
                    for hh in range(4):
                        mo = mm(bank(st, 2 + j)[:, hh * 65:(hh + 1) * 65], PT[0:CK, 2 * (hh % 2) + hh // 2, j * 128:(j + 1) * 128],
                                V[:, 4 * g + hh, :], True, True)
                dve.wait(mo)
                ob = pair(st, 1).rearrange("p (j n) -> p j n", j=2)[:, :, 0:260].rearrange("p j (c n) -> p j c n", c=4)
                t = dve.do(lambda e, ob=ob: e.reciprocal(rc, ob[:, :, :, 64]))
                dve.wait(t)
                for j in range(2):
                    t = tt(O[:, j, 256 * g:256 * (g + 1)].rearrange("p (c n) -> p c n", c=4), ob[:, j, :, 0:64],
                           rc[:, j, :].unsqueeze(2).to_broadcast([P, 4, 64]), ALU.mult)
                st.bf[2] = st.bf[3] = t
                first = False
                yield
            pe.wait(t)
            for i in range(2):
                pe.wait(st.bf[2 * i], st.bf[2 * i + 1])
                for c in range(4):
                    for j in range(2):
                        m = tp(pair(st, i)[:, c * 256 + j * 128:c * 256 + (j + 1) * 128], O[:, j, (4 * i + c) * 128:(4 * i + c + 1) * 128])
                ook = split(pair(st, i).rearrange("p (c n) -> p c n", c=4), *cols(QT, A, slice(4 * i, 4 * i + 4)), m)
                st.bf[2 * i] = st.bf[2 * i + 1] = ook
            pe.wait(ook)
            for j in range(2):
                for c in range(8):
                    m = mm3(bank(st, 0)[:, j * 256:(j + 1) * 256], cols(QT, A, c, slice(j * 128, (j + 1) * 128)), cols(wo, A, c), c == 0, c == 7)
            ended(st, pe=m, act=eok)
            layernorm(st, b, bank(st, 0).rearrange("p (j n) -> p j n", j=2), 0, (m, xbias))
            yield

        def route(st, b):
            hi, lo = (v[:, :, 256 * b:256 * (b + 1)] for v in xTall)
            to_xT(st, b, hi, lo, None)
            sc = st.sm[:, 32:48]
            v = st.sm[:, 48:64]
            cmp1 = st.sm[:, 80:208]
            cmp2 = st.sm[:, 208:336]
            rank = st.sm[:, 336:352]
            rw = tuple(v_[:, :].rearrange("p (c n) -> p c n", c=2) for v_ in rwr)
            rb = part(wr, PR, "rb")
            pe.wait(st.xT_ok, st.bf[1], rw_ok)
            for j in range(2):
                for k in range(2):
                    m = mm3(bank(st, 1)[:, 8 * j:8 * j + 8], tuple(v_[:, k, j * 128:(j + 1) * 128] for v_ in (hi, lo)), cols(rw, A, k), k == 0, k == 1)
            act.wait(m, st.last["dve"])
            t = func(sc, bank(st, 1)[:, 0:16], ACT.Tanh, scale=0.5)
            st.bf[1] = t
            dve.wait(t)
            t = ts(sc, sc, 0.5, 0.5, ALU.mult, ALU.add)
            dve.wait(t)
            t = tt(v.rearrange("p (j e) -> p j e", j=2), sc.rearrange("p (j e) -> p j e", j=2),
                   rb.unsqueeze(1).to_broadcast([P, 2, 8]), ALU.add)
            dve.wait(t)
            for j in range(2):
                mine = v[:, 8 * j:8 * j + 8].unsqueeze(2).to_broadcast([P, 8, 8])
                other = v[:, 8 * j:8 * j + 8].unsqueeze(1).to_broadcast([P, 8, 8])
                c1 = cmp1[:, 64 * j:64 * j + 64].rearrange("p (e f) -> p e f", e=8)
                c2 = cmp2[:, 64 * j:64 * j + 64].rearrange("p (e f) -> p e f", e=8)
                tt(c1, other, mine, ALU.is_gt)
                t = tt(c2, other, mine, ALU.is_equal)
                dve.wait(t)
                t = tt(c2, c2, tri, ALU.mult)
            dve.wait(t)
            t = tt(cmp1, cmp1, cmp2, ALU.add)
            dve.wait(t)
            t = dve.do(lambda e: e.tensor_reduce(rank, cmp1.rearrange("p (a f) -> p a f", f=8), AX.X, ALU.add))
            dve.wait(t)
            t = stt(gates[:, 16 * b:16 * b + 16], rank, 2.0, sc, ALU.is_lt, ALU.mult)
            st.acc = t
            ended(st, pe=m, dve=t)
            yield

        def fetch_unit(u):
            i = u % 2
            sp.wait(u_split[i])
            dma(raw[:, UW * i:UW * (i + 1)], wu_in[:, UW * u:UW * (u + 1)], d_u[i])
            loaded(pool, d_u[i], 16 * (u // 2 + 1))
            loaded(act, d_u[i], 16 * (u // 2 + 1))
            for lane in (act, pool):
                lane.wait(*u_read[i])
            h = copy(uw[i][0][:, :], raw[:, UW * i:UW * (i + 1)])
            pool.wait(h)
            u_split[i] = tt(uw[i][1][:, :], raw[:, UW * i:UW * (i + 1)], uw[i][0][:, :].bitcast(F32), ALU.subtract, pool)
            u_ok[u] = u_split[i]

        u_split = [None, None]
        u_read = [[], []]
        u_ok = {}

        def moe(st):
            hf = st.m[:, 0:1024]
            hr = tuple(st.r[:, 1024 * i:1024 * (i + 1)] for i in range(2))
            prev = None
            mdown = None
            turn_ = 0
            for u in range(NU):
                w = uw[u % 2]
                up = tuple(v[:, 0:1024].rearrange("p (k n) -> p k n", k=2) for v in w)
                dn = tuple(v[:, 1024:1536].rearrange("p (k n) -> p k n", k=2) for v in w)
                for n, half in enumerate((st.i, st.i + 2)):
                    if prev is not None:
                        mdown = down(st, *prev)
                    if st.i == 1 and n == 0 and 0 < u < NU - 1:
                        fetch_unit(u + 1)
                    a, b_ = (0, 1) if turn_ % 2 == 0 else (1, 0)
                    turn_ += 1
                    pe.wait(u_ok[u])
                    for c in range(4):
                        pr = a if c < 2 else b_
                        if c % 2 == 0:
                            pe.wait(st.bf[2 * pr], st.bf[2 * pr + 1])
                        for k in range(2):
                            m = mm3(bank(st, 2 * pr + c % 2), cols(up, A, k, slice(128 * c, 128 * (c + 1))),
                                    tuple(v[:, k, 512 * half:512 * (half + 1)] for v in xTall), k == 0, k == 1)
                        if c == 1:
                            act.wait(m, st.h_rd)
                            sok = func(hf, pair(st, a), ACT.Silu)
                            st.bf[2 * a] = st.bf[2 * a + 1] = sok
                    dve.wait(m, sok)
                    hok = tt(hf, hf, pair(st, b_), ALU.mult)
                    st.bf[2 * b_] = st.bf[2 * b_ + 1] = hok
                    act.wait(hok, mdown)
                    hh = copy(hr[0], hf)
                    pool.wait(hh, mdown)
                    st.h_rd = lok = tt(hr[1], hf, hr[0].bitcast(F32), ALU.subtract, pool)
                    prev = (u, half, lok, a, dn, hr)
                    yield
            mdown = down(st, *prev)
            ended(st, pe=mdown, act=hh, dve=st.acc, pool=lok)
            yield

        def down(st, u, half, hok, pr, dn, hr):
            h = tuple(v.rearrange("p (k n) -> p k n", k=2) for v in hr)
            pe.wait(hok, st.bf[2 * pr], st.bf[2 * pr + 1])
            for t in range(4):
                for k in range(2):
                    m = mm3(pair(st, pr)[:, 256 * t:256 * (t + 1)], cols(h, A, k, slice(128 * t, 128 * (t + 1))), cols(dn, A, k), k == 0, k == 1)
            if half == st.i + 2:
                u_read[u % 2] = ([] if st.i == 0 else u_read[u % 2]) + [m]
            dve.wait(m, st.acc)
            for t in range(4):
                tile = 4 * half + t
                xs = x[:, tile, :]
                y = pair(st, pr)[:, 256 * t:256 * (t + 1)]
                if u < NE:
                    r = stt(xs, y, gates[:, 8 * tile + u:8 * tile + u + 1], xs, ALU.mult, ALU.add)
                else:
                    r = tt(xs, y, xs, ALU.add)
                x_ok[tile] = r
            st.bf[2 * pr] = st.bf[2 * pr + 1] = st.acc = r
            return m

        def norm_only(st, b):
            layernorm(st, b)
            yield

        def heads(st):
            m, r = st.m, st.r
            qp = m[:, 0:2048].rearrange("p (j h n) -> p j h n", j=2, h=16)
            kp = m[:, 2048:4096].rearrange("p (j h n) -> p j h n", j=2, h=16)
            pt = m[:, 2048:3072]
            o = m[:, 3072:3584].rearrange("p (j n) -> p j n", j=2)
            va = m[:, 4096:4640].rearrange("p (k h n) -> p k h n", k=2, h=16)
            qT = r[:, 1024:3072].rearrange("p (c n) -> p c n", c=8)
            kT = r[:, 3072:5120].rearrange("p (c n) -> p c n", c=8)
            oT = tuple(r[:, 1024 + 512 * i:1536 + 512 * i].rearrange("p (c n) -> p c n", c=2) for i in range(2))
            return qp, kp, qT, kT, pt, oT, va, o

        def stack(q, qp, kp, j, ready):
            act.wait(ready)
            qh = qp[:, j, :, 0:32].rearrange("p h (a n) -> p h a n", a=2).bitcast(F32R)
            h1 = copy(qh, q[:, 0:16, :].unsqueeze(2).to_broadcast([P, 16, 2, 16]))
            kh = kp[:, j, :, 0:64].rearrange("p h (a n) -> p h a n", a=2)[:, :, :, 0:16].bitcast(F32R)
            h2 = copy(kh, q[:, 16:32, :].unsqueeze(2).to_broadcast([P, 16, 2, 16]))
            dve.wait(h1, h2)
            tt(qp[:, j, :, 32:48].bitcast(F32R), q[:, 0:16, :], qp[:, j, :, 0:16], ALU.subtract)
            return tt(kp[:, j, :, 16:32].bitcast(F32R), q[:, 16:32, :], kp[:, j, :, 0:16], ALU.subtract)

        def clear(st, qp, kp, va):
            pool.wait(st.last["pool"])
            mset(pool, qp[:, :, :, 48:64], 0.0)
            mset(pool, kp[:, :, :, 48:64], 0.0)
            z = mset(pool, va[:, :, :, 16:17], 1.0)
            pool.wait(z)
            return mset(pool, kp[:, :, :, 48:49], 1.0)

        def turn(st, srcs, dsts):
            for s, d in zip(srcs, dsts):
                for i in range(2):
                    pe.wait(st.bf[2 * i], st.bf[2 * i + 1])
                    for c in range(4):
                        for j in range(2):
                            h = 2 * (4 * i + c)
                            m = tp(pair(st, i)[:, c * 256 + j * 128:c * 256 + (j + 1) * 128],
                                   s[:, j, h:h + 2, :].rearrange("p h n -> p (h n)"))
                    act.wait(m)
                    t = copy(d[:, 4 * i:4 * i + 4, :].rearrange("p c n -> p (c n)"), pair(st, i))
                    st.bf[2 * i] = st.bf[2 * i + 1] = t
            return m, t

        def maxima(st, qT, kT, qp, K, turned):
            for j in range(2):
                for g in range(4):
                    i = g % 2
                    pe.wait(st.bf[2 * i], st.bf[2 * i + 1])
                    for a in range(2):
                        r = 64 * a
                        for c in range(2):
                            m = mm(bank(st, 2 * i + a)[:, c * 256:(c + 1) * 256], qT[r:r + K, 2 * g + c, j * 128:(j + 1) * 128],
                                   kT[r:r + K, 2 * g + c, :], True, True)
                    dve.wait(m, turned)
                    t = dve.do(lambda e, j=j, g=g, i=i: e.tensor_reduce(
                        qp[:, j, 4 * g:4 * g + 4, 48].rearrange("p (c a) -> p a c", a=2),
                        pair(st, i).rearrange("p (a c n) -> p a c n", a=2, c=2), AX.X, ALU.max, negate=True))
                    st.bf[2 * i] = st.bf[2 * i + 1] = t
                    if g % 2:
                        yield
            st.max_ok, st.max_pe = t, m

        def weigh(st, qT, kT, pt, va, K, scale, vok, prev):
            mo = prev
            pe.wait(st.bf[2], st.bf[3], vok)
            p4 = pt.rearrange("p (a k n) -> p a k n", a=2, k=2)
            for g in range(8):
                pe.wait(st.bf[0], st.bf[1])
                for a in range(2):
                    r = 64 * a
                    for k in range(2):
                        m = mm(pair(st, 0)[:, (2 * a + k) * 256:(2 * a + k + 1) * 256], kT[r:r + K, g, k * 128:(k + 1) * 128],
                               qT[r:r + K, g, :], True, True)
                act.wait(m, mo)
                eok = func(pt, pair(st, 0), ACT.Exp, scale=scale)
                st.bf[0] = st.bf[1] = eok
                yield
                pe.wait(eok)
                for a in range(2):
                    h = 2 * g + a
                    for j in range(2):
                        for k in range(2):
                            mo = mm(bank(st, 2 + j)[:, 17 * h:17 * h + 17], p4[:, a, k, j * 128:(j + 1) * 128], va[:, k, h, :], k == 0, k == 1)
            st.pv_ok, st.pv_exp, st.s_pe = mo, eok, m

        def normalise(st, o):
            rc = st.sm[:, 64:96].rearrange("p (j n) -> p j n", j=2)
            dve.wait(st.pv_ok)
            ob = pair(st, 1).rearrange("p (j n) -> p j n", j=2)[:, :, 0:272].rearrange("p j (h n) -> p j h n", h=16)
            t = dve.do(lambda e: e.reciprocal(rc, ob[:, :, :, 16]))
            dve.wait(t)
            for j in range(2):
                t = tt(o[:, j, :].rearrange("p (h n) -> p h n", h=16), ob[:, j, :, 0:16],
                       rc[:, j, :].unsqueeze(2).to_broadcast([P, 16, 16]), ALU.mult)
            st.bf[2] = st.bf[3] = t
            return t

        def project(st, b, o, oT, w, ook, xbias, final=False):
            pe.wait(ook, st.bf[0], st.bf[1])
            for c in range(2):
                for j in range(2):
                    m = tp(bank(st, 0)[:, c * 256 + j * 128:c * 256 + (j + 1) * 128], o[:, j, c * 128:(c + 1) * 128])
            t = split(bank(st, 0).rearrange("p (c n) -> p c n", c=2), *oT, m)
            st.bf[0] = t
            pe.wait(t)
            for j in range(2):
                for c in range(2):
                    m = mm3(bank(st, 1)[:, j * 256:(j + 1) * 256], cols(oT, A, c, slice(j * 128, (j + 1) * 128)), cols(w, A, c), c == 0, c == 1)
            ended(st, pe=m, act=st.pv_exp)
            layernorm(st, b, bank(st, 1).rearrange("p (j n) -> p j n", j=2), 1, (m, xbias), final)

        def qkv_mm(st, w):
            pe.wait(st.xT_ok)
            for j in range(2):
                pe.wait(st.bf[2 + j])
                for k in range(2):
                    m = mm3(bank(st, 2 + j), cols(st.xT, A, k, slice(j * 128, (j + 1) * 128)), cols(w, A, k, slice(0, 512)), k == 0, k == 1)
            pe.wait(st.bf[1])
            for j in range(2):
                for k in range(2):
                    m = mm3(bank(st, 1)[:, j * 256:(j + 1) * 256], cols(st.xT, A, k, slice(j * 128, (j + 1) * 128)), cols(w, A, k, slice(512, 768)), k == 0, k == 1)
            return m

        def l1_attn(st, b):
            fence(st)
            qp, kp, qT, kT, pt, oT, va, o = heads(st)
            t1 = st.m[:, 4640:5152].rearrange("p (h n) -> p h n", h=32)
            t2 = st.m[:, 5152:5664].rearrange("p (h n) -> p h n", h=32)
            z = clear(st, qp, kp, va)
            own_xT(st, b)
            xbias = add_bias(st, b, part(w1f, P1F, "bao"))
            m = qkv_mm(st, pair_of(w1, P1, "wqkv", 2))
            act.wait(m)
            vok = copy(va[:, :, :, 0:16], bank(st, 1).rearrange("p (k h n) -> p k h n", k=2, h=16))
            st.bf[1] = vok
            yield
            dve.wait(m, z)
            tl = None
            for j in range(2):
                qk = bank(st, 2 + j).rearrange("p (h n) -> p h n", h=32)
                dve.wait(tl)
                tt(t1, qk, ropec[:, j, :].unsqueeze(1).to_broadcast([P, 32, 16]), ALU.mult)
                tt(t2[:, :, 0:8], qk[:, :, 8:16], ropes[:, j, 0:8].unsqueeze(1).to_broadcast([P, 32, 8]), ALU.mult)
                a = tt(t2[:, :, 8:16], qk[:, :, 0:8], ropes[:, j, 8:16].unsqueeze(1).to_broadcast([P, 32, 8]), ALU.mult)
                st.bf[2 + j] = a
                dve.wait(a)
                a = tt(t1, t1, t2, ALU.add)
                tl = stack(t1, qp, kp, j, a)
            pe.wait(tl, z)
            m, t = turn(st, (qp, kp), (qT, kT))
            yield
            pe.wait(t)
            yield from maxima(st, qT, kT, qp, 49, m)
            pe.wait(st.max_ok)
            act.wait(st.max_pe)
            m, t = turn(st, (qp,), (qT,))
            pe.wait(t)
            yield
            yield from weigh(st, qT, kT, pt, va, 49, 0.25, vok, None)
            ook = normalise(st, o)
            yield
            project(st, b, o, oT, pair_of(w1, P1, "wao", 2), ook, xbias)
            yield

        sim = small[:, 0:16]
        gg = small[:, 16:32]
        pos = small[:, 32:48]
        qf = small[:, 48:80].rearrange("p (t n) -> p t n", n=2)
        kf = small[:, 80:112].rearrange("p (t n) -> p t n", n=2)
        qxf = small[:, 112:144].rearrange("p (t n) -> p t n", n=2)
        ext = small[:, 144:146]
        ext2 = small[:, 146:148]
        den = small[:, 148:149]
        tmp16 = small[:, 149:165]
        tmpb = small[:, 165:181]
        gsq = small[:, 192:448]
        g_ok = []
        sim_ok = []
        kept = []

        def guide():
            g = part(w1f, P1F, "g")
            t = tt(gsq, g, g, ALU.mult)
            dve.wait(t)
            g_ok.append(dve.do(lambda e: e.tensor_reduce(gg, gsq.rearrange("p (h n) -> p h n", h=16), AX.X, ALU.add)))

        def ffn_qkv(st, b):
            fence(st)
            g = part(w1f, P1F, "g")
            qkv = st.m[:, 1024:2560].rearrange("p (j n) -> p j n", j=2)
            sq = st.m[:, 0:512].rearrange("p (j n) -> p j n", j=2)
            qg = st.m[:, 512:1024].rearrange("p (j n) -> p j n", j=2)
            qq = st.sm[:, 32:64].rearrange("p (j n) -> p j n", j=2)
            dq = st.sm[:, 64:96].rearrange("p (j n) -> p j n", j=2)
            own_xT(st, b)
            add = add_bias(st, b, part(w1f, P1F, "fb"))
            x_ok[2 * b] = x_ok[2 * b + 1] = add
            m = qkv_mm(st, pair_of(w1, P1, "fqkv", 2))
            act.wait(m)
            for j in range(2):
                c1 = copy(qkv[:, j, 0:512], bank(st, 2 + j))
                st.bf[2 + j] = c1
            c2 = copy(qkv[:, :, 512:768], bank(st, 1).rearrange("p (j n) -> p j n", j=2))
            st.bf[1] = c2
            sp.wait(c2)
            dma(keep[b], st.m[:, 1024:2560], d_kp[st.i])
            kept.append(b)
            yield
            dve.wait(c1)
            qv = qkv[:, :, 0:256]
            tt(sq, qv, qv, ALU.mult)
            t = tt(qg, qv, g.unsqueeze(1).to_broadcast([P, 2, 256]), ALU.mult)
            dve.wait(t)
            dve.do(lambda e: e.tensor_reduce(qq, sq.rearrange("p j (h n) -> p j h n", h=16), AX.X, ALU.add))
            t = dve.do(lambda e: e.tensor_reduce(dq, qg.rearrange("p j (h n) -> p j h n", h=16), AX.X, ALU.add))
            dve.wait(t, g_ok[0])
            t = tt(qq, qq, gg.unsqueeze(1).to_broadcast([P, 2, 16]), ALU.mult)
            pool.wait(t)
            p = tt(qq, qq, mhalf.rearrange("p (j n) -> p j n", j=2), ALU.pow, pool)
            dve.wait(p)
            t = tt(dq, dq, qq, ALU.mult)
            dve.wait(t)
            t = dve.do(lambda e: e.tensor_reduce(sim[:, 2 * b:2 * b + 2], dq, AX.X, ALU.add))
            sim_ok.append(t)
            ended(st, pe=m, act=c2, dve=t, pool=p)
            yield

        def stored(st, b):
            for lane in (act, dve, pool):
                loaded(lane, d_kp[st.i], 16 * (b // 2 + 1))
            return
            yield

        def choose():
            dve.wait(*sim_ok)
            t = ts(sim, sim, 1.0 / 16.0, None, ALU.mult)
            dve.wait(t)
            t = tt(tmp16, sim, vm, ALU.mult)
            dve.wait(t)
            t = stt(tmpb, vmi, -BIG, tmp16, ALU.mult, ALU.add)
            t2 = stt(tmp16, vmi, BIG, tmp16, ALU.mult, ALU.add)
            dve.wait(t, t2)
            dve.do(lambda e: e.tensor_reduce(ext[:, 0:1], tmpb, AX.X, ALU.max))
            t = dve.do(lambda e: e.tensor_reduce(ext[:, 1:2], tmp16, AX.X, ALU.min, negate=True))
            pool.wait(t)
            t = pool.do(lambda e: e.partition_all_reduce(ext2, ext, P, RMAX))
            dve.wait(t)
            t = tt(den, ext2[:, 0:1], ext2[:, 1:2], ALU.add)
            t2 = ts(tmp16, sim, ext2[:, 1:2], None, ALU.add)
            dve.wait(t, t2)
            t = ts(den, den, 0.9, None, ALU.mult)
            dve.wait(t)
            t = ts(pos, tmp16, den, None, ALU.is_gt)
            dve.wait(t)
            t = tt(pos, pos, vm, ALU.mult)
            dve.wait(t)
            tt(kf[:, :, 0], vm, pos, ALU.subtract)
            dve.do(lambda e: e.tensor_copy(kf[:, :, 1], pos))
            t = tt(tmpb, pos, vmi, ALU.add)
            dve.wait(t)
            ts(qf[:, :, 0], tmpb, -BIG, None, ALU.mult)
            t = ts(qf[:, :, 1], tmpb, BIG, -BIG, ALU.mult, ALU.add)
            dve.wait(t)
            dve.do(lambda e: e.tensor_copy(qxf[:, :, 0], qf[:, :, 1]))
            t = dve.do(lambda e: e.tensor_copy(qxf[:, :, 1], qf[:, :, 0]))
            sim_ok.append(t)

        def ffn_attn(st, b):
            fence(st)
            qp, kp, qT, kT, pt, oT, va, o = heads(st)
            qx = st.m[0:32, 4640:5664].rearrange("p (h n) -> p h n", h=16)
            raw_ = st.m[:, 5664:7200].rearrange("p (j n) -> p j n", j=2)
            qxT = st.r[:, 0:256].rearrange("p (c n) -> p c n", c=8)
            wide = st.r[:, 0:384]
            ptx = st.m[:, 0:256].rearrange("p (h k n) -> p h k n", h=16, k=2)
            ox = st.m[0:8, 256:512].rearrange("p (h n) -> p h n", h=16)
            rx = st.sm[0:8, 96:112]
            z = clear(st, qp, kp, va)
            for lane in (act, dve):
                loaded(lane, d_raw[st.i], 16 * (b // 2 + 1))
                lane.wait(z)
            for j in range(2):
                tl = stack(raw_[:, j, 0:512].rearrange("p (h n) -> p h n", h=32), qp, kp, j, None)
                vok = copy(va[:, j, :, 0:16], raw_[:, j, 512:768].rearrange("p (h n) -> p h n", h=16))
            if b + 2 < B:
                sp.wait(tl, vok)
                dma(st.m[:, 5664:7200], keep[b + 2], d_raw[st.i])
            dve.wait(z, sim_ok[-1])
            for j in range(2):
                dve.do(lambda e, j=j: e.tensor_copy(qp[:, j, :, 49:51], qf[:, 2 * b + j, :].unsqueeze(1).to_broadcast([P, 16, 2])))
                t = dve.do(lambda e, j=j: e.tensor_copy(kp[:, j, :, 49:51], kf[:, 2 * b + j, :].unsqueeze(1).to_broadcast([P, 16, 2])))
            dve.wait(t, tl)
            t = dve.do(lambda e: e.tensor_copy(qx, qp[0:32, 0, :, :]))
            dve.wait(t)
            xq = dve.do(lambda e: e.tensor_copy(qx[:, :, 49:51], qxf[0:32, 2 * b, :].unsqueeze(1).to_broadcast([32, 16, 2])))
            yield
            pe.wait(xq, vok, z)
            m, t = turn(st, (qp, kp), (qT, kT))

            def turn_x():
                pe.wait(st.bf[0])
                for c in range(8):
                    m = tp(bank(st, 0)[:, 32 * c:32 * c + 32], qx[:, 2 * c:2 * c + 2, :].rearrange("p h n -> p (h n)"), 32)
                act.wait(m)
                t = copy(qxT.rearrange("p c n -> p (c n)"), bank(st, 0)[:, 0:256])
                st.bf[0] = t
                return m, t

            mx, t = turn_x()
            yield
            pe.wait(t)
            yield from maxima(st, qT, kT, qp, 51, mx)
            for g in range(4):
                i = g % 2
                pe.wait(st.bf[2 * i], st.bf[2 * i + 1])
                for a in range(2):
                    r = 64 * a
                    for c in range(2):
                        m = mm(bank(st, 2 * i + a)[:, c * 256:(c + 1) * 256], wide[r:r + 51, 32 * (2 * g + c):32 * (2 * g + c) + 128], kT[r:r + 51, 2 * g + c, :], True, True)
                dve.wait(m)
                t = dve.do(lambda e, g=g, i=i: e.tensor_reduce(
                    qx[:, 4 * g:4 * g + 4, 48].rearrange("p (c a) -> p a c", a=2),
                    pair(st, i)[0:32, :].rearrange("p (a c n) -> p a c n", a=2, c=2), AX.X, ALU.max, negate=True))
                st.bf[2 * i] = st.bf[2 * i + 1] = t
            yield
            pe.wait(t, st.max_ok)
            act.wait(m)
            turn(st, (qp,), (qT,))
            m, t = turn_x()
            pe.wait(t)
            yield
            yield from weigh(st, qT, kT, pt, va, 51, 0.25, vok, None)
            ook = normalise(st, o)
            yield
            pe.wait(*st.bf)
            for h in range(16):
                r = 64 * (h % 2)
                for k in range(2):
                    at = 16 * (h // 2) + 8 * k
                    m = mm(bank(st, h % 2)[:, at:at + 8], kT[r:r + 51, h // 2, k * 128:(k + 1) * 128], qxT[r:r + 51, h // 2, 0:8], True, True)
            act.wait(m)
            t = func(ptx.rearrange("p (r c) k n -> p r (c k n)", r=2), pair(st, 0).rearrange("p (r n) -> p r n", r=2)[:, :, 0:128],
                     ACT.Exp, scale=0.25)
            st.bf = [t] * 4
            pe.wait(t)
            for h in range(16):
                for k in range(2):
                    m = mm(bank(st, 1)[0:8, 17 * h:17 * h + 17], ptx[:, 8 * (h % 2) + h // 2, k, :], va[:, k, h, :], k == 0, k == 1)
            dve.wait(m)
            ob = bank(st, 1)[0:8, 0:272].rearrange("p (h n) -> p h n", h=16)
            t = dve.do(lambda e: e.reciprocal(rx, ob[:, :, 16]))
            dve.wait(t)
            t = tt(ox, ob[:, :, 0:16], rx.unsqueeze(2).to_broadcast([8, 16, 16]), ALU.mult)
            st.bf[1] = t
            dve.wait(t, ook)
            ov = o[0:REG, 0, :].rearrange("p (h n) -> p h n", h=16)
            t = tt(ov, ov, ox[0:REG, :, :], ALU.add)
            dve.wait(t)
            ook = ts(o[0:REG, 0, :], o[0:REG, 0, :], 0.5, None, ALU.mult)
            yield
            project(st, b, o, oT, pair_of(w1, P1, "fproj", 2), ook, x_ok[2 * b], True)
            yield

        def together(work):
            gens = [(w() if callable(w) else w) for w in work]
            while gens:
                for g in list(gens):
                    try:
                        next(g)
                    except StopIteration:
                        gens.remove(g)

        def each(st, *fs):
            for b in st.batches:
                for f in fs:
                    yield from f(st, b)

        def split_weights(pieces, hi, lo, raws):
            for (a, n, sem_), rw_ in zip(pieces, raws):
                loaded(act, sem_[0], sem_[1])
                loaded(pool, sem_[0], sem_[1])
                h = copy(hi[:, a:a + n], rw_)
                pool.wait(h)
                t = tt(lo[:, a:a + n], rw_, hi[:, a:a + n].bitcast(F32), ALU.subtract, pool)
                yield t

        ph1 = ExitStack()
        w0 = (sb("w0h", N0, F32R, ph1), sb("w0l", N0, F32R, ph1))
        w0f = sb("w0f", N0F, F32, ph1)
        work(ph1, "1", 4400, 6400)
        tail = sb("w0tail", 1024, F32, ph1)
        dma(cst[:, :], const_in, d_cst)
        dma(xres[:, :], x_in, d_x)
        cuts = [(0, 4224, streams[0].m[:, 0:4224]), (4224, 4096, streams[1].m[:, 0:4096]), (8320, 1024, tail[:, :])]
        for n in (0, 2, 1):
            a, c, r = cuts[n]
            dma(r, w0_in[:, a:a + c], d_w0[n])
            if n == 0:
                dma(w0f[:, :], w0f_in, d_w0f)
        dma(ctxT[:, :], ctx_in, d_ctx)
        for lane in (pe, act, dve, pool):
            for s in (d_cst, d_x, d_ctx, d_w0f):
                loaded(lane, s)
        idr = copy(identr, ident)
        got = list(split_weights([(cuts[n][0], cuts[n][1], (d_w0[n], 16)) for n in (0, 2, 1)], *w0, [cuts[n][2] for n in (0, 2, 1)]))
        for lane in (pe, act, dve, pool):
            lane.wait(got[-1], idr)
        together([each(st, l0_attn, lambda st, b: xattn(st, b, w0, P0, w0f, P0F)) for st in streams])
        ph1.close()

        w1 = (sb("w1h", N1, F32R), sb("w1l", N1, F32R))
        w1f = sb("w1f", N1F)
        ph2 = ExitStack()
        work(ph2, "2", 1024, 2048)
        xTall = tuple(sb(f"xTall{i}", 4096, F32R, ph2)[:, :].rearrange("p (k n) -> p k n", k=2) for i in range(2))
        gates = sb("gates", 128, F32, ph2)
        raw = sb("raw", 2 * UW, F32, ph2)
        raw1 = sb("raw1", 1024, F32, ph2)
        uw = [tuple(sb(f"uw{i}{j}", UW, F32R, ph2) for j in range(2)) for i in range(2)]
        wr = sb("wr", NR, F32, ph2)
        rwr = tuple(sb(f"rwr{j}", 16, F32R, ph2) for j in range(2))
        ended1 = over()
        for lane in (pe, act, dve, pool, sp):
            lane.wait(*ended1)
        dma(wr[:, :], wr_in, d_wr)
        loaded(act, d_wr)
        loaded(dve, d_wr)
        h = copy(rwr[0][:, :], part(wr, PR, "rw"))
        dve.wait(h)
        rw_ok = tt(rwr[1][:, :], part(wr, PR, "rw"), rwr[0][:, :].bitcast(F32), ALU.subtract)
        fetch_unit(0)
        fetch_unit(1)
        dma(w1f[:, :], w1f_in, d_w1f)
        together([each(st, route) for st in streams])
        gates_ok = [st.acc for st in streams]
        for st in streams:
            st.h_rd = None
            pe.wait(*[s.xT_ok for s in streams])
            dve.wait(*gates_ok)

        def weights1():
            done = None
            for n, (a, c) in enumerate([(1024 * i, 1024) for i in range(N1 // 1024)]):
                sp.wait(done)
                dma(raw1[:, 0:c], w1_in[:, a:a + c], d_w1)
                yield
                yield
                for t in split_weights([(a, c, (d_w1, 16 * (n + 1)))], *w1, [raw1[:, 0:c]]):
                    done = t
                yield
            w1_ok.append(done)

        w1_ok = []
        together([moe(streams[0]), moe(streams[1]), weights1()])
        for st in streams:
            ended(st, dve=st.acc)
        together([each(st, norm_only) for st in streams])
        ph2.close()

        ph3 = ExitStack()
        work(ph3, "3", 5664, 6400)
        ended2 = over()
        for lane in (pe, act, dve, pool, sp):
            lane.wait(*ended2, *w1_ok)
        for lane in (pe, act, dve, pool):
            loaded(lane, d_w1f)
        d_kp = [sem(f"d_kp{i}") for i in range(2)]
        guide()
        together([each(st, l1_attn, lambda st, b: xattn(st, b, w1, P1, w1f, P1F), ffn_qkv, stored) for st in streams])
        ph3.close()

        ph4 = ExitStack()
        work(ph4, "4", 7200, 5120)
        ended3 = over()
        for lane in (pe, act, dve, pool, sp):
            lane.wait(*ended3, *sim_ok)
            for st in streams:
                loaded(lane, d_kp[st.i], 16 * 4)
        for st in streams:
            dma(st.m[:, 5664:7200], keep[st.i], d_raw[st.i])
            pe.wait(copy(st.r[:, 256:384], ident))
        choose()
        together([each(st, ffn_attn) for st in streams])
        for n, (tile, t) in enumerate(outs):
            sp.wait(t)
            dma(out[tile * P:(tile + 1) * P, :], x[:, tile, :], d_out)
        loaded(sp, d_out, 16 * len(outs))
        ph4.close()

        for lane in (pe, act, dve, pool, sp):
            lane.count()

        block = es.enter_context(nc.Block())

        @block.sync
        def _(eng):
            sp.emit(eng)

        @block.tensor
        def _(eng):
            pe.emit(eng)

        @block.scalar
        def _(eng):
            act.emit(eng)

        @block.vector
        def _(eng):
            dve.emit(eng)

        @block.gpsimd
        def _(eng):
            pool.emit(eng)


def consts():
    c = np.zeros((P, NC_), np.float32)

    def put(name, v):
        a, n = PC[name]
        c[:, a:a + n] = v

    put("ident", np.eye(P, dtype=np.float32))
    put("ones", 1.0)
    inv = (1.0 / np.float32(10000.0) ** (np.arange(0, 16, 2, dtype=np.float32) / np.float32(16))).astype(np.float32)
    ang = np.arange(S, dtype=np.float32)[:, None] * inv[None, :]
    cos, sin = np.cos(ang).astype(np.float32), np.sin(ang).astype(np.float32)
    put("ropec", np.concatenate([cos, cos], 1).reshape(2, P, 16).transpose(1, 0, 2).reshape(P, 32))
    put("ropes", np.concatenate([-sin, sin], 1).reshape(2, P, 16).transpose(1, 0, 2).reshape(P, 32))
    put("tri", np.tril(np.ones((8, 8), np.float32), -1).reshape(1, 64))
    valid = np.ones((P, 16), np.float32)
    valid[0:REG, 0::2] = 0.0
    put("vm", valid)
    put("vmi", 1.0 - valid)
    put("half", -0.5)
    return c


def kernel(**inputs):
    import concourse.bacc as _bacc
    from concourse.bass_utils import run_bass_kernel_spmd as _run

    a = {k: np.asarray(v) for k, v in inputs.items()}

    def rows(w):
        k, n = w.shape
        return w.reshape(k // P, P, n).transpose(1, 0, 2).reshape(P, -1)

    def all_rows(v):
        return np.broadcast_to(v.reshape(1, -1), (P, v.size))

    def kv(wk, wv):
        return np.concatenate([wk[0:P], wv[0:P], np.concatenate([wk[P:CD], wv[P:CD]], 0)], 1)

    conv = np.concatenate([a["L0_attn_conv_w"], a["L0_attn_conv_b"][:, None], a["L0_attn_D"][:, None]], 1)
    w0 = np.concatenate([rows(a["L0_attn_W_in"].T), rows(a["L0_attn_W_xproj"].T), rows(a["L0_xattn_Wq"]), rows(a["L0_xattn_Wo"]),
                         rows(a["L0_attn_W_out"].T)], 1)
    w0f = np.concatenate([kv(a["L0_xattn_Wk"], a["L0_xattn_Wv"]), rows(conv), all_rows(a["L0_xattn_bo"])], 1)
    w12 = a["L0_ffn_w12"].transpose(0, 2, 1).reshape(NE, 2, P, 512)
    w3 = a["L0_ffn_w3"].transpose(0, 2, 1).reshape(NE, 2, P, 256)
    s1 = a["L0_ffn_shared_w1"].T.reshape(2, P, 4, 256)
    s2 = a["L0_ffn_shared_w2"].T.reshape(2, P, 4, 256)
    s12 = np.concatenate([s1, s2], 3).transpose(2, 0, 1, 3)
    s3 = a["L0_ffn_shared_w3"].T.reshape(4, 2, P, 256)
    up = np.concatenate([w12, s12], 0).transpose(2, 0, 1, 3).reshape(P, NU, 1024)
    dn = np.concatenate([w3, s3], 0).transpose(2, 0, 1, 3).reshape(P, NU, 512)
    wu = np.concatenate([up, dn], 2).reshape(P, -1)
    wr = np.concatenate([rows(a["L0_ffn_router_w"].T), all_rows(a["L0_ffn_expert_bias"])], 1)
    w1 = np.concatenate([rows(a["L1_attn_w_qkv"].T), rows(a["L1_attn_w_out"].T), rows(a["L1_xattn_Wq"]), rows(a["L1_xattn_Wo"]),
                         rows(a["L1_ffn_W_qkv"]), rows(a["L1_ffn_W_proj"])], 1)
    w1f = np.concatenate([kv(a["L1_xattn_Wk"], a["L1_xattn_Wv"]), all_rows(a["L1_attn_b_out"]), all_rows(a["L1_xattn_bo"]),
                          all_rows(a["L1_ffn_b_proj"]), all_rows(a["L1_ffn_g_info"][0, 0])], 1)
    cT = a["ctx_768"]
    cT = np.concatenate([cT, cT[:, CK - 1:CK]], 1).reshape(B * CP, CD).T
    ctx = np.concatenate([cT[0:P], np.concatenate([cT[P:CD], cT[P:CD]], 0)], 1)
    x = a["x"].reshape(16, P, D).transpose(1, 0, 2).reshape(P, -1)
    arrays = {"x_dram": x, "ctx_dram": ctx, "w0_dram": w0, "w0f_dram": w0f, "wu_dram": wu, "wr_dram": wr, "w1_dram": w1,
              "w1f_dram": w1f, "const_dram": consts()}
    arrays = {k: np.ascontiguousarray(v) for k, v in arrays.items()}

    nc = _bacc.Bacc("TRN2", target_bir_lowering=False, num_devices=1)
    args = [nc.dram_tensor(k, v.shape, F32, kind="ExternalInput").ap() for k, v in arrays.items()]
    args.append(nc.dram_tensor("out_dram", (B * S, D), F32, kind="ExternalOutput").ap())
    args.append(nc.dram_tensor("keep_dram", (B, P, 1536), F32, kind="Internal").ap())
    program(nc, *args)
    r = _run(nc, [arrays], core_ids=[0])
    return r.results[0]["out_dram"].reshape(B, S, D)
```

```python
from contextlib import ExitStack
from itertools import chain

import numpy as np

import concourse.bass as bass
from concourse import mybir

F32 = mybir.dt.float32
F32R = mybir.dt.float32r
BF16 = mybir.dt.bfloat16
F16 = mybir.dt.float16
LIFT = float(10 * np.log(2.0))
ALU = mybir.AluOpType
ACT = mybir.ActivationFunctionType
AX = mybir.AxisListType
RMAX = bass.bass_isa.ReduceOp.max

P = 128
B, S, D, CK, CD = 8, 256, 256, 77, 192
H = 16
NE = 8
REG = 5
BIG = float(2.0 ** 100)
EPS = 1e-5

LAY0 = [("win", 2048), ("wxp", 2176), ("wout", 1024), ("wq", 2048), ("wo", 2048)]
LAY0F = [("conv", 24), ("bo", 256), ("wkv", 3072)]
LAY1 = [("wqkv", 1536), ("wao", 512), ("wq", 2048), ("wo", 2048), ("fqkv", 1536)]
NP = 512
LAY1F = [("wkv", 3072), ("bao", 256), ("bo", 256), ("fb", 256), ("g", 256)]
LAYR = [("rw", 16), ("rb", 8)]
LAYC = [("ident", 128), ("ones", 128), ("ropec", 32), ("ropes", 32), ("tri", 64), ("vm", 16), ("vmi", 16), ("half", 32), ("lift", 1)]
NU = NE + 4
UNITS = [*range(NE, NU), *range(NE)]
UW = 1536
CP = 78


def places(lay):
    at, out = 0, {}
    for name, n in lay:
        out[name] = (at, n)
        at += n
    return out, at


P0, N0 = places(LAY0)
P0F, N0F = places(LAY0F)
P1, N1 = places(LAY1)
P1F, N1F = places(LAY1F)
PR, NR = places(LAYR)
PC, NC_ = places(LAYC)


class Token:

    def __init__(self, lane, index):
        self.lane, self.index, self.used = lane, index, False


class Lane:

    def __init__(self, name, sem):
        self.name, self.sem, self.items = name, sem, []

    def wait(self, *tokens):
        for t in tokens:
            if t is not None:
                t.used = True
                self.items.append(("wait", t))

    def do(self, call):
        t = Token(self, len(self.items))
        self.items.append(("do", call, t))
        return t

    def count(self):
        n = 0
        for it in self.items:
            if it[0] == "do" and it[2].used:
                n += 1
                it[2].value = n

    def emit(self, eng):
        seen = {}
        for it in self.items:
            if it[0] == "wait":
                t = it[1]
                if seen.get(t.lane.name, 0) < t.value:
                    seen[t.lane.name] = t.value
                    eng.wait_ge(t.lane.sem, t.value)
            else:
                ins = it[1](eng)
                if it[2].used:
                    ins.then_inc(self.sem, 1)


class Stream:
    pass


def program(nc, x_in, ctx_in, w0_in, w0f_in, wu_in, wr_in, w1_in, w1f_in, const_in, out, keep):
    es = ExitStack()
    with es:
        def sb(name, n, dt=F32, scope=es):
            return scope.enter_context(nc.sbuf_tensor(name, [P, n], dt))

        def sem(name):
            return es.enter_context(nc.semaphore(name))

        xres = sb("xres", 16 * D)
        ctxT = sb("ctxT", 2 * B * CP)
        cst = sb("cst", NC_)
        identr_t = sb("identr", P, F32R)
        small = sb("small", 512)
        x = xres[:, :].rearrange("p (t d) -> p t d", d=D)
        ctx = ctxT[:, :].rearrange("p (k n) -> p k n", k=2)

        def part(t, pl, name, c=None):
            a, n = pl[name]
            v = t[:, a:a + n]
            return v if c is None else v.rearrange("p (c n) -> p c n", c=c)

        def pair_of(t, pl, name, c):
            return part(t[0], pl, name, c), part(t[1], pl, name, c)

        ident = part(cst, PC, "ident")
        identr = identr_t[:, :]
        ones = part(cst, PC, "ones")
        ropec = part(cst, PC, "ropec", 2)
        ropes = part(cst, PC, "ropes", 2)
        tri = part(cst, PC, "tri", 8)
        vm = part(cst, PC, "vm")
        vmi = part(cst, PC, "vmi")
        mhalf = part(cst, PC, "half")
        lift = part(cst, PC, "lift")

        pe, act, dve, pool, sp = (Lane(n, sem(f"s_{n}")) for n in ("pe", "act", "dve", "pool", "sp"))
        d_cst, d_ctx, d_w0f, d_kv, d_wr, d_w1f, d_w1, d_wp, d_out = (
            sem(f"d_{n}") for n in ("cst", "ctx", "w0f", "kv", "wr", "w1f", "w1", "wp", "out"))
        d_x = [sem(f"d_x{i}") for i in range(2)]
        d_w0 = {n: sem(f"d_{n}") for n in P0}
        d_u = [sem(f"d_u{i}") for i in range(2)]
        d_raw = [sem(f"d_raw{i}") for i in range(2)]

        def loaded(lane, s, v=16):
            lane.items.append(("do", lambda e: e.wait_ge(s, v), Token(lane, 0)))

        def dma(o, i, s):
            sp.do(lambda e: e.dma_start(o, i).then_inc(s, 16))

        streams = []
        for i in range(2):
            st = Stream()
            st.i = i
            st.sm = sb(f"sm{i}", 448)
            st.ps = es.enter_context(nc.psum_tensor(f"ps{i}", [P, 2048], F32))
            st.bf = [None] * 4
            st.xT_rd = None
            st.last = {"pe": None, "act": None, "dve": None, "pool": None}
            st.batches = [b for b in range(B) if b % 2 == i]
            streams.append(st)

        x_ok = [None] * 16

        def work(scope, name, nf, nr):
            for st in streams:
                st.m = sb(f"m{name}{st.i}", nf, F32, scope)
                st.r = sb(f"r{name}{st.i}", nr, F32R, scope)

        def over():
            return [t for st in streams for t in st.last.values()]

        def bank(st, i, n=512):
            return st.ps[:, 512 * i:512 * i + n]

        def pair(st, i):
            return st.ps[:, 1024 * i:1024 * (i + 1)]

        def mm(o, l, r, start, stop):
            return pe.do(lambda e: e.matmul(o, l, r, start=start, stop=stop))

        def tp(o, i, n=128):
            return pe.do(lambda e: e.transpose(o, i, ident[0:n, 0:n]))

        def copy(o, i):
            return act.do(lambda e: e.activation(o, i, ACT.Copy))

        def func(o, i, f, scale=1.0, bias=0.0):
            return act.do(lambda e: e.activation(o, i, f, scale=scale, bias=bias))

        def tt(o, a, b_, op, lane=None):
            return (lane or dve).do(lambda e: e.tensor_tensor(o, a, b_, op))

        def ts(o, a, s1, s2, op0, op1=None, lane=None):
            if op1 is None:
                return (lane or dve).do(lambda e: e.tensor_scalar(o, a, s1, None, op0))
            return (lane or dve).do(lambda e: e.tensor_scalar(o, a, s1, s2, op0, op1))

        def stt(o, a, s, b_, op0, op1):
            return dve.do(lambda e: e.scalar_tensor_tensor(out=o, in0=a, scalar=s, in1=b_, op0=op0, op1=op1))

        A = slice(None)

        def mset(lane, o, v):
            return lane.do(lambda e: e.memset(o, v))

        def split(ps, hi, lo, made, rd=None):
            act.wait(made, rd)
            h = copy(hi, ps)
            dve.wait(h, made)
            return tt(lo, ps, hi.bitcast(F32), ALU.subtract)

        def mm3(o, l, r, start, stop):
            mm(o, l[0], r[0], start, False)
            mm(o, l[0], r[1], False, False)
            return mm(o, l[1], r[0], False, stop)

        def cols(t, *idx):
            return tuple(v[idx] for v in t)

        def thirds(v3, v, rest, ready, one):
            n = v.shape[-1]
            act.wait(ready, one)
            h = copy(v3[0][..., 0:n], v)
            dve.wait(h, ready)
            t = read = tt(rest, v, v3[0][..., 0:n], ALU.subtract)
            act.wait(t)
            t = copy(v3[1][..., 0:n], rest)
            dve.wait(t)
            return read, tt(v3[2][..., 0:n], rest, v3[1][..., 0:n], ALU.subtract)

        def weights_of(ps, pf, ph, pl, scale, made, free, free_lo=None):
            act.wait(made, *free)
            h = func(ph, ps, ACT.Exp, scale=scale, bias=lift[0:ps.shape[0], :])
            f = func(pf, ps, ACT.Exp, scale=scale, bias=lift[0:ps.shape[0], :])
            dve.wait(f, h, *free, free_lo)
            return f, tt(pl, pf, ph, ALU.subtract)

        def fence(st):
            for lane in (pe, act, dve, pool):
                lane.wait(*[t for n, t in st.last.items() if n != lane.name])

        def ended(st, **last):
            st.last.update(last)

        def to_xT(st, b, hi, lo, rd):
            pe.wait(x_ok[2 * b], x_ok[2 * b + 1], st.bf[0])
            bk = bank(st, 0)
            for c in range(2):
                for j in range(2):
                    m = tp(bk[:, c * 256 + j * 128:c * 256 + (j + 1) * 128], x[:, 2 * b + j, c * 128:(c + 1) * 128])
            st.xT_src = m
            st.xT_ok = split(bk.rearrange("p (k n) -> p k n", k=2), hi, lo, m, rd)
            st.bf[0] = st.xT_ok

        def own_xT(st, b):
            st.xT = tuple(st.r[:, 512 * i:512 * (i + 1)].rearrange("p (k n) -> p k n", k=2) for i in range(2))
            to_xT(st, b, *st.xT, None)

        def add_bias(st, b, bias):
            pool.wait(st.xT_src, x_ok[2 * b], x_ok[2 * b + 1])
            for j in range(2):
                t = tt(x[:, 2 * b + j, :], x[:, 2 * b + j, :], bias, ALU.add, pool)
            return t

        def layernorm(st, b, ps=None, bk=None, after=(), final=False):
            xb = x[:, 2 * b:2 * b + 2, :]
            dve.wait(x_ok[2 * b], x_ok[2 * b + 1], *after)
            if ps is not None:
                r = tt(xb, ps, xb, ALU.add)
                st.bf[bk] = r
                dve.wait(r)
            s6 = st.sm[:, 0:12].rearrange("p (j n) -> p j n", j=2)
            mv = st.sm[:, 12:16].rearrange("p (j n) -> p j n", j=2)
            rs = st.sm[:, 16:18]
            t = [dve.do(lambda e, j=j: e.bn_stats(s6[:, j, :], xb[:, j, :])) for j in range(2)]
            for j in range(2):
                dve.wait(t[j])
                g = dve.do(lambda e, j=j: e.bn_aggr(mv[:, j, :], s6[:, j, :]))
            pool.wait(g)
            a = ts(rs, mv[:, :, 1], EPS, None, ALU.add, None, pool)
            pool.wait(a)
            q = tt(rs, rs, mhalf[:, 0:2], ALU.pow, pool)
            yield
            dve.wait(q, g)
            for j in range(2):
                n = ts(xb[:, j, :], xb[:, j, :], mv[:, j, 0:1], rs[:, j:j + 1], ALU.subtract, ALU.mult)
                x_ok[2 * b + j] = n
                if final:
                    outs.append((2 * b + j, n))
            ended(st, dve=n, pool=q)

        outs = []

        def l0_attn(st, b):
            fence(st)
            xb = st.m[:, 0:1036].rearrange("p (c n) -> p c n", c=4)
            xcf = st.m[:, 1036:2060]
            xc = xcf.rearrange("p (c n) -> p c n", c=4)
            szf = st.m[:, 2060:3084]
            sz = szf.rearrange("p (c n) -> p c n", c=4)
            tAf = st.m[:, 3084:4108]
            tA = tAf.rearrange("p (c n) -> p c n", c=4)
            Bc = st.m[:, 4108:4364]
            xr = tuple(st.r[:, 1024 * i:1024 * (i + 1)].rearrange("p (c n) -> p c n", c=4) for i in (1, 2))
            yr = tuple(st.r[:, 1024 * i:1024 * (i + 1)].rearrange("p (c n) -> p c n", c=4) for i in (3, 4))
            win = pair_of(w0, P0, "win", 2)
            cv = part(w0f, P0F, "conv", 4)
            wxp = pair_of(w0, P0, "wxp", 4)
            wout = pair_of(w0, P0, "wout", 4)
            if b < 4:
                for lane in (pe, dve, pool):
                    loaded(lane, d_x[b // 2])
            z0 = mset(dve, xb[:, :, 0:3], 0.0)
            own_xT(st, b)
            yield
            pe.wait(st.xT_ok, st.bf[2], st.bf[3], w0_ok["win"])
            for c in range(4):
                for k in range(2):
                    m = mm3(st.ps[:, 1024 + c * 256:1280 + c * 256], cols(win, A, k, slice(c * 128, (c + 1) * 128)), cols(st.xT, A, k), k == 0, k == 1)
            act.wait(m)
            cp = copy(xb[:, :, 3:259], pair(st, 1).rearrange("p (c n) -> p c n", c=4))
            st.bf[2] = st.bf[3] = cp
            pe.wait(st.bf[0], st.bf[1])
            for c in range(4):
                for k in range(2):
                    m = mm3(st.ps[:, c * 256:256 + c * 256], cols(win, A, k, slice(512 + c * 128, 640 + c * 128)), cols(st.xT, A, k), k == 0, k == 1)
            act.wait(m)
            zs = func(szf, pair(st, 0), ACT.Silu)
            st.bf[0] = st.bf[1] = zs
            yield
            if b < 2:
                loaded(dve, d_w0f)
                loaded(pool, d_w0f)
            dve.wait(cp, z0)
            last = [ts(xc[:, c, :], xb[:, c, 3:259], cv[:, c, 3:4], cv[:, c, 4:5], ALU.mult, ALU.add) for c in range(4)]
            for k in (2, 1, 0):
                for c in range(4):
                    dve.wait(last[c])
                    last[c] = stt(xc[:, c, :], xb[:, c, k:k + 256], cv[:, c, k:k + 1], xc[:, c, :], ALU.mult, ALU.add)
            act.wait(last[3])
            xs = func(xcf, xcf, ACT.Silu)
            act.wait(xs)
            t = copy(xr[0], xc)
            yield
            dve.wait(t, xs)
            xs = tt(xr[1], xc, xr[0].bitcast(F32), ALU.subtract)
            yield
            pe.wait(xs, st.bf[2], st.bf[3], w0_ok["wxp"])
            for c in range(4):
                for k in range(4):
                    m = mm3(st.ps[:, 1024 + c * 256:1280 + c * 256], cols(wxp, A, k, slice(32 + c * 128, 160 + c * 128)), cols(xr, A, k), k == 0, k == 3)
            pe.wait(st.bf[0])
            for c in range(2):
                for k in range(4):
                    m2 = mm3(st.ps[:, c * 256:(c + 1) * 256], cols(wxp, A, k, slice(16 * c, 16 * c + 128)), cols(xr, A, k), k == 0, k == 3)
            act.wait(m2)
            t = copy(Bc[0:16, :], st.ps[0:16, 0:256])
            dve.wait(t, m)
            t = tt(Bc[0:16, :], Bc[0:16, :], st.ps[0:16, 256:512], ALU.mult)
            st.bf[0] = t
            pe.wait(t, st.bf[1])
            mb = mm(st.ps[:, 512:768], ones[0:16, :], Bc[0:16, :], True, True)
            yield
            act.wait(m)
            t = func(tAf, pair(st, 1), ACT.Abs)
            act.wait(t)
            t = func(tAf, tAf, ACT.Exp, scale=-1.0)
            dve.wait(xs, zs)
            g = tt(szf, szf, xcf, ALU.mult)
            yield
            act.wait(t)
            t = func(tAf, tAf, ACT.Ln, bias=1.0)
            yield
            dve.wait(t)
            t = stt(tAf, pair(st, 1), 0.0, tAf, ALU.max, ALU.add)
            st.bf[2] = st.bf[3] = t
            dve.wait(t, mb)
            t = tt(tA, tA, st.ps[:, 512:768].unsqueeze(1).to_broadcast([P, 4, 256]), ALU.mult)
            st.bf[1] = t
            yield
            dve.wait(t, g)
            for c in range(4):
                t = stt(sz[:, c, :], tA[:, c, :], cv[:, c, 5:6], sz[:, c, :], ALU.add, ALU.mult)
            yield
            act.wait(t)
            ya = copy(yr[0], sz)
            yield
            dve.wait(ya)
            t = tt(yr[1], sz, yr[0].bitcast(F32), ALU.subtract)
            yield
            if b == 0:
                rest((pe, act, dve, pool))
            pe.wait(t, st.bf[3], w0_ok["wout"])
            for j in range(2):
                for k in range(4):
                    m = mm3(bank(st, 3)[:, j * 256:(j + 1) * 256], cols(yr, A, k, slice(j * 128, (j + 1) * 128)), cols(wout, A, k), k == 0, k == 3)
            ended(st, pe=m, act=ya)
            yield from layernorm(st, b, bank(st, 3).rearrange("p (j n) -> p j n", j=2), 3, (m,))
            yield

        def xattn(st, b, w, pl, wf, plf, w_ok, wide):
            fence(st)
            V = tuple(st.m[0:CK, 520 * i:520 * (i + 1)].bitcast(BF16).rearrange("p (h n) -> p h n", h=16) for i in range(3))
            vf = st.m[0:CK, 2584:3608].rearrange("p (h n) -> p h n", h=16)
            ptf = st.m[0:CK, 1560:2584]
            O = st.m[:, 2584:4632].rearrange("p (j n) -> p j n", j=2)
            pth = [st.m[0:CK, 4632 + 512 * i:5144 + 512 * i].bitcast(F16) for i in range(2)]
            ptl = [st.m[0:CK, 5656 + 512 * i:6168 + 512 * i].bitcast(F16) for i in (0, 1 if wide else 0)]
            QT = tuple(st.r[:, 1024 + 2048 * i:3072 + 2048 * i].rearrange("p (c n) -> p c n", c=8) for i in range(2))
            KT = tuple(st.r[:, a:a + 624].rearrange("p (c n) -> p c n", c=8) for a in (5120, 256))
            nmT = st.r[:, 0:256]
            nm = st.sm[:, 32:288].rearrange("p (j n) -> p j n", j=2)
            rc = st.sm[:, 288:296].rearrange("p (j n) -> p j n", j=2)
            wq = pair_of(w, pl, "wq", 2)
            wkv = part(wf, plf, "wkv", 3)
            wo = pair_of(w, pl, "wo", 8)
            kw = [(wkv[:, 0, :], 0, 128, 0), (wkv[0:64, 2, :], 0, 64, 1)]
            vw = [(wkv[:, 1, :], 0, 128, 0), (wkv[64:128, 2, :], 64, 64, 1)]
            pool.wait(st.last["pool"])
            mset(pool, st.sm[:, 32:288], 0.0)
            for i in range(3):
                one = mset(pool, V[i][:, :, 64:65], 0.0 if i else 1.0)
            own_xT(st, b)
            xbias = add_bias(st, b, part(wf, plf, "bo"))
            pe.wait(st.bf[2], st.bf[3], *w_ok)
            for i in range(2):
                for k, (w_, p0, n, r) in enumerate(vw):
                    m = mm(bank(st, 2 + i)[0:CK, :], ctx[p0:p0 + n, r, b * CP:b * CP + CK], w_[:, i * 512:(i + 1) * 512], k == 0, k == 1)
            vread, vok = thirds(V, st.ps[0:CK, 1024:2048].rearrange("p (h n) -> p h n", h=16), vf, m, one)
            st.bf[2] = st.bf[3] = vread
            yield
            pe.wait(st.xT_ok)
            for i in range(2):
                pe.wait(st.bf[2 * i], st.bf[2 * i + 1])
                for c in range(4):
                    for k in range(2):
                        m = mm3(pair(st, i)[:, c * 256:(c + 1) * 256], cols(wq, A, k, slice((4 * i + c) * 128, (4 * i + c + 1) * 128)), cols(st.xT, A, k), k == 0, k == 1)
                qok = split(pair(st, i).rearrange("p (c n) -> p c n", c=4), *cols(QT, A, slice(4 * i, 4 * i + 4)), m)
                st.bf[2 * i] = st.bf[2 * i + 1] = qok
                yield
            pe.wait(st.bf[0], st.bf[1])
            for c in range(8):
                for k, (w_, p0, n, r) in enumerate(kw):
                    m = mm(bank(st, c // 4)[:, CP * (c % 4):CP * (c % 4) + CP],
                           w_[:, c * 128:(c + 1) * 128], ctx[p0:p0 + n, r, b * CP:(b + 1) * CP], k == 0, k == 1)
            for i in range(2):
                kok = split(bank(st, i)[:, 0:4 * CP].rearrange("p (c n) -> p c n", c=4), *cols(KT, A, slice(4 * i, 4 * i + 4)), m)
            st.bf[0] = st.bf[1] = kok
            yield
            pe.wait(qok, kok)
            for j in range(2):
                for i in range(2):
                    pe.wait(st.bf[2 * i], st.bf[2 * i + 1])
                    for hh in range(8):
                        h = 8 * i + hh
                        r = 64 * (h % 2)
                        m = mm(bank(st, 2 * i + hh % 2)[:, CP * (hh // 2):CP * (hh // 2) + CP],
                               QT[0][r:r + 64, h // 2, j * 128:(j + 1) * 128], KT[0][r:r + 64, h // 2, :], True, True)
                    dve.wait(m, one)
                    src = pair(st, i).rearrange("p (a n) -> p a n", a=2)[:, :, 0:4 * CP].rearrange("p a (c n) -> p a c n", c=4)
                    dst = nm[:, j, 8 * i:8 * i + 8].rearrange("p (c a) -> p a c", a=2)
                    t = dve.do(lambda e, dst=dst, src=src: e.tensor_reduce(dst, src, AX.X, ALU.max, negate=True))
                    dve.wait(t)
                    up = dve.do(lambda e, i=i, j=j: e.tensor_copy(nm[:, j, 64 + 8 * i:72 + 8 * i], nm[:, j, 8 * i:8 * i + 8]))
                    st.bf[2 * i] = st.bf[2 * i + 1] = t
                yield
            pe.wait(up, t)
            for j in range(2):
                m = tp(st.ps[:, j * 128:(j + 1) * 128], nm[:, j, :])
            act.wait(m)
            nok = copy(nmT, st.ps[:, 0:256])
            st.bf[0] = nok
            pe.wait(nok)
            av = [None, None]
            eok = None

            def weigh_values(g, lok):
                ph, pl = (v[g % 2].rearrange("p (h n) -> p h n", h=4) for v in (pth, ptl))
                pe.wait(lok, vok, one, st.bf[2], st.bf[3])
                for j in range(2):
                    for hh in range(4):
                        q = 2 * (hh % 2) + hh // 2
                        o = bank(st, 2 + j)[:, hh * 65:(hh + 1) * 65]
                        js = slice(j * 128, (j + 1) * 128)
                        for n, (p_, i) in enumerate(((ph, 0), (ph, 1), (ph, 2), (pl, 0), (pl, 1))):
                            mo = mm(o, p_[:, q, js], V[i][:, 4 * g + hh, :], n == 0, n == 4)
                av[g % 2] = mo
                dve.wait(mo)
                ob = pair(st, 1).rearrange("p (j n) -> p j n", j=2)[:, :, 0:260].rearrange("p j (c n) -> p j c n", c=4)
                t = dve.do(lambda e, ob=ob: e.reciprocal(rc, ob[:, :, :, 64]))
                dve.wait(t)
                for j in range(2):
                    t = tt(O[:, j, 256 * g:256 * (g + 1)].rearrange("p (c n) -> p c n", c=4), ob[:, j, :, 0:64],
                           rc[:, j, :].unsqueeze(2).to_broadcast([P, 4, 64]), ALU.mult)
                st.bf[2] = st.bf[3] = t
                return t

            before = None
            for g in range(4):
                pe.wait(st.bf[0], st.bf[1])
                for hh in range(4):
                    h = 4 * g + hh
                    r = 64 * (h % 2)
                    at = (hh % 2) * 512 + (hh // 2) * 256
                    o = st.ps[0:CK, at:at + 256]
                    mm3(o, cols(KT, slice(r, r + 64), h // 2, slice(0, CK)), cols(QT, slice(r, r + 64), h // 2), True, False)
                    m = mm(o, identr[r:r + 64, r + h:r + h + 1].to_broadcast([64, CK]), nmT[r:r + 64, :], False, True)
                made = m
                if not wide:
                    yield
                    if before is not None:
                        weigh_values(*before)
                eok, lok = weights_of(st.ps[0:CK, 0:1024], ptf, pth[g % 2], ptl[g % 2], 0.125, made,
                                      (av[g % 2], before and before[1], vok), av[g % 2 if wide else (g + 1) % 2])
                st.bf[0] = st.bf[1] = eok
                if wide:
                    yield
                    if before is not None:
                        weigh_values(*before)
                before = (g, lok)
                yield
            t = weigh_values(*before)
            yield
            pe.wait(t)
            for i in range(2):
                pe.wait(st.bf[2 * i], st.bf[2 * i + 1])
                for c in range(4):
                    for j in range(2):
                        m = tp(pair(st, i)[:, c * 256 + j * 128:c * 256 + (j + 1) * 128], O[:, j, (4 * i + c) * 128:(4 * i + c + 1) * 128])
                ook = split(pair(st, i).rearrange("p (c n) -> p c n", c=4), *cols(QT, A, slice(4 * i, 4 * i + 4)), m)
                st.bf[2 * i] = st.bf[2 * i + 1] = ook
                yield
            pe.wait(ook)
            for j in range(2):
                for c in range(8):
                    m = mm3(bank(st, 0)[:, j * 256:(j + 1) * 256], cols(QT, A, c, slice(j * 128, (j + 1) * 128)), cols(wo, A, c), c == 0, c == 7)
            ended(st, pe=m, act=eok)
            yield from layernorm(st, b, bank(st, 0).rearrange("p (j n) -> p j n", j=2), 0, (m, xbias))
            yield

        def route(st, b):
            to_xT(st, b, *(v[:, :, 256 * b:256 * (b + 1)] for v in xTall), None)
            yield

        def gating(st, b):
            hi, lo = (v[:, :, 256 * b:256 * (b + 1)] for v in xTall)
            sc = st.sm[:, 32:48]
            v = st.sm[:, 48:64]
            cmp1 = st.sm[:, 80:208]
            cmp2 = st.sm[:, 208:336]
            rank = st.sm[:, 336:352]
            rw = tuple(v_[:, :].rearrange("p (c n) -> p c n", c=2) for v_ in rwr)
            rb = part(wr, PR, "rb")
            pe.wait(st.bf[1], rw_ok)
            for j in range(2):
                for k in range(2):
                    m = mm3(bank(st, 1)[:, 8 * j:8 * j + 8], tuple(v_[:, k, j * 128:(j + 1) * 128] for v_ in (hi, lo)), cols(rw, A, k), k == 0, k == 1)
            act.wait(m, st.gate)
            t = func(sc, bank(st, 1)[:, 0:16], ACT.Tanh, scale=0.5)
            st.bf[1] = t
            dve.wait(t)
            t = ts(sc, sc, 0.5, 0.5, ALU.mult, ALU.add)
            dve.wait(t)
            t = tt(v.rearrange("p (j e) -> p j e", j=2), sc.rearrange("p (j e) -> p j e", j=2),
                   rb.unsqueeze(1).to_broadcast([P, 2, 8]), ALU.add)
            dve.wait(t)
            for j in range(2):
                mine = v[:, 8 * j:8 * j + 8].unsqueeze(2).to_broadcast([P, 8, 8])
                other = v[:, 8 * j:8 * j + 8].unsqueeze(1).to_broadcast([P, 8, 8])
                c1 = cmp1[:, 64 * j:64 * j + 64].rearrange("p (e f) -> p e f", e=8)
                c2 = cmp2[:, 64 * j:64 * j + 64].rearrange("p (e f) -> p e f", e=8)
                tt(c1, other, mine, ALU.is_gt)
                t = tt(c2, other, mine, ALU.is_equal)
                dve.wait(t)
                t = tt(c2, c2, tri, ALU.mult)
            dve.wait(t)
            t = tt(cmp1, cmp1, cmp2, ALU.add)
            dve.wait(t)
            t = dve.do(lambda e: e.tensor_reduce(rank, cmp1.rearrange("p (a f) -> p a f", f=8), AX.X, ALU.add))
            dve.wait(t)
            t = stt(gates[:, 16 * b:16 * b + 16], rank, 2.0, sc, ALU.is_lt, ALU.mult)
            st.gate = t
            yield

        def fetch_unit(n):
            i, u = n % 2, UNITS[n]
            sp.wait(u_split[i])
            dma(raw[:, UW * i:UW * (i + 1)], wu_in[:, UW * u:UW * (u + 1)], d_u[i])
            loaded(pool, d_u[i], 16 * (n // 2 + 1))
            loaded(act, d_u[i], 16 * (n // 2 + 1))
            for lane in (act, pool):
                lane.wait(*u_read[i])
            h = copy(uw[i][0][:, :], raw[:, UW * i:UW * (i + 1)])
            pool.wait(h)
            u_split[i] = tt(uw[i][1][:, :], raw[:, UW * i:UW * (i + 1)], uw[i][0][:, :].bitcast(F32), ALU.subtract, pool)
            u_ok[n] = u_split[i]

        u_split = [None, None]
        u_read = [[], []]
        u_ok = {}

        def moe(st):
            hf = st.m[:, 0:1024]
            hr = tuple(st.r[:, 1024 * i:1024 * (i + 1)] for i in range(2))
            prev = None
            mdown = None
            turn_ = 0
            for n_, u in enumerate(UNITS):
                w = uw[n_ % 2]
                up = tuple(v[:, 0:1024].rearrange("p (k n) -> p k n", k=2) for v in w)
                dn = tuple(v[:, 1024:1536].rearrange("p (k n) -> p k n", k=2) for v in w)
                for n, half in enumerate((st.i, st.i + 2)):
                    if prev is not None:
                        mdown = down(st, *prev)
                    if st.i == 1 and n == 0 and 0 < n_ < NU - 1:
                        fetch_unit(n_ + 1)
                    a, b_ = (0, 1) if turn_ % 2 == 0 else (1, 0)
                    turn_ += 1
                    pe.wait(u_ok[n_])
                    for c in range(4):
                        pr = a if c < 2 else b_
                        if c % 2 == 0:
                            pe.wait(st.bf[2 * pr], st.bf[2 * pr + 1])
                        for k in range(2):
                            m = mm3(bank(st, 2 * pr + c % 2), cols(up, A, k, slice(128 * c, 128 * (c + 1))),
                                    tuple(v[:, k, 512 * half:512 * (half + 1)] for v in xTall), k == 0, k == 1)
                        if c == 1:
                            act.wait(m, st.h_rd)
                            sok = func(hf, pair(st, a), ACT.Silu)
                            st.bf[2 * a] = st.bf[2 * a + 1] = sok
                    dve.wait(m, sok)
                    hok = tt(hf, hf, pair(st, b_), ALU.mult)
                    st.bf[2 * b_] = st.bf[2 * b_ + 1] = hok
                    act.wait(hok, mdown)
                    hh = copy(hr[0], hf)
                    pool.wait(hh, mdown)
                    st.h_rd = lok = tt(hr[1], hf, hr[0].bitcast(F32), ALU.subtract, pool)
                    prev = (n_, half, lok, a, dn, hr)
                    yield
            mdown = down(st, *prev)
            ended(st, pe=mdown, act=hh, dve=st.acc, pool=lok)
            yield

        def down(st, n_, half, hok, pr, dn, hr):
            h = tuple(v.rearrange("p (k n) -> p k n", k=2) for v in hr)
            pe.wait(hok, st.bf[2 * pr], st.bf[2 * pr + 1])
            for t in range(4):
                for k in range(2):
                    m = mm3(pair(st, pr)[:, 256 * t:256 * (t + 1)], cols(h, A, k, slice(128 * t, 128 * (t + 1))), cols(dn, A, k), k == 0, k == 1)
            if half == st.i + 2:
                u_read[n_ % 2] = ([] if st.i == 0 else u_read[n_ % 2]) + [m]
            u = UNITS[n_]
            dve.wait(m, st.acc)
            if u < NE:
                dve.wait(*[s.gate for s in streams])
            for t in range(4):
                tile = 4 * half + t
                xs = x[:, tile, :]
                y = pair(st, pr)[:, 256 * t:256 * (t + 1)]
                if u < NE:
                    r = stt(xs, y, gates[:, 8 * tile + u:8 * tile + u + 1], xs, ALU.mult, ALU.add)
                else:
                    r = tt(xs, y, xs, ALU.add)
                x_ok[tile] = r
            st.bf[2 * pr] = st.bf[2 * pr + 1] = st.acc = r
            return m

        def norm_only(st, b):
            yield from layernorm(st, b)
            yield

        def heads(st):
            m, r = st.m, st.r
            qp = m[:, 0:2048].rearrange("p (j h n) -> p j h n", j=2, h=16)
            kp = m[:, 2048:4096].rearrange("p (j h n) -> p j h n", j=2, h=16)
            va = m[:, 4096:4912].bitcast(BF16).rearrange("p (k h i n) -> p k h i n", k=2, h=16, i=3)
            qT = r[:, 1024:3072].rearrange("p (c n) -> p c n", c=8)
            kT = r[:, 3072:5120].rearrange("p (c n) -> p c n", c=8)
            oT = tuple(r[:, 1024 + 512 * i:1536 + 512 * i].rearrange("p (c n) -> p c n", c=2) for i in range(2))
            return qp, kp, qT, kT, oT, va

        def in_place(qp, kp):
            pt = []
            for i in range(2):
                q, k = (v[:, :, 8 * i:8 * i + 8, :].rearrange("p j h n -> p j (h n)") for v in (qp, kp))
                pt.append((k, q[:, 0, :].bitcast(F16), q[:, 1, :].bitcast(F16)))
            return pt

        def stack(q, qp, kp, j, ready):
            act.wait(ready)
            qh = qp[:, j, :, 0:32].rearrange("p h (a n) -> p h a n", a=2).bitcast(F32R)
            h1 = copy(qh, q[:, 0:16, :].unsqueeze(2).to_broadcast([P, 16, 2, 16]))
            kh = kp[:, j, :, 0:64].rearrange("p h (a n) -> p h a n", a=2)[:, :, :, 0:16].bitcast(F32R)
            h2 = copy(kh, q[:, 16:32, :].unsqueeze(2).to_broadcast([P, 16, 2, 16]))
            dve.wait(h1, h2)
            tt(qp[:, j, :, 32:48].bitcast(F32R), q[:, 0:16, :], qp[:, j, :, 0:16], ALU.subtract)
            return tt(kp[:, j, :, 16:32].bitcast(F32R), q[:, 16:32, :], kp[:, j, :, 0:16], ALU.subtract)

        def clear(st, qp, kp, va):
            pool.wait(st.last["pool"])
            mset(pool, qp[:, :, :, 48:64], 0.0)
            mset(pool, kp[:, :, :, 48:64], 0.0)
            mset(pool, va[:, :, :, 1:3, 16:17], 0.0)
            z = mset(pool, va[:, :, :, 0:1, 16:17], 1.0)
            pool.wait(z)
            return mset(pool, kp[:, :, :, 48:49], 1.0)

        class Half:
            pass

        def half_of(st, i, qp, kp, qT, kT, va, o, pt):
            hv = Half()
            hv.i, hv.va, hv.o = i, va[:, :, 8 * i:8 * i + 8, :, :], o[:, :, 128 * i:128 * i + 128]
            hv.qp, hv.kp = (v[:, :, 8 * i:8 * i + 8, :] for v in (qp, kp))
            hv.qT, hv.kT = (v[:, 4 * i:4 * i + 4, :] for v in (qT, kT))
            hv.pf, hv.ph, hv.pl = pt[i]
            hv.before = (None, None)
            hv.s3 = st.sm[:, 64 + 80 * i:132 + 80 * i].rearrange("p (j a n) -> p j a n", j=2, a=2)
            hv.rc = st.sm[:, 224 + 4 * i:228 + 4 * i].rearrange("p (j a) -> p j a", j=2)
            return hv

        def turn(st, hv, s, d):
            i = hv.i
            pe.wait(st.bf[2 * i], st.bf[2 * i + 1])
            for c in range(4):
                for j in range(2):
                    hv.turned = tp(pair(st, i)[:, c * 256 + j * 128:c * 256 + (j + 1) * 128],
                                   s[:, j, 2 * c:2 * c + 2, :].rearrange("p h n -> p (h n)"))
            act.wait(hv.turned)
            hv.T_ok = copy(d.rearrange("p c n -> p (c n)"), pair(st, i))
            st.bf[2 * i] = st.bf[2 * i + 1] = hv.T_ok

        def maxima(st, hv, K):
            i, qT, kT = hv.i, hv.qT, hv.kT
            pe.wait(hv.T_ok)
            dve.wait(hv.turned)
            for j in range(2):
                for g in range(2):
                    pe.wait(st.bf[2 * i], st.bf[2 * i + 1])
                    for a in range(2):
                        r = 64 * a
                        for c in range(2):
                            m = mm(bank(st, 2 * i + a)[:, c * 256:(c + 1) * 256], qT[r:r + K, 2 * g + c, j * 128:(j + 1) * 128],
                                   kT[r:r + K, 2 * g + c, :], True, True)
                    dve.wait(m)
                    t = dve.do(lambda e, j=j, g=g: e.tensor_reduce(
                        hv.qp[:, j, 4 * g:4 * g + 4, 48].rearrange("p (c a) -> p a c", a=2),
                        pair(st, i).rearrange("p (a c n) -> p a c n", a=2, c=2), AX.X, ALU.max, negate=True))
                    st.bf[2 * i] = st.bf[2 * i + 1] = t
                    yield
            pe.wait(t)
            act.wait(m)
            turn(st, hv, hv.qp, qT)
            yield

        def weigh(st, hv, K, scale, vok):
            i, qT, kT = hv.i, hv.qT, hv.kT
            pe.wait(hv.T_ok)
            mo, lok = hv.before
            for g in range(4):
                pe.wait(st.bf[2 * i], st.bf[2 * i + 1])
                for a in range(2):
                    r = 64 * a
                    for k in range(2):
                        m = mm(pair(st, i)[:, (2 * a + k) * 256:(2 * a + k + 1) * 256], kT[r:r + K, g, k * 128:(k + 1) * 128],
                               qT[r:r + K, g, :], True, True)
                wide = [v.rearrange("p (a n) -> p a n", a=2) for v in (pair(st, i), hv.ph, hv.pl)]
                eok, lok = weights_of(wide[0], hv.pf, wide[1], wide[2], scale, m, (mo, lok, hv.turned))
                st.bf[2 * i] = st.bf[2 * i + 1] = eok
                yield
                hi, lo = (v.rearrange("p (a k n) -> p a k n", a=2, k=2) for v in (hv.ph, hv.pl))
                pe.wait(lok, vok, st.bf[2 * i])
                for a in range(2):
                    for j in range(2):
                        js = slice(j * 128, (j + 1) * 128)
                        ov = bank(st, 2 * i)[:, 51 * (2 * j + a):51 * (2 * j + a) + 51]
                        for k in range(2):
                            vv = hv.va[:, k, 2 * g + a, :, :].rearrange("p i n -> p (i n)")
                            mm(ov, hi[:, a, k, js], vv, k == 0, False)
                            mo = mm(ov[:, 0:34], lo[:, a, k, js], vv[:, 0:34], False, k == 1)
                dve.wait(mo)
                ob = bank(st, 2 * i)[:, 0:204].rearrange("p (q i n) -> p q n i", q=4, i=3)
                t = dve.do(lambda e, ob=ob: e.tensor_reduce(hv.s3.rearrange("p j a n -> p (j a) n"), ob, AX.X, ALU.add))
                st.bf[2 * i] = t
                dve.wait(t)
                t = dve.do(lambda e: e.reciprocal(hv.rc, hv.s3[:, :, :, 16]))
                dve.wait(t)
                hv.ook = tt(hv.o[:, :, 32 * g:32 * g + 32].rearrange("p j (a n) -> p j a n", a=2), hv.s3[:, :, :, 0:16],
                            hv.rc.unsqueeze(3).to_broadcast([P, 2, 2, 16]), ALU.mult)
                yield
            hv.exp, hv.after = eok, (mo, lok)

        def beside(gens):
            while gens:
                for g in list(gens):
                    try:
                        next(g)
                        yield
                    except StopIteration:
                        gens.remove(g)

        def project(st, b, o, oT, w, ook, exps, xbias, final=False):
            pe.wait(*ook, st.bf[0], st.bf[1])
            for c in range(2):
                for j in range(2):
                    m = tp(bank(st, 0)[:, c * 256 + j * 128:c * 256 + (j + 1) * 128], o[:, j, c * 128:(c + 1) * 128])
            t = split(bank(st, 0).rearrange("p (c n) -> p c n", c=2), *oT, m)
            st.bf[0] = t
            yield
            pe.wait(t)
            for j in range(2):
                for c in range(2):
                    m = mm3(bank(st, 1)[:, j * 256:(j + 1) * 256], cols(oT, A, c, slice(j * 128, (j + 1) * 128)), cols(w, A, c), c == 0, c == 1)
            ended(st, pe=m, act=max(exps, key=lambda t: t.index))
            yield from layernorm(st, b, bank(st, 1).rearrange("p (j n) -> p j n", j=2), 1, (m, xbias), final)

        def qkv_mm(st, w):
            pe.wait(st.xT_ok)
            for j in range(2):
                pe.wait(st.bf[2 + j])
                for k in range(2):
                    m = mm3(bank(st, 2 + j), cols(st.xT, A, k, slice(j * 128, (j + 1) * 128)), cols(w, A, k, slice(0, 512)), k == 0, k == 1)
            pe.wait(st.bf[1])
            for j in range(2):
                for k in range(2):
                    m = mm3(bank(st, 1)[:, j * 256:(j + 1) * 256], cols(st.xT, A, k, slice(j * 128, (j + 1) * 128)), cols(w, A, k, slice(512, 768)), k == 0, k == 1)
            return m

        def l1_attn(st, b):
            fence(st)
            qp, kp, qT, kT, oT, va = heads(st)
            o = st.m[:, 4912:5424].rearrange("p (j n) -> p j n", j=2)
            t1 = st.m[:, 4912:5424].rearrange("p (h n) -> p h n", h=32)
            t2 = st.m[:, 5424:5936].rearrange("p (h n) -> p h n", h=32)
            z = clear(st, qp, kp, va)
            own_xT(st, b)
            xbias = add_bias(st, b, part(w1f, P1F, "bao"))
            m = qkv_mm(st, pair_of(w1, P1, "wqkv", 2))
            vf = st.m[:, 5936:6448].rearrange("p (k h n) -> p k h n", k=2, h=16)
            vread, vok = thirds([va[:, :, :, i, :] for i in range(3)], bank(st, 1).rearrange("p (k h n) -> p k h n", k=2, h=16), vf, m, z)
            st.bf[1] = vread
            yield
            dve.wait(m, z)
            tl = None
            for j in range(2):
                qk = bank(st, 2 + j).rearrange("p (h n) -> p h n", h=32)
                dve.wait(tl)
                tt(t1, qk, ropec[:, j, :].unsqueeze(1).to_broadcast([P, 32, 16]), ALU.mult)
                tt(t2[:, :, 0:8], qk[:, :, 8:16], ropes[:, j, 0:8].unsqueeze(1).to_broadcast([P, 32, 8]), ALU.mult)
                a = tt(t2[:, :, 8:16], qk[:, :, 0:8], ropes[:, j, 8:16].unsqueeze(1).to_broadcast([P, 32, 8]), ALU.mult)
                st.bf[2 + j] = a
                dve.wait(a)
                a = tt(t1, t1, t2, ALU.add)
                tl = stack(t1, qp, kp, j, a)
            pe.wait(tl, z)
            halves = [half_of(st, i, qp, kp, qT, kT, va, o, in_place(qp, kp)) for i in range(2)]
            for hv in halves:
                turn(st, hv, hv.qp, hv.qT)
            yield
            for hv in halves:
                turn(st, hv, hv.kp, hv.kT)
            yield
            yield from beside([chain(maxima(st, hv, 49), weigh(st, hv, 49, 0.25, vok)) for hv in halves])
            yield from project(st, b, o, oT, pair_of(w1, P1, "wao", 2), [hv.ook for hv in halves], [hv.exp for hv in halves], xbias)
            yield

        sim = small[:, 0:16]
        gg = small[:, 16:32]
        pos = small[:, 32:48]
        qf = small[:, 48:80].rearrange("p (t n) -> p t n", n=2)
        kf = small[:, 80:112].rearrange("p (t n) -> p t n", n=2)
        qxf = small[:, 112:144].rearrange("p (t n) -> p t n", n=2)
        ext = small[:, 144:146]
        ext2 = small[:, 146:148]
        den = small[:, 148:149]
        tmp16 = small[:, 149:165]
        tmpb = small[:, 165:181]
        gsq = small[:, 192:448]
        g_ok = []
        sim_ok = []
        kept = []

        def guide():
            g = part(w1f, P1F, "g")
            t = tt(gsq, g, g, ALU.mult)
            dve.wait(t)
            g_ok.append(dve.do(lambda e: e.tensor_reduce(gg, gsq.rearrange("p (h n) -> p h n", h=16), AX.X, ALU.add)))

        def ffn_qkv(st, b):
            fence(st)
            g = part(w1f, P1F, "g")
            qkv = st.m[:, 1024:2560].rearrange("p (j n) -> p j n", j=2)
            sq = st.m[:, 0:512].rearrange("p (j n) -> p j n", j=2)
            qg = st.m[:, 512:1024].rearrange("p (j n) -> p j n", j=2)
            qq = st.sm[:, 32:64].rearrange("p (j n) -> p j n", j=2)
            dq = st.sm[:, 64:96].rearrange("p (j n) -> p j n", j=2)
            own_xT(st, b)
            add = add_bias(st, b, part(w1f, P1F, "fb"))
            x_ok[2 * b] = x_ok[2 * b + 1] = add
            m = qkv_mm(st, pair_of(w1, P1, "fqkv", 2))
            act.wait(m)
            for j in range(2):
                c1 = copy(qkv[:, j, 0:512], bank(st, 2 + j))
                st.bf[2 + j] = c1
            c2 = copy(qkv[:, :, 512:768], bank(st, 1).rearrange("p (j n) -> p j n", j=2))
            st.bf[1] = c2
            sp.wait(c2)
            dma(keep[b], st.m[:, 1024:2560], d_kp[st.i])
            kept.append(b)
            yield
            dve.wait(c1)
            qv = qkv[:, :, 0:256]
            tt(sq, qv, qv, ALU.mult)
            t = tt(qg, qv, g.unsqueeze(1).to_broadcast([P, 2, 256]), ALU.mult)
            dve.wait(t)
            dve.do(lambda e: e.tensor_reduce(qq, sq.rearrange("p j (h n) -> p j h n", h=16), AX.X, ALU.add))
            t = dve.do(lambda e: e.tensor_reduce(dq, qg.rearrange("p j (h n) -> p j h n", h=16), AX.X, ALU.add))
            dve.wait(t, g_ok[0])
            t = tt(qq, qq, gg.unsqueeze(1).to_broadcast([P, 2, 16]), ALU.mult)
            pool.wait(t)
            p = tt(qq, qq, mhalf.rearrange("p (j n) -> p j n", j=2), ALU.pow, pool)
            dve.wait(p)
            t = tt(dq, dq, qq, ALU.mult)
            dve.wait(t)
            t = dve.do(lambda e: e.tensor_reduce(sim[:, 2 * b:2 * b + 2], dq, AX.X, ALU.add))
            sim_ok.append(t)
            ended(st, pe=m, act=c2, dve=t, pool=p)
            yield

        def stored(st, b):
            for lane in (act, dve, pool):
                loaded(lane, d_kp[st.i], 16 * (b // 2 + 1))
            return
            yield

        def choose():
            dve.wait(*sim_ok)
            t = ts(sim, sim, 1.0 / 16.0, None, ALU.mult)
            dve.wait(t)
            t = tt(tmp16, sim, vm, ALU.mult)
            dve.wait(t)
            t = stt(tmpb, vmi, -BIG, tmp16, ALU.mult, ALU.add)
            t2 = stt(tmp16, vmi, BIG, tmp16, ALU.mult, ALU.add)
            dve.wait(t, t2)
            dve.do(lambda e: e.tensor_reduce(ext[:, 0:1], tmpb, AX.X, ALU.max))
            t = dve.do(lambda e: e.tensor_reduce(ext[:, 1:2], tmp16, AX.X, ALU.min, negate=True))
            pool.wait(t)
            t = pool.do(lambda e: e.partition_all_reduce(ext2, ext, P, RMAX))
            dve.wait(t)
            t = tt(den, ext2[:, 0:1], ext2[:, 1:2], ALU.add)
            t2 = ts(tmp16, sim, ext2[:, 1:2], None, ALU.add)
            dve.wait(t, t2)
            t = ts(den, den, 0.9, None, ALU.mult)
            dve.wait(t)
            t = ts(pos, tmp16, den, None, ALU.is_gt)
            dve.wait(t)
            t = tt(pos, pos, vm, ALU.mult)
            dve.wait(t)
            tt(kf[:, :, 0], vm, pos, ALU.subtract)
            dve.do(lambda e: e.tensor_copy(kf[:, :, 1], pos))
            t = tt(tmpb, pos, vmi, ALU.add)
            dve.wait(t)
            ts(qf[:, :, 0], tmpb, -BIG, None, ALU.mult)
            t = ts(qf[:, :, 1], tmpb, BIG, -BIG, ALU.mult, ALU.add)
            dve.wait(t)
            dve.do(lambda e: e.tensor_copy(qxf[:, :, 0], qf[:, :, 1]))
            t = dve.do(lambda e: e.tensor_copy(qxf[:, :, 1], qf[:, :, 0]))
            sim_ok.append(t)

        def lay4(st):
            m, r = st.m, st.r
            st.qp = m[:, 0:2048].rearrange("p (j h n) -> p j h n", j=2, h=16)
            st.kp = m[:, 2048:4096].rearrange("p (j h n) -> p j h n", j=2, h=16)
            st.va = [m[:, a:a + 816].bitcast(BF16).rearrange("p (k h i n) -> p k h i n", k=2, h=16, i=3) for a in (4096, 4912)]
            st.qx = m[0:32, 5728:6752].rearrange("p (h n) -> p h n", h=16)
            st.raw = m[:, 6752:8288]
            st.px = m[:, 8288:8544], m[:, 8544:8672].bitcast(F16), m[:, 8672:8800].bitcast(F16)
            st.sx = m[0:8, 8800:9072].rearrange("p (h n) -> p h n", h=16)
            st.o = m[:, 9072:9584].rearrange("p (j n) -> p j n", j=2)
            st.pt = []
            for a in (9584, 11632):
                st.pt.append((m[:, a:a + 1024].rearrange("p (a n) -> p a n", a=2), m[:, a + 1024:a + 1536].bitcast(F16), m[:, a + 1536:a + 2048].bitcast(F16)))
            st.bd = r[:, 0:240]
            st.sets = []
            for a in (240, 4336):
                st.sets.append((r[:, a:a + 2048].rearrange("p (c n) -> p c n", c=8), r[:, a + 2048:a + 4096].rearrange("p (c n) -> p c n", c=8),
                                tuple(r[:, a + 512 * i:a + 512 * (i + 1)].rearrange("p (c n) -> p c n", c=2) for i in range(2))))
            st.before, st.reg_pe, st.qx_rd = [(None, None)] * 2, None, None
            pool.wait(mset(pool, st.qp[:, :, :, 48:64], 0.0), mset(pool, st.kp[:, :, :, 48:64], 0.0))
            for v in st.va:
                mset(pool, v[:, :, :, 1:3, 16:17], 0.0)
                mset(pool, v[:, :, :, 0:1, 16:17], 1.0)
            st.clean = mset(pool, st.kp[:, :, :, 48:49], 1.0)
            act.do(lambda e: e.activation(st.bd[:, 0:128], ident, ACT.Copy, scale=0.0))
            st.bd0 = act.do(lambda e: e.activation(st.bd[:, 128:240], ident[:, 0:112], ACT.Copy, scale=0.0))
            dma(st.raw, keep[st.i], d_raw[st.i])

        def front(st, b):
            n = b // 2 % 2
            qp, kp, qx, va = st.qp, st.kp, st.qx, st.va[n]
            qT, kT, oT = st.sets[n]
            raw_ = st.raw.rearrange("p (j n) -> p j n", j=2)
            for lane in (act, dve):
                loaded(lane, d_raw[st.i], 16 * (b // 2 + 1))
                lane.wait(st.clean, st.qx_rd, st.last["pe"])
            z = mset(dve, qp[:, :, :, 48:49], 0.0)
            for j in range(2):
                tl = stack(raw_[:, j, 0:512].rearrange("p (h n) -> p h n", h=32), qp, kp, j, None)
            dve.wait(z, sim_ok[-1])
            for j in range(2):
                dve.do(lambda e, j=j: e.tensor_copy(qp[:, j, :, 49:51], qf[:, 2 * b + j, :].unsqueeze(1).to_broadcast([P, 16, 2])))
                t = dve.do(lambda e, j=j: e.tensor_copy(kp[:, j, :, 49:51], kf[:, 2 * b + j, :].unsqueeze(1).to_broadcast([P, 16, 2])))
            dve.wait(t, tl)
            t = dve.do(lambda e: e.tensor_copy(qx, qp[0:32, 0, :, :]))
            dve.wait(t)
            xq = dve.do(lambda e: e.tensor_copy(qx[:, :, 49:51], qxf[0:32, 2 * b, :].unsqueeze(1).to_broadcast([32, 16, 2])))
            yield
            pe.wait(xq)
            halves = [half_of(st, i, qp, kp, qT, kT, va, st.o, st.pt) for i in range(2)]
            for hv in halves:
                turn(st, hv, hv.kp, hv.kT)
                yield
            vraw = raw_[:, :, 512:768].rearrange("p j (h n) -> p j h n", h=16)
            vread, vok = thirds([va[:, :, :, i, :] for i in range(3)], vraw, vraw, tl, st.clean)
            if b + 2 < B:
                sp.wait(tl, vok)
                dma(st.raw, keep[b + 2], d_raw[st.i])
            for hv in halves:
                turn(st, hv, hv.qp, hv.qT)
                yield
            st.front = halves, vok

        def ffn_attn(st, b):
            if b < 2:
                yield from front(st, b)
            halves, vok = st.front
            qx, o, sx = st.qx, st.o, st.sx
            qT, kT, oT = st.sets[b // 2 % 2]
            va = st.va[b // 2 % 2]
            pxf, pxh, pxl = st.px
            ox = pxf[0:8, :].rearrange("p (h n) -> p h n", h=16)
            rx = st.sm[0:8, 240:256]
            nx = st.sm[0:16, 256:264]
            bd = st.bd[:, 0:128].rearrange("p (c n) -> p c n", c=8)
            dgx = st.sx_diag

            def register_maxima():
                pe.wait(st.bf[0], st.bf[1])
                for c in range(8):
                    m = tp(bank(st, 0)[:, 32 * c:32 * c + 32], qx[:, 2 * c:2 * c + 2, :].rearrange("p h n -> p (h n)"), 32)
                st.qx_rd = m
                act.wait(m, st.bd0, st.reg_pe)
                src = bank(st, 0)[:, 0:256].rearrange("p (c n) -> p c n", c=8)
                for a in range(2):
                    t = copy(bd[64 * a:64 * a + 64, :, 8 * a:8 * a + 8], src[64 * a:64 * a + 64, :, 0:8])
                st.bf[0] = st.bf[1] = t
                pe.wait(t)
                yield
                for i in range(2):
                    pe.wait(st.bf[2 * i], st.bf[2 * i + 1])
                    for c in range(4):
                        cc = 4 * i + c
                        m = mm(pair(st, i)[:, 256 * c:256 * (c + 1)], st.bd[:, 16 * cc:16 * cc + 128], kT[:, cc, :], True, True)
                    dve.wait(m)
                    t = dve.do(lambda e, i=i: e.tensor_reduce(nx[:, 4 * i:4 * i + 4], pair(st, i)[0:16, :].rearrange("p (c n) -> p c n", c=4),
                                                              AX.X, ALU.max, negate=True))
                    st.bf[2 * i] = st.bf[2 * i + 1] = t
                    yield
                dve.wait(t, st.reg_pe)
                st.dg_ok = dve.do(lambda e: e.tensor_tensor(
                    dgx.rearrange("p (c n) -> p c n", c=8), ident[0:16, 0:16].unsqueeze(1).to_broadcast([16, 8, 16]),
                    nx.unsqueeze(2).to_broadcast([16, 8, 16]), ALU.mult))
                yield

            def registers():
                pe.wait(st.bf[0], st.dg_ok)
                s_ = bank(st, 0)[:, 0:256]
                for k in range(2):
                    mm(s_[:, 128 * k:128 * (k + 1)], onesr[0:16, :], dgx, True, False)
                    for c in range(8):
                        m = mm(s_[:, 128 * k + 16 * c:128 * k + 16 * c + 16], kT[:, c, k * 128:(k + 1) * 128], bd[:, c, :], False, c == 7)
                e_, t = weights_of(s_, pxf, pxh, pxl, 0.25, m, (st.reg_pe, st.ox_rd))
                st.reg_exp = e_
                st.bf[0] = e_
                xh, xl = (v.rearrange("p (k c a n) -> p c k a n", c=8, k=2, a=2) for v in (pxh, pxl))
                yield
                pe.wait(t, vok, st.bf[2], st.bf[3])
                for half in range(2):
                    for h in range(8 * half, 8 * half + 8):
                        ov = bank(st, 2 + half)[0:8, 51 * (h % 8):51 * (h % 8) + 51]
                        for k in range(2):
                            vv = va[:, k, h, :, :].rearrange("p i n -> p (i n)")
                            mm(ov, xh[:, h // 2, k, h % 2, :], vv, k == 0, False)
                            m = mm(ov[:, 0:34], xl[:, h // 2, k, h % 2, :], vv[:, 0:34], False, k == 1)
                st.reg_pe = m
                dve.wait(m)
                for half in range(2):
                    ob = bank(st, 2 + half)[0:8, 0:408].rearrange("p (h i n) -> p h n i", h=8, i=3)
                    t = dve.do(lambda e, ob=ob, half=half: e.tensor_reduce(sx[:, 8 * half:8 * half + 8, :], ob, AX.X, ALU.add))
                st.bf[2] = st.bf[3] = t
                dve.wait(t)
                t = dve.do(lambda e: e.reciprocal(rx, sx[:, :, 16]))
                dve.wait(t)
                st.ox_ok = tt(ox, sx[:, :, 0:16], rx.unsqueeze(2).to_broadcast([8, 16, 16]), ALU.mult)
                yield

            dve.wait(st.last["pe"])
            for hv in halves:
                hv.before = st.before[hv.i]
            yield from beside([maxima(st, hv, 51) for hv in halves] + [register_maxima()])
            yield from beside([weigh(st, hv, 51, 0.25, vok) for hv in halves] + [registers()] + ([front(st, b + 2)] if b + 2 < B else []))
            st.before = [hv.after for hv in halves]
            ooks = [hv.ook for hv in halves]
            dve.wait(st.ox_ok, *ooks)
            ov = o[0:REG, 0, :].rearrange("p (h n) -> p h n", h=16)
            t = st.ox_rd = tt(ov, ov, ox[0:REG, :, :], ALU.add)
            dve.wait(t)
            ook = ts(o[0:REG, 0, :], o[0:REG, 0, :], 0.5, None, ALU.mult)
            yield
            yield from project(st, b, o, oT, pair_of(wp, {"fproj": (0, 512)}, "fproj", 2), ooks + [ook], [hv.exp for hv in halves] + [st.reg_exp], x_ok[2 * b], True)
            yield

        def together(work):
            for _ in beside(list(work)):
                pass

        def each(st, *fs):
            for b in st.batches:
                for f in fs:
                    yield from f(st, b)

        def weights(name, n, scope):
            with ExitStack() as first:
                raw_ = sb(name + "raw", n, F32, first)
            lo = sb(name + "l", n, F32R, scope)
            return (sb(name + "h", n, F32R, scope), lo), raw_

        def split_weights(w, raw_, a, n, s, v=16, lane=None):
            lane = lane or pool
            hi, lo, f = w[0][:, a:a + n], w[1][:, a:a + n], raw_[:, a:a + n]
            loaded(act, s, v)
            h = copy(hi, f)
            loaded(lane, s, v)
            lane.wait(h)
            return tt(lo, f, hi.bitcast(F32), ALU.subtract, lane)

        ph1 = ExitStack()
        w0, w0_raw = weights("w0", N0, ph1)
        w0f = sb("w0f", N0F, F32, ph1)
        work(ph1, "1", 6168, 5744)
        dma(cst[:, :], const_in, d_cst)
        dma(xres[:, 0:4 * D], x_in[:, 0:4 * D], d_x[0])

        def load0(name):
            a, n = P0[name]
            dma(w0_raw[:, a:a + n], w0_in[:, a:a + n], d_w0[name])

        load0("win")
        dma(w0f[:, 0:280], w0f_in[:, 0:280], d_w0f)
        load0("wxp")
        load0("wout")
        dma(xres[:, 4 * D:], x_in[:, 4 * D:], d_x[1])
        dma(ctxT[:, :], ctx_in, d_ctx)
        dma(w0f[:, 280:], w0f_in[:, 280:], d_kv)
        load0("wq")
        load0("wo")
        for lane in (pe, act, dve, pool):
            loaded(lane, d_cst)
        pe.wait(copy(identr, ident))
        w0_ok = {n: split_weights(w0, w0_raw, *P0[n], d_w0[n], lane=dve if n == "win" else pool) for n in ("win", "wxp", "wout")}

        def rest(lanes):
            for lane in lanes:
                for s in (d_ctx, d_kv):
                    loaded(lane, s)
            for n in ("wq", "wo"):
                w0_ok[n] = split_weights(w0, w0_raw, *P0[n], d_w0[n])

        together([each(st, l0_attn, lambda st, b: xattn(st, b, w0, P0, w0f, P0F, (w0_ok["wq"], w0_ok["wo"]), False)) for st in streams])
        ph1.close()

        wp, wp_raw = weights("wp", NP, es)
        phw = ExitStack()
        w1, w1_raw = weights("w1", N1, phw)
        w1f = sb("w1f", N1F, F32, phw)
        ph2 = ExitStack()
        work(ph2, "2", 1024, 2048)
        xTall = tuple(sb(f"xTall{i}", 4096, F32R, ph2)[:, :].rearrange("p (k n) -> p k n", k=2) for i in range(2))
        gates = sb("gates", 128, F32, ph2)
        raw = sb("raw", 2 * UW, F32, ph2)
        uw = [tuple(sb(f"uw{i}{j}", UW, F32R, ph2) for j in range(2)) for i in range(2)]
        wr = sb("wr", NR, F32, ph2)
        rwr = tuple(sb(f"rwr{j}", 16, F32R, ph2) for j in range(2))
        ended1 = over()
        for lane in (pe, act, dve, pool, sp):
            lane.wait(*ended1)
        dma(wr[:, :], wr_in, d_wr)
        loaded(act, d_wr)
        loaded(dve, d_wr)
        h = copy(rwr[0][:, :], part(wr, PR, "rw"))
        dve.wait(h)
        rw_ok = tt(rwr[1][:, :], part(wr, PR, "rw"), rwr[0][:, :].bitcast(F32), ALU.subtract)
        fetch_unit(0)
        fetch_unit(1)
        dma(w1_raw[:, :], w1_in[:, 0:N1], d_w1)
        dma(wp_raw[:, :], w1_in[:, N1:N1 + NP], d_wp)
        dma(w1f[:, :], w1f_in, d_w1f)
        together([each(st, route) for st in streams])
        for st in streams:
            st.h_rd = st.acc = st.gate = None
            pe.wait(*[s.xT_ok for s in streams])

        def weights1():
            yield
            yield
            for a in range(0, N1, 960):
                split_weights(w1, w1_raw, a, 960, d_w1)
                yield
                yield
            w1_ok.append(split_weights(wp, wp_raw, 0, NP, d_wp))
            yield

        w1_ok = []
        together([moe(streams[0]), moe(streams[1]), weights1()] + [each(st, gating) for st in streams])
        for st in streams:
            ended(st, dve=st.acc)
        together([each(st, norm_only) for st in streams])
        ph2.close()

        ph3 = ExitStack()
        work(ph3, "3", 6680, 5744)
        ended2 = over()
        for lane in (pe, act, dve, pool, sp):
            lane.wait(*ended2, *w1_ok)
        for lane in (pe, act, dve, pool):
            loaded(lane, d_w1f)
        d_kp = [sem(f"d_kp{i}") for i in range(2)]
        guide()
        together([each(st, l1_attn, lambda st, b: xattn(st, b, w1, P1, w1f, P1F, (), True), ffn_qkv, stored) for st in streams])
        ph3.close()
        phw.close()

        ph4 = ExitStack()
        work(ph4, "4", 13680, 8432)
        onesr_t = sb("onesr", P, F32R, ph4)
        onesr = onesr_t[:, :]
        for st in streams:
            st.sx_diag_t = sb(f"diag{st.i}", 128, F32R, ph4)
            st.sx_diag, st.ox_rd = st.sx_diag_t[0:16, :], None
        ended3 = over()
        for lane in (pe, act, dve, pool, sp):
            lane.wait(*ended3, *sim_ok)
            for st in streams:
                loaded(lane, d_kp[st.i], 16 * 4)
        for st in streams:
            lay4(st)
        pe.wait(copy(onesr, ones))
        choose()
        together([each(st, ffn_attn) for st in streams])
        for n, (tile, t) in enumerate(outs):
            sp.wait(t)
            dma(out[tile * P:(tile + 1) * P, :], x[:, tile, :], d_out)
        loaded(sp, d_out, 16 * len(outs))
        ph4.close()

        for lane in (pe, act, dve, pool, sp):
            lane.count()

        block = es.enter_context(nc.Block())

        @block.sync
        def _(eng):
            sp.emit(eng)

        @block.tensor
        def _(eng):
            pe.emit(eng)

        @block.scalar
        def _(eng):
            act.emit(eng)

        @block.vector
        def _(eng):
            dve.emit(eng)

        @block.gpsimd
        def _(eng):
            pool.emit(eng)


def consts():
    c = np.zeros((P, NC_), np.float32)

    def put(name, v):
        a, n = PC[name]
        c[:, a:a + n] = v

    put("ident", np.eye(P, dtype=np.float32))
    put("ones", 1.0)
    inv = (1.0 / np.float32(10000.0) ** (np.arange(0, 16, 2, dtype=np.float32) / np.float32(16))).astype(np.float32)
    ang = np.arange(S, dtype=np.float32)[:, None] * inv[None, :]
    cos, sin = np.cos(ang).astype(np.float32), np.sin(ang).astype(np.float32)
    put("ropec", np.concatenate([cos, cos], 1).reshape(2, P, 16).transpose(1, 0, 2).reshape(P, 32))
    put("ropes", np.concatenate([-sin, sin], 1).reshape(2, P, 16).transpose(1, 0, 2).reshape(P, 32))
    put("tri", np.tril(np.ones((8, 8), np.float32), -1).reshape(1, 64))
    valid = np.ones((P, 16), np.float32)
    valid[0:REG, 0::2] = 0.0
    put("vm", valid)
    put("vmi", 1.0 - valid)
    put("half", -0.5)
    put("lift", LIFT)
    return c


def kernel(**inputs):
    import concourse.bacc as _bacc
    from concourse.bass_utils import run_bass_kernel_spmd as _run

    a = {k: np.asarray(v) for k, v in inputs.items()}

    def rows(w):
        k, n = w.shape
        return w.reshape(k // P, P, n).transpose(1, 0, 2).reshape(P, -1)

    def all_rows(v):
        return np.broadcast_to(v.reshape(1, -1), (P, v.size))

    def kv(wk, wv):
        return np.concatenate([wk[0:P], wv[0:P], np.concatenate([wk[P:CD], wv[P:CD]], 0)], 1)

    conv = np.concatenate([a["L0_attn_conv_w"], a["L0_attn_conv_b"][:, None], a["L0_attn_D"][:, None]], 1)
    w0 = np.concatenate([rows(a["L0_attn_W_in"].T), rows(a["L0_attn_W_xproj"].T), rows(a["L0_attn_W_out"].T),
                         rows(a["L0_xattn_Wq"]), rows(a["L0_xattn_Wo"])], 1)
    w0f = np.concatenate([rows(conv), all_rows(a["L0_xattn_bo"]), kv(a["L0_xattn_Wk"], a["L0_xattn_Wv"])], 1)
    w12 = a["L0_ffn_w12"].transpose(0, 2, 1).reshape(NE, 2, P, 512)
    w3 = a["L0_ffn_w3"].transpose(0, 2, 1).reshape(NE, 2, P, 256)
    s1 = a["L0_ffn_shared_w1"].T.reshape(2, P, 4, 256)
    s2 = a["L0_ffn_shared_w2"].T.reshape(2, P, 4, 256)
    s12 = np.concatenate([s1, s2], 3).transpose(2, 0, 1, 3)
    s3 = a["L0_ffn_shared_w3"].T.reshape(4, 2, P, 256)
    up = np.concatenate([w12, s12], 0).transpose(2, 0, 1, 3).reshape(P, NU, 1024)
    dn = np.concatenate([w3, s3], 0).transpose(2, 0, 1, 3).reshape(P, NU, 512)
    wu = np.concatenate([up, dn], 2).reshape(P, -1)
    wr = np.concatenate([rows(a["L0_ffn_router_w"].T), all_rows(a["L0_ffn_expert_bias"])], 1)
    w1 = np.concatenate([rows(a["L1_attn_w_qkv"].T), rows(a["L1_attn_w_out"].T), rows(a["L1_xattn_Wq"]), rows(a["L1_xattn_Wo"]),
                         rows(a["L1_ffn_W_qkv"]), rows(a["L1_ffn_W_proj"])], 1)
    w1f = np.concatenate([kv(a["L1_xattn_Wk"], a["L1_xattn_Wv"]), all_rows(a["L1_attn_b_out"]), all_rows(a["L1_xattn_bo"]),
                          all_rows(a["L1_ffn_b_proj"]), all_rows(a["L1_ffn_g_info"][0, 0])], 1)
    cT = a["ctx_768"]
    cT = np.concatenate([cT, cT[:, CK - 1:CK]], 1).reshape(B * CP, CD).T
    ctx = np.concatenate([cT[0:P], np.concatenate([cT[P:CD], cT[P:CD]], 0)], 1)
    x = a["x"].reshape(16, P, D).transpose(1, 0, 2).reshape(P, -1)
    arrays = {"x_dram": x, "ctx_dram": ctx, "w0_dram": w0, "w0f_dram": w0f, "wu_dram": wu, "wr_dram": wr, "w1_dram": w1,
              "w1f_dram": w1f, "const_dram": consts()}
    arrays = {k: np.ascontiguousarray(v) for k, v in arrays.items()}

    nc = _bacc.Bacc("TRN2", target_bir_lowering=False, num_devices=1)
    args = [nc.dram_tensor(k, v.shape, F32, kind="ExternalInput").ap() for k, v in arrays.items()]
    args.append(nc.dram_tensor("out_dram", (B * S, D), F32, kind="ExternalOutput").ap())
    args.append(nc.dram_tensor("keep_dram", (B, P, 1536), F32, kind="Internal").ap())
    program(nc, *args)
    r = _run(nc, [arrays], core_ids=[0])
    return r.results[0]["out_dram"].reshape(B, S, D)
```
